# Optimizing a Trainium2 kernel written in Bass

```python
import numpy as np
import jax
import jax.numpy as jnp

def _softmax(x, axis=-1):
    return jax.nn.softmax(x, axis=axis)

def _gelu(x):
    return jax.nn.gelu(x, approximate=True)

def _silu(x):
    return jax.nn.silu(x)

def _sigmoid(x):
    return jax.nn.sigmoid(x)

def _layernorm(x, axis=-1, eps=1e-05):
    m = jnp.mean(x, axis=axis, keepdims=True)
    v = jnp.var(x, axis=axis, keepdims=True)
    return (x - m) / jnp.sqrt(v + eps)

def _scatter_add(tgt, idx, src, axis=0):
    return tgt.at[idx].add(src)

def _segment_sum(src, seg, n):
    return jax.ops.segment_sum(src, seg, n)
kernel_name = 'mk_macaron_d2_jaxref_r4_3aaf96'

def setup_inputs(seed: int=0):
    np.random.seed(seed)
    _w = jnp.asarray

    def _L0_attn_setup():
        import jax, jax.numpy as jnp
        import numpy as np
        D_MODEL = 256
        H = 4
        DK = 256
        DV = 512
        HQK = DK // H
        HV = DV // H
        LOW_RANK = 32
        CHUNK = 16
        GATE_NORM = 32.0
        GATE_MULT = 1.0
        EPS = 1e-05

        def gla_fused_chunk(q, k, v, g, chunk=CHUNK):
            B, Hh, N, Dk = q.shape
            Dv = v.shape[-1]
            q = q * Dk ** (-0.5)
            nc = N // chunk

            def to_chunks(t, d):
                return t.reshape(B, Hh, nc, chunk, d).transpose(2, 0, 1, 3, 4)
            qc, kc, vc, gc = (to_chunks(q, Dk), to_chunks(k, Dk), to_chunks(v, Dv), to_chunks(g, Dk))
            bc = jnp.cumsum(gc, axis=-2)
            causal = jnp.tril(jnp.ones((chunk, chunk), bool))

            def step(S, inp):
                qi, ki, vi, bi = inp
                o_inter = jnp.einsum('bhtd,bhde->bhte', qi * jnp.exp(bi), S)
                diff = bi[:, :, :, None, :] - bi[:, :, None, :, :]
                diff = jnp.where(causal[None, None, :, :, None], diff, -jnp.inf)
                A = jnp.einsum('bhtd,bhjd,bhtjd->bhtj', qi, ki, jnp.exp(diff))
                o_intra = jnp.einsum('bhtj,bhje->bhte', A, vi)
                blast = bi[:, :, -1:, :]
                kdec = ki * jnp.exp(blast - bi)
                S_new = jnp.exp(blast)[:, :, 0, :, None] * S + jnp.einsum('bhtd,bhte->bhde', kdec, vi)
                return (S_new, o_inter + o_intra)
            S0 = jnp.zeros((B, Hh, Dk, Dv), q.dtype)
            _, o = jax.lax.scan(step, S0, (qc, kc, vc, bc))
            return o.transpose(1, 2, 0, 3, 4).reshape(B, Hh, N, Dv)
        key = jax.random.key(seed)
        ks = jax.random.split(key, 10)
        B, N = (2, 1024)
        s = 0.02
        return {'x': jax.random.normal(ks[0], (B, N, D_MODEL), jnp.float32), 'Wq': jax.random.normal(ks[1], (DK, D_MODEL), jnp.float32) * s, 'Wk': jax.random.normal(ks[2], (DK, D_MODEL), jnp.float32) * s, 'Wv': jax.random.normal(ks[3], (DV, D_MODEL), jnp.float32) * s, 'Wg': jax.random.normal(ks[4], (DV, D_MODEL), jnp.float32) * s, 'Wgk1': jax.random.normal(ks[5], (LOW_RANK, D_MODEL), jnp.float32) * s, 'Wgk2': jax.random.normal(ks[6], (DK, LOW_RANK), jnp.float32) * s, 'bgk2': jax.random.normal(ks[7], (DK,), jnp.float32) * 0.1, 'Wout': jax.random.normal(ks[8], (D_MODEL, DV), jnp.float32) * s, 'rms_w': jnp.ones((HV,), jnp.float32)}
    _L0_attn_in = _L0_attn_setup()

    def _L0_ffn_setup():
        import jax, jax.numpy as jnp
        import numpy as np
        N_EXPERTS = 8
        TOP_K = 2
        D_MODEL = 256
        HIDDEN = 1024
        ROUTED_H = 256
        BATCH, SEQ = (2, 1024)
        key = jax.random.key(seed)
        ks = jax.random.split(key, 8)
        std = 0.02
        return {'x': jax.random.normal(ks[0], (BATCH, SEQ, D_MODEL), dtype=jnp.float32), 'w12': std * jax.random.normal(ks[1], (N_EXPERTS, 2 * ROUTED_H, D_MODEL), dtype=jnp.float32), 'w3': std * jax.random.normal(ks[2], (N_EXPERTS, D_MODEL, ROUTED_H), dtype=jnp.float32), 'shared_w1': std * jax.random.normal(ks[3], (HIDDEN, D_MODEL), dtype=jnp.float32), 'shared_w2': std * jax.random.normal(ks[4], (HIDDEN, D_MODEL), dtype=jnp.float32), 'shared_w3': std * jax.random.normal(ks[5], (D_MODEL, HIDDEN), dtype=jnp.float32), 'router_w': std * jax.random.normal(ks[6], (N_EXPERTS, D_MODEL), dtype=jnp.float32), 'expert_bias': jnp.zeros((N_EXPERTS,), dtype=jnp.float32)}
    _L0_ffn_in = _L0_ffn_setup()

    def _L1_attn_setup():
        import jax, jax.numpy as jnp
        import numpy as np
        HIDDEN = 256
        NUM_HEADS = 16
        HEAD_DIM = HIDDEN // NUM_HEADS
        WINDOW = 33
        PAD = WINDOW // 2
        B, S = (2, 512)
        key = jax.random.key(seed)
        k = jax.random.split(key, 5)
        x = jax.random.normal(k[0], (B, S, HIDDEN), dtype=jnp.float32)
        w_qkv = jax.random.normal(k[1], (3 * HIDDEN, HIDDEN), dtype=jnp.float32) * 0.02
        b_qkv = jax.random.normal(k[2], (3 * HIDDEN,), dtype=jnp.float32) * 0.02
        w_out = jax.random.normal(k[3], (HIDDEN, HIDDEN), dtype=jnp.float32) * 0.02
        b_out = jax.random.normal(k[4], (HIDDEN,), dtype=jnp.float32) * 0.02
        return {'x': x, 'w_qkv': w_qkv, 'b_qkv': b_qkv, 'w_out': w_out, 'b_out': b_out}
    _L1_attn_in = _L1_attn_setup()

    def _L1_ffn_setup():
        import jax, jax.numpy as jnp
        import numpy as np
        EPS = 1e-05

        def _quantize(W):
            gamma = jnp.mean(jnp.abs(W))
            return jnp.clip(jnp.round(W / (gamma + EPS)), -1.0, 1.0)
        key = jax.random.key(seed)
        k_x, k_w1, k_b1, k_w2, k_b2 = jax.random.split(key, 5)
        n_embd = 256
        d_ff = 4 * n_embd
        B, S = (4, 1024)
        bound1 = 1.0 / np.sqrt(n_embd)
        bound2 = 1.0 / np.sqrt(d_ff)
        x = jax.random.normal(k_x, (B, S, n_embd), dtype=jnp.float32)
        W1 = jax.random.uniform(k_w1, (d_ff, n_embd), jnp.float32, -bound1, bound1)
        b1 = jax.random.uniform(k_b1, (d_ff,), jnp.float32, -bound1, bound1)
        W2 = jax.random.uniform(k_w2, (n_embd, d_ff), jnp.float32, -bound2, bound2)
        b2 = jax.random.uniform(k_b2, (n_embd,), jnp.float32, -bound2, bound2)
        return {'x': x, 'W1': W1, 'b1': b1, 'W2': W2, 'b2': b2}
    _L1_ffn_in = _L1_ffn_setup()
    _d = {'L0_attn_x': _L0_attn_in['x'], 'L0_attn_Wq': _L0_attn_in['Wq'], 'L0_attn_Wk': _L0_attn_in['Wk'], 'L0_attn_Wv': _L0_attn_in['Wv'], 'L0_attn_Wg': _L0_attn_in['Wg'], 'L0_attn_Wgk1': _L0_attn_in['Wgk1'], 'L0_attn_Wgk2': _L0_attn_in['Wgk2'], 'L0_attn_bgk2': _L0_attn_in['bgk2'], 'L0_attn_Wout': _L0_attn_in['Wout'], 'L0_attn_rms_w': _L0_attn_in['rms_w'], 'L0_ffn_w12': _L0_ffn_in['w12'], 'L0_ffn_w3': _L0_ffn_in['w3'], 'L0_ffn_shared_w1': _L0_ffn_in['shared_w1'], 'L0_ffn_shared_w2': _L0_ffn_in['shared_w2'], 'L0_ffn_shared_w3': _L0_ffn_in['shared_w3'], 'L0_ffn_router_w': _L0_ffn_in['router_w'], 'L0_ffn_expert_bias': _L0_ffn_in['expert_bias'], 'L1_attn_w_qkv': _L1_attn_in['w_qkv'], 'L1_attn_b_qkv': _L1_attn_in['b_qkv'], 'L1_attn_w_out': _L1_attn_in['w_out'], 'L1_attn_b_out': _L1_attn_in['b_out'], 'L1_ffn_W1': _L1_ffn_in['W1'], 'L1_ffn_b1': _L1_ffn_in['b1'], 'L1_ffn_W2': _L1_ffn_in['W2'], 'L1_ffn_b2': _L1_ffn_in['b2']}
    _x0 = _d['L0_attn_x']
    _d['L0_attn_x'] = jax.random.normal(jax.random.fold_in(jax.random.key(seed), 1), (8, 512, 256), dtype=_x0.dtype)
    del _x0
    return _d

def reference(L0_attn_x, L0_attn_Wq, L0_attn_Wk, L0_attn_Wv, L0_attn_Wg, L0_attn_Wgk1, L0_attn_Wgk2, L0_attn_bgk2, L0_attn_Wout, L0_attn_rms_w, L0_ffn_w12, L0_ffn_w3, L0_ffn_shared_w1, L0_ffn_shared_w2, L0_ffn_shared_w3, L0_ffn_router_w, L0_ffn_expert_bias, L1_attn_w_qkv, L1_attn_b_qkv, L1_attn_w_out, L1_attn_b_out, L1_ffn_W1, L1_ffn_b1, L1_ffn_W2, L1_ffn_b2):

    def _L0_attn_ref(x, Wq, Wk, Wv, Wg, Wgk1, Wgk2, bgk2, Wout, rms_w):
        import jax, jax.numpy as jnp
        import numpy as np
        D_MODEL = 256
        H = 4
        DK = 256
        DV = 512
        HQK = DK // H
        HV = DV // H
        LOW_RANK = 32
        CHUNK = 16
        GATE_NORM = 32.0
        GATE_MULT = 1.0
        EPS = 1e-05

        def gla_fused_chunk(q, k, v, g, chunk=CHUNK):
            B, Hh, N, Dk = q.shape
            Dv = v.shape[-1]
            q = q * Dk ** (-0.5)
            nc = N // chunk

            def to_chunks(t, d):
                return t.reshape(B, Hh, nc, chunk, d).transpose(2, 0, 1, 3, 4)
            qc, kc, vc, gc = (to_chunks(q, Dk), to_chunks(k, Dk), to_chunks(v, Dv), to_chunks(g, Dk))
            bc = jnp.cumsum(gc, axis=-2)
            causal = jnp.tril(jnp.ones((chunk, chunk), bool))

            def step(S, inp):
                qi, ki, vi, bi = inp
                o_inter = jnp.einsum('bhtd,bhde->bhte', qi * jnp.exp(bi), S)
                diff = bi[:, :, :, None, :] - bi[:, :, None, :, :]
                diff = jnp.where(causal[None, None, :, :, None], diff, -jnp.inf)
                A = jnp.einsum('bhtd,bhjd,bhtjd->bhtj', qi, ki, jnp.exp(diff))
                o_intra = jnp.einsum('bhtj,bhje->bhte', A, vi)
                blast = bi[:, :, -1:, :]
                kdec = ki * jnp.exp(blast - bi)
                S_new = jnp.exp(blast)[:, :, 0, :, None] * S + jnp.einsum('bhtd,bhte->bhde', kdec, vi)
                return (S_new, o_inter + o_intra)
            S0 = jnp.zeros((B, Hh, Dk, Dv), q.dtype)
            _, o = jax.lax.scan(step, S0, (qc, kc, vc, bc))
            return o.transpose(1, 2, 0, 3, 4).reshape(B, Hh, N, Dv)
        B, N, _ = x.shape
        split = lambda t, hd: t.reshape(B, N, H, hd).transpose(0, 2, 1, 3)
        q = split(x @ Wq.T, HQK)
        k = split(x @ Wk.T, HQK)
        v = split(x @ Wv.T, HV)
        g_logits = x @ Wgk1.T @ Wgk2.T + bgk2
        g = jax.nn.log_sigmoid(g_logits * GATE_MULT) / GATE_NORM
        g = split(g, HQK)
        o = gla_fused_chunk(q, k, v, g)
        o = o.transpose(0, 2, 1, 3)
        o = o * jax.lax.rsqrt(jnp.mean(o * o, axis=-1, keepdims=True) + EPS) * rms_w
        gate = jax.nn.silu(x @ Wg.T)
        return o.reshape(B, N, DV) * gate @ Wout.T

    def _L0_ffn_ref(x, w12, w3, shared_w1, shared_w2, shared_w3, router_w, expert_bias):
        import jax, jax.numpy as jnp
        import numpy as np
        N_EXPERTS = 8
        TOP_K = 2
        D_MODEL = 256
        HIDDEN = 1024
        ROUTED_H = 256
        BATCH, SEQ = (2, 1024)
        b, s, d = x.shape
        xf = x.reshape(-1, d)
        shared = jax.nn.silu(xf @ shared_w1.T) * (xf @ shared_w2.T) @ shared_w3.T
        scores = jax.nn.sigmoid(xf @ router_w.T)
        _, top_idx = jax.lax.top_k(scores + expert_bias, TOP_K)
        mask = jax.nn.one_hot(top_idx, N_EXPERTS, dtype=xf.dtype).sum(axis=-2)
        gates = scores * mask
        h12 = jnp.einsum('td,ehd->teh', xf, w12)
        h1, h2 = jnp.split(h12, 2, axis=-1)
        h = jax.nn.silu(h1) * h2 * gates[:, :, None]
        routed = jnp.einsum('teh,edh->td', h, w3)
        return (shared + routed).reshape(b, s, d)

    def _L1_attn_ref(x, w_qkv, b_qkv, w_out, b_out):
        import jax, jax.numpy as jnp
        import numpy as np
        HIDDEN = 256
        NUM_HEADS = 16
        HEAD_DIM = HIDDEN // NUM_HEADS
        WINDOW = 33
        PAD = WINDOW // 2
        B, S = (2, 512)
        b, s, _ = x.shape
        qkv = x @ w_qkv.T + b_qkv
        qkv = qkv.reshape(b, s, NUM_HEADS, 3 * HEAD_DIM).transpose(0, 2, 1, 3)
        q, k, v = jnp.split(qkv, 3, axis=-1)
        k_pad = jnp.pad(k, ((0, 0), (0, 0), (PAD, PAD), (0, 0)))
        v_pad = jnp.pad(v, ((0, 0), (0, 0), (PAD, PAD), (0, 0)))
        idx = jnp.arange(s)[:, None] + jnp.arange(WINDOW)[None, :]
        k_win = k_pad[:, :, idx, :]
        v_win = v_pad[:, :, idx, :]
        scores = jnp.einsum('bhsd,bhswd->bhsw', q, k_win) / jnp.sqrt(jnp.asarray(HEAD_DIM, dtype=q.dtype))
        attn = jax.nn.softmax(scores, axis=-1)
        ctx = jnp.einsum('bhsw,bhswd->bhsd', attn, v_win)
        ctx = ctx.transpose(0, 2, 1, 3).reshape(b, s, HIDDEN)
        return ctx @ w_out.T + b_out

    def _L1_ffn_ref(x, W1, b1, W2, b2):
        import jax, jax.numpy as jnp
        import numpy as np
        EPS = 1e-05

        def _quantize(W):
            gamma = jnp.mean(jnp.abs(W))
            return jnp.clip(jnp.round(W / (gamma + EPS)), -1.0, 1.0)
        Wq1 = _quantize(W1)
        Wq2 = _quantize(W2)
        h = jax.nn.relu(jnp.einsum('bsd,fd->bsf', x, Wq1) + b1)
        out = jnp.einsum('bsf,df->bsd', h, Wq2) + b2
        return out
    x = L0_attn_x
    x = x + 0.5 * _L0_ffn_ref(_layernorm(x, axis=-1), L0_ffn_w12, L0_ffn_w3, L0_ffn_shared_w1, L0_ffn_shared_w2, L0_ffn_shared_w3, L0_ffn_router_w, L0_ffn_expert_bias)
    x = x + _L0_attn_ref(_layernorm(x, axis=-1), L0_attn_Wq, L0_attn_Wk, L0_attn_Wv, L0_attn_Wg, L0_attn_Wgk1, L0_attn_Wgk2, L0_attn_bgk2, L0_attn_Wout, L0_attn_rms_w)
    x = x + 0.5 * _L0_ffn_ref(_layernorm(x, axis=-1), L0_ffn_w12, L0_ffn_w3, L0_ffn_shared_w1, L0_ffn_shared_w2, L0_ffn_shared_w3, L0_ffn_router_w, L0_ffn_expert_bias)
    x = x + 0.5 * _L1_ffn_ref(_layernorm(x, axis=-1), L1_ffn_W1, L1_ffn_b1, L1_ffn_W2, L1_ffn_b2)
    x = x + _L1_attn_ref(_layernorm(x, axis=-1), L1_attn_w_qkv, L1_attn_b_qkv, L1_attn_w_out, L1_attn_b_out)
    x = x + 0.5 * _L1_ffn_ref(_layernorm(x, axis=-1), L1_ffn_W1, L1_ffn_b1, L1_ffn_W2, L1_ffn_b2)
    return x

_drawn_inputs = setup_inputs


def setup_inputs(seed=0):
    import zlib

    import numpy as np

    out = dict(_drawn_inputs(seed))
    spreads = {'L0_attn_rms_w': (1.0, 0.6), 'L0_ffn_expert_bias': (0.0, 0.648)}
    factors = {'L0_attn_Wgk1': 8.0,
     'L0_attn_Wgk2': 8.0,
     'L0_attn_bgk2': 8.0,
     'L0_ffn_w12': 4.958,
     'L0_ffn_w3': 4.655,
     'L0_ffn_router_w': 7.042,
     'L1_attn_w_qkv': 8.0,
     'L1_attn_b_qkv': 64.0,
     'L1_attn_w_out': 8.0,
     'L1_attn_b_out': 200.0,
     'L1_ffn_b1': 8.0,
     'L1_ffn_b2': 200.0}
    for name, (base, spread) in spreads.items():
        noise = np.random.default_rng([zlib.crc32(name.encode()), seed]).standard_normal(out[name].shape)
        drawn = base * np.exp(spread * noise) if base else spread * noise
        out[name] = jnp.asarray(drawn.astype(out[name].dtype))
    for name, factor in factors.items():
        out[name] = (out[name] * factor).astype(out[name].dtype)
    return out
```

```python
from contextlib import ExitStack

import concourse.bass as bass
from concourse import mybir

P = 128
D = 256
KT = D // P
NSEQ, SEQ = 8, 512
TPS = SEQ // P
EPS = 1e-5
WS = 64.0
HS = 16.0

NE, HE = 8, 256
HSH = 1024
SU, EU = HSH // P, HE // P
UNITS = SU + NE * EU
JOBS = 1 + NE

FF = 1024
FU = FF // P

H, DK, DV = 4, 64, 128
GPAIR = H // 2
LOW = 32
GATE_NORM = 32.0

AH, AD = 16, 16
PAD = 16
QB, KB = 32, 64
NB = SEQ // QB
BPT = P // QB
HG = AH // 4
VF = NB // 2 + 1
MASKED = -1e30

ALU = mybir.AluOpType
ACT = mybir.ActivationFunctionType
AX = mybir.AxisListType
F32 = mybir.dt.float32
F16 = mybir.dt.float16


class Space:
    pass


SUBLAYERS = ("ffn0", "gla", "ffn0", "l1ffn", "win", "l1ffn")

CONST_COLS = {"ident": 128, "ones": 128, "causal": 128, "cumref": 128, "after": 128, "ends": 2, "tri": NE * NE,
              "window": 64, "fold": 32, "hgsum": 2, "edge": 2, "heads": 8}


def const_at(name):
    at = 0
    for n, w in CONST_COLS.items():
        if n == name:
            return slice(at, at + w)
        at += w


NCONST = sum(CONST_COLS.values())


def ds(at, n):
    return bass.ds(at, n)


def build(nc, T, out):
    ctx = ExitStack()
    with ctx:
        def sb(name, shape, dt=F32):
            return ctx.enter_context(nc.sbuf_tensor(name, shape, dt))

        def sem(name):
            return ctx.enter_context(nc.semaphore(name))

        x = sb("x", [P, NSEQ * TPS, D])
        consts = sb("consts", [P, NCONST])
        window16 = sb("window16", [P, 8, KB], mybir.dt.bfloat16)
        ident16 = sb("ident16", [P, P], mybir.dt.bfloat16)

        def const(name):
            return consts[:, const_at(name)]

        ident = const("ident")

        def pair(name, cols, rows=P):
            return sb(name + "_hi", [rows, cols], F16), sb(name + "_lo", [rows, cols], F16)

        wup = pair("wup", KT * NE * 2 * HE)
        wsh1 = pair("wsh1", KT * HSH)
        wsh2 = pair("wsh2", KT * HSH)
        wsh3 = pair("wsh3", SU * D)
        wdn = pair("wdn", NE * EU * D)
        wr = pair("wr", KT * NE)
        gqk = pair("gqk", KT * 2 * H * DK)
        gv = pair("gv", KT * H * DV)
        gg = pair("gg", KT * H * DV)
        gk1 = pair("gk1", KT * LOW)
        gk2 = pair("gk2", H * DK, LOW)
        go = pair("go", H * D)
        aqkv = pair("aqkv", KT * 3 * D)
        ao = pair("ao", KT * D)
        w1q = sb("w1q", [P, KT * FF], F16)
        w2q = sb("w2q", [P, FU * D], F16)
        rows = sb("rows", [P, 5 * D + NE])
        bgk_row, b2_row, bo_row = (rows[:, n * D:(n + 1) * D] for n in range(3))
        bv_row = rows[:, 3 * D:5 * D]
        ebias_row = rows[:, 5 * D:]
        cols = sb("cols", [P, FU + 2 * KT + 1])
        b1_col, bq_col, bk_col = cols[:, 0:FU], cols[:, FU:FU + KT], cols[:, FU + KT:FU + 2 * KT]
        rms_col = cols[:, FU + 2 * KT:]

        xn = sb("xn", [P, TPS, D])
        stats = sb("stats", [P, TPS, 6])
        mv = sb("mv", [P, TPS, 2])
        rstd = sb("rstd", [P, TPS])
        tsum, thr = sb("tsum", [P, 2]), sb("thr", [P, 2, 2])
        eps = sb("eps", [P, TPS])
        neghalf = sb("neghalf", [P, 4 * TPS])
        XW = SEQ + 2 * PAD
        xt_hi = sb("xt_hi", [P, 2, KT, XW], F16)
        xt_lo = sb("xt_lo", [P, 2, KT, XW], F16)
        TOK = slice(PAD, PAD + SEQ)

        WORK = 45 * 1024
        work = sb("work", [P, WORK // 4])

        class Carve:
            def __init__(self, base=None):
                self.base = work if base is None else base
                self.room = (4 if base is None else 2) * self.base.shape[1]
                self.at = 0

            def __call__(self, shape, dt=F32):
                n = 1
                for s in shape:
                    n *= s
                size = (4 if dt == F32 else 2) * n
                each = 4 if self.base is work else 2
                a = self.base[:, self.at // each:(self.at + size) // each]
                self.at += size
                assert self.at <= self.room, self.at
                if dt != (F32 if each == 4 else F16):
                    a = a.bitcast(dt)
                names = "abcd"[:len(shape)]
                if len(shape) == 1:
                    return a
                return a.rearrange(f"p ({' '.join(names)}) -> p {' '.join(names)}",
                                   **{n: s for n, s in zip(names[1:], shape[1:])})

        ps = ctx.enter_context(nc.psum_tensor("ps", [P, 8, 512], F32))

        x_loaded = [sem(f"x_loaded{n}") for n in range(2)]
        small_loaded = sem("small_loaded")
        x_stored = sem("x_stored")
        ready0 = sem("constants_ready")
        NST = 4
        staged = [sem(f"staged{n}") for n in range(NST)]
        w_hi_done, w_lo_done = sem("w_hi_done"), sem("w_lo_done")
        tern = sem("ternary_steps")
        tern_sum = sem("ternary_sum")
        mv_ready, rstd_ready, xn_ready = sem("mv_ready"), sem("rstd_ready"), sem("xn_ready")
        ln_step = sem("ln_step")
        pt_ready, xt_hi_ready, xt_lo_ready = sem("pt_ready"), sem("xt_hi_ready"), sem("xt_lo_ready")
        x_updated = sem("x_updated")
        rstd_step = sem("rstd_step")
        stood = sem("wait_stood_alone")

        def names(prefix, text):
            return {n: sem(f"{prefix}_{n}") for n in text.split()}

        S = []
        for n, kind in enumerate(SUBLAYERS):
            text = {
                "ffn0": "router_ready scores_ready gate_step up_ready silu_ready prod_ready h_hi_ready "
                        "h_lo_ready y_ready y_taken",
                "l1ffn": "up_ready relu_ready h_hi_ready h_lo_ready y_ready y_taken bias_added",
                "gla": "t_ready t_hi t_lo qk_ready qk_copied logits_ready lb_ready soft_step g_ready v_ready v_copied "
                       "kt_ready cum_ready exps_ready q_ready k_ready kdec_ready at_ready masked st_ready s_step "
                       "gate_ready gate_done o_ready sq_ready ss_ready orstd_step orstd_ready og_ready ogt_ready "
                       "ogt_hi ogt_lo y_ready y_taken",
                "win": "zeroed qk_ready qk_copied qz_ready v_ready v_copied sc_ready mx_ready sub_ready "
                       "exp_ready pt_ready pt_copied c_ready rl_ready cn_ready ct_ready ct_hi ct_lo y_ready "
                       "y_taken bias_added",
            }[kind]
            S.append(names(f"{kind}{n}", text))

        N0 = lambda n: n * NSEQ

        SPLIT = [("w_sh1", wsh1, KT * HSH, P), ("w_sh2", wsh2, KT * HSH, P), ("w_r", wr, KT * NE, P),
                 ("w_up", wup, KT * NE * 2 * HE, P), ("w_sh3", wsh3, SU * D, P), ("w_dn", wdn, NE * EU * D, P),
                 ("g_qk", gqk, KT * 2 * H * DK, P), ("g_v", gv, KT * H * DV, P), ("g_g", gg, KT * H * DV, P),
                 ("g_k1", gk1, KT * LOW, P), ("g_k2", gk2, H * DK, LOW), ("g_o", go, H * D, P),
                 ("a_qkv", aqkv, KT * 3 * D, P), ("a_o", ao, KT * D, P)]
        CH = 2048
        chunks = [(name, dst, c, min(CH, n - c), r) for name, dst, n, r in SPLIT for c in range(0, n, CH)]
        TERN = [("w_1", w1q), ("w_2", w2q)]
        stage = Carve()([NST, CH])
        NCH = len(chunks)
        loads = [(name, c, n, r) for name, _, c, n, r in chunks] + [(name, 0, CH, P) for name, _ in TERN]

        def load_done(eng, m):
            eng.wait_ge(staged[m % NST], 16 * (m // NST + 1))

        def gla_space():
            r = Carve()
            m = Space()
            m.t_hi, m.t_lo = r([SEQ], F16), r([SEQ], F16)
            m.q = r([GPAIR, SEQ])
            m.states = m.q.rearrange("p a (b c) -> p (a b) c", c=DV).rearrange("p (c a) d -> p c a d", a=GPAIR)
            m.k = r([GPAIR, SEQ])
            m.squares = m.k
            m.v = r([TPS, H * DV])
            m.lb = r([TPS, H * DK])
            m.soft = r([TPS, H * DK])
            at = Carve()
            at.at = r.at - 2 * 4 * TPS * H * DK
            m.gate = at([TPS, H * DV])
            m.up, m.down = r([GPAIR, SEQ]), r([GPAIR, SEQ])
            at.at = r.at - 2 * 4 * GPAIR * SEQ
            m.att = at([TPS, H * P])
            at.at = r.at - 2 * 4 * GPAIR * SEQ
            m.o_hi, m.o_lo = at([TPS, H, P], F16), at([TPS, H, P], F16)
            m.qz = r([GPAIR, 2, SEQ])
            m.ends = r([GPAIR, TPS, 2])
            m.s = r([GPAIR, DV])
            m.ss, m.orstd = r([TPS, H]), r([TPS, H])
            return m

        def win_space():
            r = Carve()
            m = Space()
            m.vz = Carve(wup[0])([NB, KT, P])
            m.qz = Carve(wup[1])([2 * KT, BPT, 8, QB])
            m.q = r([KT, SEQ])
            m.k = r([KT, XW])
            m.p = r([2, BPT * KT * 2, KB])
            m.pt = r([2, BPT * KT, P])
            m.c = r([BPT * KT, P])
            m.c_hi, m.c_lo = r([KT, SEQ], F16), r([KT, SEQ], F16)
            m.mx, m.rl = r([BPT * KT * 2]), r([BPT * KT * 2])
            return m

        GB = (3, 4, 5, 6)
        SB = (0, 1, 2, 7)

        block = ctx.enter_context(nc.Block())

        @block.sync
        def _(sp):
            sp.dma_start(consts[:], T["consts"]).then_inc(small_loaded, 16)
            xd = T["x"].rearrange("(t p) d -> p t d", p=P)
            sp.dma_start(x[:, 0:TPS, :], xd[:, 0:TPS, :]).then_inc(x_loaded[0], 16)
            sp.dma_start(rows[:], T["rows"]).then_inc(small_loaded, 16)
            sp.dma_start(cols[:], T["cols"]).then_inc(small_loaded, 16)
            for m, (name, c, n, r) in enumerate(loads):
                if m >= NST:
                    sp.wait_ge(w_lo_done, m - NST + 1)
                sp.dma_start(stage[0:r, m % NST, 0:n], T[name][:, c:c + n]).then_inc(staged[m % NST], 16)
                if m == 3:
                    sp.dma_start(x[:, TPS:, :], xd[:, TPS:, :]).then_inc(x_loaded[1], 16)
            od = out.rearrange("(t p) d -> p t d", p=P)
            last = len(SUBLAYERS) - 1
            for g in range(NSEQ):
                sp.wait_ge(x_updated, N0(last) + g + 1)
                sp.dma_start(od[:, g * TPS:(g + 1) * TPS, :], x[:, g * TPS:(g + 1) * TPS, :]).then_inc(x_stored, 16)
            sp.wait_ge(x_stored, 16 * NSEQ)

        def each_sequence(eng, body):
            with eng.Fori(0, NSEQ // 2) as i:
                for u in range(2):
                    body(2 * i + u, u)

        @block.gpsimd
        def _(pool):
            nc.gpsimd.memset(neghalf[:], -0.5).then_inc(rstd_step, 1)
            nc.gpsimd.memset(eps[:], EPS).then_inc(rstd_step, 1)
            pool.wait_ge(rstd_step, 2)

            def rstd_of(m):
                pool.wait_ge(mv_ready, m + 1)
                nc.gpsimd.tensor_tensor(rstd[:], mv[:, :, 1], eps[:], ALU.add).then_inc(rstd_step, 1)
                pool.wait_ge(rstd_step, m + 3)
                nc.gpsimd.tensor_tensor(rstd[:], rstd[:], neghalf[:, 0:TPS], ALU.pow).then_inc(rstd_ready, 1)

            def work_left(n):
                if n:
                    pool.wait_ge(x_updated, N0(n))
                else:
                    pool.wait_ge(pt_ready, 1)

            def l1ffn(n):
                s = S[n]

                def body(g, u):
                    pool.wait_ge(xn_ready, g + N0(n) + 1)
                    for t in range(TPS):
                        ins = nc.gpsimd.tensor_tensor(x[:, ds(g * TPS + t, 1), :], x[:, ds(g * TPS + t, 1), :],
                                                      b2_row[:, None, :], ALU.add)
                    ins.then_inc(s["bias_added"], 1)
                    rstd_of(g + N0(n) + 1)
                each_sequence(pool, body)

            def ffn0(n):
                each_sequence(pool, lambda g, u: rstd_of(g + N0(n) + 1))

            def gla(n):
                s, m = S[n], gla_space()
                work_left(n)
                nc.gpsimd.memset(m.qz, 0.0).then_inc(s["q_ready"], 2)

                def body(g, u):
                    rstd_of(g + N0(n) + 1)
                    pool.wait_ge(s["ss_ready"], g * TPS + TPS)
                    nc.gpsimd.tensor_tensor(m.orstd, m.ss, eps[:, None, :].broadcast_to([P, TPS, H]), ALU.add).then_inc(s["orstd_step"], 1)
                    pool.wait_ge(s["orstd_step"], g + 1)
                    nc.gpsimd.tensor_tensor(m.orstd, m.orstd, neghalf.rearrange("p (a b) -> p a b", b=H), ALU.pow).then_inc(s["orstd_ready"], 1)
                each_sequence(pool, body)

            def win(n):
                s, m = S[n], win_space()
                work_left(n)
                for a in (m.vz, m.c, m.k[:, :, 0:PAD]):
                    nc.gpsimd.memset(a, 0.0)
                nc.gpsimd.memset(m.k[:, :, PAD + SEQ:], 0.0).then_inc(s["zeroed"], 1)
                heads = const("heads")

                def body(g, u):
                    pool.wait_ge(xn_ready, g + N0(n) + 1)
                    for t in range(TPS):
                        ins = nc.gpsimd.tensor_tensor(x[:, ds(g * TPS + t, 1), :], x[:, ds(g * TPS + t, 1), :],
                                                      bo_row[:, None, :], ALU.add)
                    ins.then_inc(s["bias_added"], 1)
                    pool.wait_ge(s["qk_copied"], g * 2 * KT + KT)
                    for t in range(TPS):
                        pool.wait_ge(s["sc_ready"], g * TPS + t + 1)
                        for f in range(KT):
                            ins = nc.gpsimd.tensor_tensor(
                                m.qz[:, t % 2 * KT + f],
                                m.q[:, f, t * P:(t + 1) * P].rearrange("p (b q) -> p b q", q=QB)[:, :, None].broadcast_to([P, BPT, 8, QB]),
                                heads[:, None, :, None].broadcast_to([P, BPT, 8, QB]), ALU.mult)
                        ins.then_inc(s["qz_ready"], 1)
                    rstd_of(g + N0(n) + 1)
                each_sequence(pool, body)

            pool.wait_ge(small_loaded, 48)
            nc.gpsimd.tensor_scalar(b2_row, b2_row, 0.5, None, ALU.mult).then_inc(ready0, 1)
            nc.gpsimd.tensor_scalar(rms_col, rms_col, WS, None, ALU.mult).then_inc(ready0, 1)
            pool.wait_ge(ready0, 2)
            for w in (xt_hi, xt_lo):
                nc.gpsimd.memset(w[:, :, :, 0:PAD], 0.0)
                nc.gpsimd.memset(w[:, :, :, PAD + SEQ:], 0.0).then_inc(ready0, 1)
            rstd_of(0)
            for n, kind in enumerate(SUBLAYERS):
                {"ffn0": ffn0, "l1ffn": l1ffn, "gla": gla, "win": win}[kind](n)

        @block.scalar
        def _(act):
            def halves_hi():
                for m, (name, dst, c, n, r) in enumerate(chunks):
                    load_done(act, m)
                    nc.scalar.activation(dst[0][0:r, c:c + n], stage[0:r, m % NST, 0:n], ACT.Copy,
                                         scale=rms_col if name == "g_o" else WS).then_inc(w_hi_done, 1)

            def xt_hi_of(m, u):
                act.wait_ge(pt_ready, m + 1)
                nc.scalar.activation(xt_hi[:, u, :, TOK], ps[:, 0:KT, :], ACT.Copy).then_inc(xt_hi_ready, 1)

            def ffn0(n):
                s = S[n]
                r = Carve()
                h_hi, h_lo = r([SU + 4 * EU, SEQ], F16), r([SU + 4 * EU, SEQ], F16)
                silu, prod = r([2, SEQ]), r([2, SEQ])
                scores = r([TPS, NE])

                def slot(k):
                    return k if k < SU else SU + (k - SU) % (4 * EU)

                def body(g, u):
                    def hi(k):
                        act.wait_ge(s["prod_ready"], g * UNITS + k + 3)
                        if k < SU and k == 0:
                            act.wait_ge(s["y_ready"], g * 2 * JOBS + 2)
                        if k >= SU and (k - SU) % EU == 0:
                            e = (k - SU) // EU
                            act.wait_ge(s["y_ready"], g * 2 * JOBS + 2 * (e - 4 + 2) + 2 * JOBS if e >= 4
                                        else g * 2 * JOBS + 2 * (e + NE - 4 + 2))
                        nc.scalar.activation(h_hi[:, slot(k), :], prod[:, k % 2, :], ACT.Copy).then_inc(s["h_hi_ready"], 1)

                    act.wait_ge(s["router_ready"], g + 1)
                    nc.scalar.activation(scores.rearrange("p a b -> p (a b)"), ps[:, 0, 0:TPS * NE], ACT.Sigmoid,
                                         scale=1 / WS).then_inc(s["scores_ready"], 1)
                    for k in range(UNITS):
                        b = 2 + 2 * (k % 2)
                        act.wait_ge(s["up_ready"], g * UNITS + k + 1)
                        act.wait_ge(s["prod_ready"], g * UNITS + k + 1)
                        nc.scalar.activation(silu[:, k % 2, :], ps[:, b, :], ACT.Silu, scale=1 / WS).then_inc(s["silu_ready"], 1)
                        if k >= 1:
                            hi(k - 1)
                    hi(UNITS - 1)
                    xt_hi_of(g + N0(n) + 1, 1 - u)
                each_sequence(act, body)

            def l1ffn(n):
                s = S[n]
                r = Carve()
                h_hi, h_lo = r([FU, SEQ], F16), r([FU, SEQ], F16)
                relu = r([2, SEQ])

                def body(g, u):
                    def hi(k):
                        act.wait_ge(s["relu_ready"], g * FU + k + 1)
                        if k == 0:
                            act.wait_ge(s["y_ready"], g * 2 + 2)
                        nc.scalar.activation(h_hi[:, k, :], relu[:, k % 2, :], ACT.Copy).then_inc(s["h_hi_ready"], 1)

                    for k in range(FU):
                        act.wait_ge(s["up_ready"], g * FU + k + 1)
                        act.wait_ge(s["h_lo_ready"], g * FU + k + 1)
                        nc.scalar.activation(relu[:, k % 2, :], ps[:, 2 + k % 4, :], ACT.Relu,
                                             bias=b1_col[:, k:k + 1]).then_inc(s["relu_ready"], 1)
                        if k >= 1:
                            hi(k - 1)
                    hi(FU - 1)
                    xt_hi_of(g + N0(n) + 1, 1 - u)
                each_sequence(act, body)

            def gla(n):
                s, m = S[n], gla_space()

                def body(g, u):
                    act.wait_ge(s["t_ready"], g + 1)
                    nc.scalar.activation(m.t_hi[0:LOW], ps[0:LOW, 2, :], ACT.Copy, scale=1 / WS).then_inc(s["t_hi"], 1)
                    for j in range(2 * GPAIR):
                        act.wait_ge(s["qk_ready"], g * 2 * GPAIR + j + 1)
                        dst, p = (m.q, j) if j < GPAIR else (m.k, j - GPAIR)
                        nc.scalar.activation(dst[:, p], ps[:, 3 + j, :], ACT.Copy,
                                             scale=(DK ** -0.5 if j < GPAIR else 1.0) / WS).then_inc(s["qk_copied"], 1)
                    act.wait_ge(s["lb_ready"], g * 2 + 2)
                    nc.scalar.activation(m.soft, m.lb, ACT.Abs).then_inc(s["soft_step"], 1)
                    act.wait_ge(s["soft_step"], g * 3 + 1)
                    nc.scalar.activation(m.soft, m.soft, ACT.Exp, scale=-1.0).then_inc(s["soft_step"], 1)
                    act.wait_ge(s["soft_step"], g * 3 + 2)
                    nc.scalar.activation(m.soft, m.soft, ACT.Ln, bias=1.0).then_inc(s["soft_step"], 1)
                    for c in range(TPS):
                        act.wait_ge(s["v_ready"], g * TPS + c + 1)
                        nc.scalar.activation(m.v[:, c], ps[:, GB[c], :], ACT.Copy, scale=1 / WS).then_inc(s["v_copied"], 1)
                    act.wait_ge(s["cum_ready"], g + 1)
                    nc.scalar.activation(m.up, ps[:, 3:5, :], ACT.Exp).then_inc(s["exps_ready"], 1)
                    nc.scalar.activation(m.down, ps[:, 3:5, :], ACT.Exp, scale=-1.0).then_inc(s["exps_ready"], 1)
                    nc.scalar.activation(m.soft.rearrange("p (a b) c -> p a (b c)", a=2), ps[:, 5:7, :], ACT.Exp).then_inc(s["exps_ready"], 1)
                    nc.scalar.activation(m.ends.rearrange("p a b c -> p (a b c)"), ps[:, 0, 0:GPAIR * TPS * 2], ACT.Exp).then_inc(s["exps_ready"], 1)
                    for c in range(TPS):
                        act.wait_ge(s["gate_ready"], g * TPS + c + 1)
                        act.wait_ge(s["st_ready"], g * TPS + TPS)
                        nc.scalar.activation(m.gate[:, c], ps[:, GB[c], :], ACT.Silu, scale=1 / WS).then_inc(s["gate_done"], 1)
                    for c in range(TPS):
                        act.wait_ge(s["o_ready"], g * TPS + c + 1)
                        if c >= 2:
                            act.wait_ge(s["ss_ready"], g * TPS + c - 1)
                        nc.scalar.activation(m.squares[:, c % 2], ps[:, GB[c], :], ACT.Square,
                                             scale=DV ** -0.5).then_inc(s["sq_ready"], 1)
                    for c in range(TPS):
                        act.wait_ge(s["ogt_ready"], g * TPS + c + 1)
                        nc.scalar.activation(m.o_hi[:, c].rearrange("p h t -> p (h t)"), ps[:, SB[c], :], ACT.Copy).then_inc(s["ogt_hi"], 1)
                    xt_hi_of(g + N0(n) + 1, 1 - u)
                each_sequence(act, body)

            def win(n):
                s, m = S[n], win_space()
                act.wait_ge(s["zeroed"], 1)

                def body(g, u):
                    for j in range(2 * KT):
                        act.wait_ge(s["qk_ready"], g * 2 * KT + j + 1)
                        f = j % KT
                        dst, b = (m.q[:, f], bq_col) if j < KT else (m.k[:, f, TOK], bk_col)
                        nc.scalar.activation(dst, ps[:, 2 + j, :], ACT.Identity, bias=b[:, f:f + 1],
                                             scale=1 / WS).then_inc(s["qk_copied"], 1)
                    for t in range(TPS):
                        i = t % 2
                        act.wait_ge(s["sub_ready"], g * TPS + t + 1)
                        nc.scalar.activation(m.p[:, i], m.p[:, i], ACT.Exp, scale=AD ** -0.5).then_inc(s["exp_ready"], 1)
                        act.wait_ge(s["pt_ready"], g * TPS + t + 1)
                        for b in range(2):
                            ins = nc.scalar.activation(m.pt[:, i, 4 * b:4 * b + 4].rearrange("p a b -> p (a b)"),
                                                       ps[:, 4 + b, :], ACT.Copy)
                        ins.then_inc(s["pt_copied"], 1)
                        if t >= 1:
                            ct_hi(s, m, g, t - 1)
                    ct_hi(s, m, g, TPS - 1)
                    xt_hi_of(g + N0(n) + 1, 1 - u)

                def ct_hi(s, m, g, t):
                    act.wait_ge(s["ct_ready"], g * TPS + t + 1)
                    nc.scalar.activation(m.c_hi[:, :, t * P:(t + 1) * P], ps[:, 1, 0:KT * P].rearrange("p (f q) -> p f q", f=KT),
                                         ACT.Copy).then_inc(s["ct_hi"], 1)
                each_sequence(act, body)

            act.wait_ge(small_loaded, 48)
            act.wait_ge(ready0, 4)
            nc.scalar.activation(window16[:], const("window")[:, None, :].broadcast_to([P, 8, KB]), ACT.Copy)
            nc.scalar.activation(ident16[:], ident, ACT.Copy)
            halves_hi()
            xt_hi_of(0, 0)
            for n, kind in enumerate(SUBLAYERS):
                {"ffn0": ffn0, "l1ffn": l1ffn, "gla": gla, "win": win}[kind](n)

        @block.vector
        def _(dve):
            def halves_lo():
                for m, (name, dst, c, n, r) in enumerate(chunks):
                    dve.wait_ge(w_hi_done, m + 1)
                    nc.vector.scalar_tensor_tensor(out=dst[1][0:r, c:c + n], in0=stage[0:r, m % NST, 0:n],
                                                   scalar=rms_col if name == "g_o" else WS,
                                                   in1=dst[0][0:r, c:c + n], op0=ALU.mult,
                                                   op1=ALU.subtract).then_inc(w_lo_done, 1)

            def ternary():
                step = 0
                for k, (name, dst) in enumerate(TERN):
                    load_done(dve, NCH + k)
                    nc.vector.tensor_reduce(tsum[:, k:k + 1], stage[:, (NCH + k) % NST, :], AX.X, ALU.add,
                                            apply_absolute_value=True).then_inc(tern, 1)
                for k, (name, dst) in enumerate(TERN):
                    dve.wait_ge(tern_sum, 1)
                    for sign, c in ((1, 0), (-1, 1)):
                        nc.vector.tensor_scalar(thr[:, k, c:c + 1], ps[:, 7, k:k + 1], sign * 0.5 / (CH * P), sign * 0.5 * EPS,
                                                ALU.mult, ALU.add).then_inc(tern, 1)
                dve.wait_ge(tern, 6)
                for k, (name, dst) in enumerate(TERN):
                    w = stage[:, (NCH + k) % NST, :]
                    nc.vector.tensor_scalar(dst[:], w, thr[:, k, 1:2], None, ALU.is_lt).then_inc(tern, 1)
                    dve.wait_ge(tern, 7 + 2 * k)
                    nc.vector.scalar_tensor_tensor(out=dst[:], in0=w, scalar=thr[:, k, 0:1], in1=dst[:],
                                                   op0=ALU.is_gt, op1=ALU.subtract).then_inc(tern, 1)
                dve.wait_ge(tern, 10)

            def ln_stats(m, at):
                for t in range(TPS):
                    ins = nc.vector.bn_stats(stats[:, t, :], x[:, ds(at + t, 1), :].rearrange("p a d -> p (a d)"))
                ins.then_inc(ln_step, 1)
                dve.wait_ge(ln_step, m + 1)
                dve.sem_inc(stood, 1)
                for t in range(TPS):
                    ins = nc.vector.bn_aggr(mv[:, t, :], stats[:, t, :])
                ins.then_inc(mv_ready, 1)

            def ln_scale(m, at, first=False):
                dve.wait_ge(mv_ready, m + 1)
                dve.wait_ge(rstd_ready, m + 1)
                if not first:
                    dve.wait_ge(pt_ready, m)
                for t in range(TPS):
                    ins = nc.vector.tensor_scalar(xn[:, t, :], x[:, ds(at + t, 1), :].rearrange("p a d -> p (a d)"),
                                                  mv[:, t, 0:1], rstd[:, t:t + 1], ALU.subtract, ALU.mult)
                ins.then_inc(xn_ready, 1)

            def xt_lo_of(m, u):
                dve.wait_ge(xt_hi_ready, m + 1)
                nc.vector.tensor_tensor(xt_lo[:, u, :, TOK], ps[:, 0:KT, :], xt_hi[:, u, :, TOK], ALU.subtract).then_inc(xt_lo_ready, 1)

            def next_at(g):
                return ((g + 1) % NSEQ) * TPS

            def ffn0(n):
                s = S[n]
                r = Carve()
                h_hi, h_lo = r([SU + 4 * EU, SEQ], F16), r([SU + 4 * EU, SEQ], F16)
                silu, prod = r([2, SEQ]), r([2, SEQ])
                scores, biased, gates = r([TPS, NE]), r([TPS, NE]), r([TPS, NE])
                beats, ties = r([TPS, NE, NE]), r([TPS, NE, NE])
                rank = r([TPS, NE])
                tri = const("tri").rearrange("p (e j) -> p e j", e=NE)
                GSTEPS = 7

                def slot(k):
                    return k if k < SU else SU + (k - SU) % (4 * EU)

                dve.sem_inc(s["h_lo_ready"], 2)
                dve.sem_inc(s["prod_ready"], 2)
                dve.sem_inc(s["y_taken"], 2)

                def body(g, u):
                    step = [0]

                    def link(ins):
                        step[0] += 1
                        ins.then_inc(s["gate_step"], 1)
                        dve.wait_ge(s["gate_step"], g * GSTEPS + step[0])

                    def route():
                        dve.wait_ge(s["scores_ready"], g + 1)
                        link(nc.vector.tensor_tensor(biased, scores, ebias_row[:, None, :].broadcast_to([P, TPS, NE]), ALU.add))
                        other = biased[:, :, None, :].broadcast_to([P, TPS, NE, NE])
                        own = biased[:, :, :, None].broadcast_to([P, TPS, NE, NE])
                        nc.vector.tensor_tensor(beats, other, own, ALU.is_gt)
                        link(nc.vector.tensor_tensor(ties, other, own, ALU.is_equal))
                        link(nc.vector.tensor_tensor(ties, ties, tri[:, None].broadcast_to([P, TPS, NE, NE]), ALU.mult))
                        link(nc.vector.tensor_tensor(beats, beats, ties, ALU.add))
                        link(nc.vector.tensor_reduce(rank, beats, AX.X, ALU.add))
                        link(nc.vector.tensor_scalar(rank, rank, 2.0, 0.5 / (WS * HS), ALU.is_lt, ALU.mult))
                        link(nc.vector.tensor_tensor(gates, rank, scores, ALU.mult))

                    def lo(k):
                        dve.wait_ge(s["h_hi_ready"], g * UNITS + k + 1)
                        nc.vector.tensor_tensor(h_lo[:, slot(k), :], prod[:, k % 2, :], h_hi[:, slot(k), :],
                                                ALU.subtract).then_inc(s["h_lo_ready"], 1)

                    def take(job):
                        for half in range(2):
                            hj = 2 * job + half
                            dve.wait_ge(s["y_ready"], g * 2 * JOBS + hj + 1 + 2 * JOBS)
                            dve.wait_ge(s["y_taken"], g * 2 * JOBS + hj + 1)
                            xs = x[:, ds(g * TPS + 2 * half, 2), :]
                            if job == 0:
                                ins = nc.vector.scalar_tensor_tensor(
                                    out=xs, in0=ps[:, 6 + half, :].rearrange("p (t d) -> p t d", t=2), scalar=0.5 / (WS * HS),
                                    in1=xs, op0=ALU.mult, op1=ALU.add)
                            else:
                                for t in range(2):
                                    xs = x[:, ds(g * TPS + 2 * half + t, 1), :].rearrange("p a d -> p (a d)")
                                    ins = nc.vector.scalar_tensor_tensor(
                                        out=xs, in0=ps[:, 6 + half, t * D:(t + 1) * D],
                                        scalar=gates[:, 2 * half + t, job - 1:job], in1=xs, op0=ALU.mult, op1=ALU.add)
                            ins.then_inc(s["y_taken"], 1)

                    for k in range(UNITS):
                        b = 3 + 2 * (k % 2)
                        dve.wait_ge(s["silu_ready"], g * UNITS + k + 1)
                        dve.wait_ge(s["h_lo_ready"], g * UNITS + k + 1)
                        nc.vector.scalar_tensor_tensor(out=prod[:, k % 2, :], in0=ps[:, b, :], scalar=HS / WS,
                                                       in1=silu[:, k % 2, :], op0=ALU.mult, op1=ALU.mult).then_inc(s["prod_ready"], 1)
                        if k >= 1:
                            lo(k - 1)
                        if k == 2:
                            route()
                        if k == 4:
                            ln_stats(g + N0(n) + 1, next_at(g))
                        if k == 6:
                            ln_scale(g + N0(n) + 1, next_at(g))
                        if k >= SU + EU and (k - SU) % EU == 0:
                            take((k - SU) // EU - 1)
                    lo(UNITS - 1)
                    take(NE - 1)
                    xt_lo_of(g + N0(n) + 1, 1 - u)
                    take(NE)
                    dve.wait_ge(s["y_taken"], g * 2 * JOBS + 2 * JOBS + 2)
                    dve.sem_inc(x_updated, 1)
                each_sequence(dve, body)

            def l1ffn(n):
                s = S[n]
                r = Carve()
                h_hi, h_lo = r([FU, SEQ], F16), r([FU, SEQ], F16)
                relu = r([2, SEQ])
                dve.sem_inc(s["h_lo_ready"], 2)
                dve.sem_inc(s["y_taken"], 2)

                def body(g, u):
                    for k in range(FU):
                        dve.wait_ge(s["h_hi_ready"], g * FU + k + 1)
                        nc.vector.tensor_tensor(h_lo[:, k, :], relu[:, k % 2, :], h_hi[:, k, :],
                                                ALU.subtract).then_inc(s["h_lo_ready"], 1)
                        if k == 1:
                            ln_stats(g + N0(n) + 1, next_at(g))
                        if k == 4:
                            ln_scale(g + N0(n) + 1, next_at(g))
                    xt_lo_of(g + N0(n) + 1, 1 - u)
                    for half in range(2):
                        dve.wait_ge(s["y_ready"], g * 2 + half + 3)
                        dve.wait_ge(s["bias_added"], g + 1)
                        xs = x[:, ds(g * TPS + 2 * half, 2), :]
                        nc.vector.scalar_tensor_tensor(out=xs, in0=ps[:, 6 + half, :].rearrange("p (t d) -> p t d", t=2),
                                                       scalar=0.5, in1=xs, op0=ALU.mult, op1=ALU.add).then_inc(s["y_taken"], 1)
                    dve.wait_ge(s["y_taken"], g * 2 + 4)
                    dve.sem_inc(x_updated, 1)
                each_sequence(dve, body)

            def gla(n):
                s, m = S[n], gla_space()
                dve.sem_inc(s["y_taken"], 2)

                def body(g, u):
                    step = [0]

                    def link(ins):
                        step[0] += 1
                        ins.then_inc(s["s_step"], 1)
                        dve.wait_ge(s["s_step"], g * (1 + 2 * TPS) + step[0])

                    dve.wait_ge(s["t_hi"], g + 1)
                    nc.vector.scalar_tensor_tensor(out=m.t_lo[0:LOW], in0=ps[0:LOW, 2, :], scalar=1 / WS, in1=m.t_hi[0:LOW],
                                                   op0=ALU.mult, op1=ALU.subtract).then_inc(s["t_lo"], 1)
                    for j, b in enumerate((2, 7)):
                        dve.wait_ge(s["logits_ready"], g * 2 + j + 1)
                        nc.vector.scalar_tensor_tensor(
                            out=m.lb[:, 2 * j:2 * j + 2], in0=ps[:, b, :].rearrange("p (t d) -> p t d", t=2), scalar=1 / WS,
                            in1=bgk_row[:, None, :].broadcast_to([P, 2, H * DK]), op0=ALU.mult, op1=ALU.add).then_inc(s["lb_ready"], 1)
                    ln_stats(g + N0(n) + 1, next_at(g))
                    dve.wait_ge(s["soft_step"], g * 3 + 3)
                    nc.vector.scalar_tensor_tensor(out=m.lb, in0=m.lb, scalar=0.0, in1=m.soft, op0=ALU.min,
                                                   op1=ALU.subtract).then_inc(s["g_ready"], 1)
                    ln_scale(g + N0(n) + 1, next_at(g))
                    dve.wait_ge(s["exps_ready"], g * 4 + 1)
                    for h in range(2):
                        sl = slice(h * DK, (h + 1) * DK)
                        nc.vector.tensor_tensor(m.qz[sl, :, h], m.q[sl], m.up[sl], ALU.mult).then_inc(s["q_ready"], 1)
                    dve.wait_ge(s["exps_ready"], g * 4 + 2)
                    nc.vector.tensor_tensor(m.k, m.k, m.down, ALU.mult).then_inc(s["k_ready"], 1)
                    dve.wait_ge(s["exps_ready"], g * 4 + 4)
                    for j, b in enumerate((2, 7)):
                        dve.wait_ge(s["kt_ready"], g * 2 + j + 1)
                        sl = m.soft[:, 2 * j:2 * j + 2]
                        nc.vector.scalar_tensor_tensor(out=sl, in0=ps[:, b, :].rearrange("p (t d) -> p t d", t=2), scalar=1 / WS,
                                                       in1=sl, op0=ALU.mult, op1=ALU.mult).then_inc(s["kdec_ready"], 1)
                    dve.wait_ge(s["q_ready"], g * 2 + 4)
                    link(nc.vector.memset(m.s, 0.0))
                    for c in range(TPS):
                        for p in range(GPAIR):
                            ins = nc.vector.tensor_scalar(m.states[:, c, p], m.s[:, p], m.ends[:, p, c, 0:1], None, ALU.mult)
                        link(ins)
                        dve.wait_ge(s["st_ready"], g * TPS + c + 1)
                        for p in range(GPAIR):
                            for h in range(2):
                                sl = slice(h * DK, (h + 1) * DK)
                                at = (2 * p + h) * DV
                                ins = nc.vector.scalar_tensor_tensor(
                                    out=m.s[sl, p], in0=m.s[sl, p], scalar=m.ends[sl, p, c, 1:2],
                                    in1=ps[sl, SB[c], at:at + DV], op0=ALU.mult, op1=ALU.add)
                        link(ins)
                        dve.wait_ge(s["at_ready"], g * TPS + c + 1)
                        nc.vector.tensor_tensor(m.att[:, c].rearrange("p (h t) -> p h t", h=H), ps[:, GB[c], :].rearrange("p (h t) -> p h t", h=H),
                                                const("causal")[:, None, :].broadcast_to([P, H, P]), ALU.mult).then_inc(s["masked"], 1)
                    for c in range(TPS):
                        dve.wait_ge(s["sq_ready"], g * TPS + c + 1)
                        nc.vector.tensor_reduce(m.ss[:, c], m.squares[:, c % 2].rearrange("p (h e) -> p h e", h=H), AX.X,
                                                ALU.add).then_inc(s["ss_ready"], 1)
                    dve.wait_ge(s["orstd_ready"], g + 1)
                    dve.wait_ge(s["gate_done"], g * TPS + TPS)
                    for c in range(TPS):
                        for h in range(H):
                            sl = slice(h * DV, (h + 1) * DV)
                            ins = nc.vector.scalar_tensor_tensor(out=m.gate[:, c, sl], in0=ps[:, GB[c], sl],
                                                                 scalar=m.orstd[:, c, h:h + 1], in1=m.gate[:, c, sl],
                                                                 op0=ALU.mult, op1=ALU.mult)
                        ins.then_inc(s["og_ready"], 1)
                    for c in range(TPS):
                        dve.wait_ge(s["ogt_hi"], g * TPS + c + 1)
                        nc.vector.tensor_tensor(m.o_lo[:, c].rearrange("p h t -> p (h t)"), ps[:, SB[c], :],
                                                m.o_hi[:, c].rearrange("p h t -> p (h t)"), ALU.subtract).then_inc(s["ogt_lo"], 1)
                    xt_lo_of(g + N0(n) + 1, 1 - u)
                    for half in range(2):
                        dve.wait_ge(s["y_ready"], g * 2 + half + 1)
                        xs = x[:, ds(g * TPS + 2 * half, 2), :]
                        nc.vector.scalar_tensor_tensor(out=xs, in0=ps[:, 3 + half, :].rearrange("p (t d) -> p t d", t=2),
                                                       scalar=1 / WS, in1=xs, op0=ALU.mult, op1=ALU.add).then_inc(s["y_taken"], 1)
                    dve.wait_ge(s["y_taken"], g * 2 + 4)
                    dve.sem_inc(x_updated, 1)
                each_sequence(dve, body)

            def win(n):
                s, m = S[n], win_space()
                dve.wait_ge(s["zeroed"], 1)
                dve.sem_inc(s["y_taken"], 2)

                def body(g, u):
                    def softmax(t):
                        i = t % 2
                        sc = ps[:, 2:4, :].rearrange("p a (b k) -> p (a b) k", k=KB)
                        dve.wait_ge(s["sc_ready"], g * TPS + t + 3)
                        nc.vector.tensor_reduce(m.mx, sc, AX.X, ALU.max).then_inc(s["mx_ready"], 1)
                        dve.wait_ge(s["mx_ready"], g * TPS + t + 1)
                        nc.vector.tensor_tensor(m.p[:, i], sc, m.mx[:, :, None].broadcast_to([P, BPT * KT * 2, KB]),
                                                ALU.subtract).then_inc(s["sub_ready"], 1)

                    def normalize(t):
                        dve.wait_ge(s["c_ready"], g * TPS + t + 1)
                        nc.vector.reciprocal(m.rl, ps[:, 0, 0:BPT * KT * 2]).then_inc(s["rl_ready"], 1)
                        dve.wait_ge(s["rl_ready"], g * TPS + t + 1)
                        for h in range(4):
                            sl = slice(h * QB, (h + 1) * QB)
                            c = ps[sl, 6:8, :].rearrange("p a (b k) -> p (a b) k", k=4 * AD)
                            ins = nc.vector.tensor_tensor(
                                m.c[sl].rearrange("p a (b k) -> p (a b) k", k=4 * AD)[:, :, h * AD:(h + 1) * AD],
                                c[:, :, h * AD:(h + 1) * AD], m.rl[sl, :, None].broadcast_to([QB, BPT * KT * 2, AD]), ALU.mult)
                        ins.then_inc(s["cn_ready"], 1)

                    def ct_lo(t):
                        dve.wait_ge(s["ct_hi"], g * TPS + t + 1)
                        sl = slice(t * P, (t + 1) * P)
                        nc.vector.tensor_tensor(m.c_lo[:, :, sl], ps[:, 1, 0:KT * P].rearrange("p (f q) -> p f q", f=KT),
                                                m.c_hi[:, :, sl], ALU.subtract).then_inc(s["ct_lo"], 1)

                    softmax(0)
                    for j in range(VF):
                        dve.wait_ge(s["v_ready"], g * VF + j + 1)
                        for h in range(2):
                            w = 2 * (j - 1 + h)
                            if not 0 <= w < NB:
                                continue
                            sl = slice(h * KB, (h + 1) * KB)
                            ins = nc.vector.scalar_tensor_tensor(
                                out=m.vz[sl, w:w + 2].rearrange("p w f d -> p (w f) d")[:, :, sl],
                                in0=ps[sl, 4 + j % 4, :].rearrange("p (w d) -> p w d", d=P)[:, :, sl], scalar=1 / WS,
                                in1=bv_row[sl].rearrange("p (w d) -> p w d", d=P)[:, :, sl], op0=ALU.mult, op1=ALU.add)
                        ins.then_inc(s["v_copied"], 1)
                    dve.wait_ge(s["v_copied"], g * (VF + 2) + VF)
                    for e, w in enumerate((0, NB - 1)):
                        nc.vector.tensor_scalar(m.vz[:, w], m.vz[:, w], const("edge")[:, e:e + 1], None,
                                                ALU.mult).then_inc(s["v_copied"], 1)
                    ln_stats(g + N0(n) + 1, next_at(g))
                    for t in range(TPS):
                        if t + 1 < TPS:
                            softmax(t + 1)
                        if t == 1:
                            ln_scale(g + N0(n) + 1, next_at(g))
                        normalize(t)
                        if t >= 1:
                            ct_lo(t - 1)
                    ct_lo(TPS - 1)
                    xt_lo_of(g + N0(n) + 1, 1 - u)
                    for half in range(2):
                        dve.wait_ge(s["y_ready"], g * 2 + half + 1)
                        dve.wait_ge(s["bias_added"], g + 1)
                        xs = x[:, ds(g * TPS + 2 * half, 2), :]
                        nc.vector.scalar_tensor_tensor(out=xs, in0=ps[:, 2 + half, :].rearrange("p (t d) -> p t d", t=2),
                                                       scalar=1 / WS, in1=xs, op0=ALU.mult, op1=ALU.add).then_inc(s["y_taken"], 1)
                    dve.wait_ge(s["y_taken"], g * 2 + 4)
                    dve.sem_inc(x_updated, 1)
                each_sequence(dve, body)

            dve.wait_ge(small_loaded, 48)
            dve.wait_ge(ready0, 4)
            dve.wait_ge(x_loaded[0], 16)
            ln_stats(0, 0)
            halves_lo()
            ternary()
            dve.wait_ge(x_loaded[1], 16)
            ln_scale(0, 0, first=True)
            xt_lo_of(0, 0)
            for n, kind in enumerate(SUBLAYERS):
                {"ffn0": ffn0, "l1ffn": l1ffn, "gla": gla, "win": win}[kind](n)

        @block.tensor
        def _(pe):
            def mm3(out_, a, b, start, stop):
                nc.tensor.matmul(out_, a[0], b[0], start=start, stop=False)
                nc.tensor.matmul(out_, a[0], b[1], start=False, stop=False)
                return nc.tensor.matmul(out_, a[1], b[0], start=False, stop=stop)

            def both(w, sl):
                return w[0][:, sl], w[1][:, sl]

            def xt(u, k, sl=slice(0, SEQ)):
                sl = slice(PAD + sl.start, PAD + sl.stop)
                return xt_hi[:, u, k, sl], xt_lo[:, u, k, sl]

            def transposes(m):
                pe.wait_ge(xn_ready, m + 1)
                for k in range(KT):
                    for t in range(TPS):
                        ins = nc.tensor.transpose(ps[:, k, t * P:(t + 1) * P], xn[:, t, k * P:(k + 1) * P], ident)
                ins.then_inc(pt_ready, 1)

            def xt_ready(m):
                pe.wait_ge(xt_hi_ready, m + 1)
                pe.wait_ge(xt_lo_ready, m + 1)

            def ffn0(n):
                s = S[n]
                r = Carve()
                h = r([SU + 4 * EU, SEQ], F16), r([SU + 4 * EU, SEQ], F16)
                pe.sem_inc(s["y_ready"], 2 * JOBS)

                def slot(k):
                    return k if k < SU else SU + (k - SU) % (4 * EU)

                def body(g, u):
                    xt_ready(g + N0(n))
                    for t in range(TPS):
                        for k in range(KT):
                            ins = mm3(ps[:, 0, t * NE:(t + 1) * NE], xt(u, k, slice(t * P, (t + 1) * P)),
                                      both(wr, slice(k * NE, (k + 1) * NE)), k == 0, k == KT - 1)
                    ins.then_inc(s["router_ready"], 1)

                    def up(q):
                        b = 2 + 2 * (q % 2)
                        pe.wait_ge(s["prod_ready"], g * UNITS + q + 1)
                        for half in range(2):
                            for k in range(KT):
                                if q < SU:
                                    w = both((wsh1, wsh2)[half], slice(k * HSH + q * P, k * HSH + (q + 1) * P))
                                else:
                                    e, a = divmod(q - SU, EU)
                                    c = (k * NE + e) * 2 * HE + half * HE + a * P
                                    w = both(wup, slice(c, c + P))
                                ins = mm3(ps[:, b + half, :], w, xt(u, k), k == 0, k == KT - 1)
                        ins.then_inc(s["up_ready"], 1)

                    def down(job):
                        units = range(SU) if job == 0 else range(SU + (job - 1) * EU, SU + job * EU)
                        pe.wait_ge(s["h_hi_ready"], g * UNITS + units[-1] + 1)
                        pe.wait_ge(s["h_lo_ready"], g * UNITS + units[-1] + 3)
                        for half in range(2):
                            pe.wait_ge(s["y_taken"], g * 2 * JOBS + 2 * job + half + 1)
                            for t in range(2 * half, 2 * half + 2):
                                sl = slice(t * P, (t + 1) * P)
                                for q in units:
                                    w = both(wsh3, slice(q * D, (q + 1) * D)) if job == 0 else \
                                        both(wdn, slice((q - SU) * D, (q - SU + 1) * D))
                                    ins = mm3(ps[:, 6 + half, (t % 2) * D:(t % 2 + 1) * D],
                                              (h[0][:, slot(q), sl], h[1][:, slot(q), sl]), w,
                                              q == units[0], q == units[-1])
                            ins.then_inc(s["y_ready"], 1)

                    for q in range(SU):
                        up(q)
                    for e in range(NE):
                        for a in range(EU):
                            up(SU + e * EU + a)
                        down(e)
                    pe.wait_ge(s["scores_ready"], g + 1)
                    transposes(g + N0(n) + 1)
                    down(NE)
                each_sequence(pe, body)

            def l1ffn(n):
                s = S[n]
                r = Carve()
                h = r([FU, SEQ], F16), r([FU, SEQ], F16)
                pe.sem_inc(s["y_ready"], 2)

                def body(g, u):
                    xt_ready(g + N0(n))
                    for q in range(FU):
                        if q >= 4:
                            pe.wait_ge(s["relu_ready"], g * FU + q - 3)
                        for k in range(KT):
                            w = w1q[:, k * FF + q * P:k * FF + (q + 1) * P]
                            nc.tensor.matmul(ps[:, 2 + q % 4, :], w, xt_hi[:, u, k, TOK], start=(k == 0), stop=False)
                            ins = nc.tensor.matmul(ps[:, 2 + q % 4, :], w, xt_lo[:, u, k, TOK], start=False, stop=(k == KT - 1))
                        ins.then_inc(s["up_ready"], 1)
                    transposes(g + N0(n) + 1)
                    pe.wait_ge(s["h_hi_ready"], g * FU + FU)
                    pe.wait_ge(s["h_lo_ready"], g * FU + FU + 2)
                    for half in range(2):
                        pe.wait_ge(s["y_taken"], g * 2 + half + 1)
                        for t in range(2 * half, 2 * half + 2):
                            sl = slice(t * P, (t + 1) * P)
                            for q in range(FU):
                                o = ps[:, 6 + half, (t % 2) * D:(t % 2 + 1) * D]
                                w = w2q[:, q * D:(q + 1) * D]
                                nc.tensor.matmul(o, h[0][:, q, sl], w, start=(q == 0), stop=False)
                                ins = nc.tensor.matmul(o, h[1][:, q, sl], w, start=False, stop=(q == FU - 1))
                        ins.then_inc(s["y_ready"], 1)
                each_sequence(pe, body)

            def gla(n):
                s, m = S[n], gla_space()

                def body(g, u):
                    def project(out_, w, c, n_, transposed=None):
                        for k in range(KT):
                            wk = both(w, slice(k * (w[0].shape[1] // KT) + c, k * (w[0].shape[1] // KT) + c + n_))
                            if transposed is None:
                                ins = mm3(out_, wk, xt(u, k), k == 0, k == KT - 1)
                            else:
                                ins = mm3(out_, xt(u, k, slice(transposed * P, (transposed + 1) * P)), wk, k == 0, k == KT - 1)
                        return ins

                    xt_ready(g + N0(n))
                    pe.wait_ge(s["y_taken"], g * 2 + 2)
                    project(ps[0:LOW, 2, :], gk1, 0, LOW).then_inc(s["t_ready"], 1)
                    for j in range(2 * GPAIR):
                        project(ps[:, 3 + j, :], gqk, j * P, P).then_inc(s["qk_ready"], 1)
                    pe.wait_ge(s["t_hi"], g + 1)
                    pe.wait_ge(s["t_lo"], g + 1)
                    for j, b in enumerate((2, 7)):
                        for t in range(2):
                            sl = slice((2 * j + t) * P, (2 * j + t + 1) * P)
                            ins = mm3(ps[:, b, t * H * DK:(t + 1) * H * DK], (m.t_hi[0:LOW, sl], m.t_lo[0:LOW, sl]),
                                      (gk2[0][:, :], gk2[1][:, :]), True, True)
                        ins.then_inc(s["logits_ready"], 1)
                    for c in range(TPS):
                        pe.wait_ge(s["qk_copied"], g * 2 * GPAIR + c + 1)
                        project(ps[:, GB[c], :], gv, 0, H * DV, c).then_inc(s["v_ready"], 1)
                    for j, b in enumerate((2, 7)):
                        pe.wait_ge(s["lb_ready"], g * 2 + j + 1)
                        for t in range(2):
                            ins = project(ps[:, b, t * H * DK:(t + 1) * H * DK], gqk, H * DK, H * DK, 2 * j + t)
                        ins.then_inc(s["kt_ready"], 1)
                    pe.wait_ge(s["g_ready"], g + 1)
                    pe.wait_ge(s["v_copied"], g * TPS + TPS)
                    for p in range(GPAIR):
                        for c in range(TPS):
                            gp = m.lb[:, c, p * P:(p + 1) * P]
                            nc.tensor.matmul(ps[:, 3 + p, c * P:(c + 1) * P], gp, const("cumref"), start=True, stop=True)
                            at = (p * TPS + c) * 2
                            nc.tensor.matmul(ps[:, 0, at:at + 2], gp, const("ends"), start=True, stop=True)
                    for c in range(TPS):
                        ins = nc.tensor.matmul(ps[:, 5 + c // 2, (c % 2) * 256:(c % 2 + 1) * 256], const("after"), m.lb[:, c],
                                               start=True, stop=True)
                    ins.then_inc(s["cum_ready"], 1)
                    pe.wait_ge(s["kdec_ready"], g * 2 + 2)
                    for c in range(TPS):
                        for p in range(GPAIR):
                            ins = nc.tensor.matmul(ps[:, SB[c], p * 256:(p + 1) * 256], m.soft[:, c, p * P:(p + 1) * P],
                                                   m.v[:, c, p * 256:(p + 1) * 256], start=True, stop=True)
                        ins.then_inc(s["st_ready"], 1)
                    pe.wait_ge(s["q_ready"], g * 2 + 4)
                    pe.wait_ge(s["k_ready"], g + 1)
                    for c in range(TPS):
                        sl = slice(c * P, (c + 1) * P)
                        for p in range(GPAIR):
                            ins = nc.tensor.matmul(ps[:, GB[c], p * 256:(p + 1) * 256], m.k[:, p, sl], m.qz[:, p, :, sl],
                                                   start=True, stop=True)
                        ins.then_inc(s["at_ready"], 1)
                    for c in range(TPS):
                        pe.wait_ge(s["masked"], g * TPS + c + 1)
                        project(ps[:, GB[c], :], gg, 0, H * DV, c).then_inc(s["gate_ready"], 1)
                    for c in range(TPS):
                        pe.wait_ge(s["gate_done"], g * TPS + c + 1)
                        for h in range(H):
                            o = ps[:, GB[c], h * DV:(h + 1) * DV]
                            nc.tensor.matmul(o, m.att[:, c, h * P:(h + 1) * P], m.v[:, c, h * DV:(h + 1) * DV],
                                             start=True, stop=False)
                            ins = nc.tensor.matmul(o, m.qz[:, h // 2, h % 2, c * P:(c + 1) * P], m.states[:, c, h // 2],
                                                   start=False, stop=True)
                        ins.then_inc(s["o_ready"], 1)
                    for c in range(TPS):
                        pe.wait_ge(s["og_ready"], g * TPS + c + 1)
                        for h in range(H):
                            ins = nc.tensor.transpose(ps[:, SB[c], h * P:(h + 1) * P], m.gate[:, c, h * DV:(h + 1) * DV], ident)
                        ins.then_inc(s["ogt_ready"], 1)
                    for half in range(2):
                        pe.wait_ge(s["ogt_hi"], g * TPS + 2 * half + 2)
                        pe.wait_ge(s["ogt_lo"], g * TPS + 2 * half + 2)
                        for t in range(2):
                            c = 2 * half + t
                            for h in range(H):
                                ins = mm3(ps[:, 3 + half, t * D:(t + 1) * D], (m.o_hi[:, c, h], m.o_lo[:, c, h]),
                                          both(go, slice(h * D, (h + 1) * D)), h == 0, h == H - 1)
                        ins.then_inc(s["y_ready"], 1)
                    transposes(g + N0(n) + 1)
                each_sequence(pe, body)

            def win(n):
                s, m = S[n], win_space()
                pe.sem_inc(s["sc_ready"], 2)
                pe.wait_ge(s["zeroed"], 1)

                def body(g, u):
                    xt_ready(g + N0(n))
                    for j in range(2 * KT):
                        if j < 2:
                            pe.wait_ge(s["y_taken"], g * 2 + j + 1)
                        for k in range(KT):
                            c = k * 3 * D + j * P
                            ins = mm3(ps[:, 2 + j, :], both(aqkv, slice(c, c + P)), xt(u, k), k == 0, k == KT - 1)
                        ins.then_inc(s["qk_ready"], 1)

                    def scores(t):
                        pe.wait_ge(s["qz_ready"], g * TPS + t + 1)
                        for b in range(2):
                            nc.tensor.matmul(ps[:, 2 + b, :], ident16[:], window16[:], start=True, stop=False, skip_group_check=True)
                            for w in range(2):
                                for f in range(KT):
                                    for hg in range(2):
                                        blk = 2 * b + w
                                        at = ((w * KT + f) * 2 + hg) * KB
                                        key = (t * BPT + blk) * QB
                                        ins = nc.tensor.matmul(
                                            ps[:, 2 + b, at:at + KB], m.qz[:, t % 2 * KT + f, blk, 4 * hg:4 * hg + 4].rearrange("p h q -> p (h q)"),
                                            m.k[:, f, key:key + KB], start=False, stop=True, skip_group_check=True)
                        ins.then_inc(s["sc_ready"], 1)

                    def turn(t):
                        pe.wait_ge(s["exp_ready"], g * TPS + t + 1)
                        if t == 0:
                            pe.wait_ge(s["v_copied"], g * (VF + 2) + VF + 2)
                        for j in range(BPT * KT):
                            ins = nc.tensor.transpose(ps[:, 4 + j // 4, (j % 4) * P:(j % 4 + 1) * P],
                                                      m.p[:, t % 2, 2 * j:2 * j + 2].rearrange("p a b -> p (a b)"), ident)
                        ins.then_inc(s["pt_ready"], 1)

                    def values(t):
                        pe.wait_ge(s["pt_copied"], g * TPS + t + 1)
                        if t >= 1:
                            pe.wait_ge(s["cn_ready"], g * TPS + t)
                        for j in range(BPT * KT):
                            w = m.pt[:, t % 2, j]
                            nc.tensor.matmul(ps[:, 6 + j // 4, (j % 4) * P:(j % 4 + 1) * P], w,
                                             m.vz[:, t * BPT + j // KT, j % KT], start=True, stop=True)
                            ins = nc.tensor.matmul(ps[:, 0, 2 * j:2 * j + 2], w, const("hgsum"), start=True, stop=True)
                        ins.then_inc(s["c_ready"], 1)

                    def context(t):
                        pe.wait_ge(s["cn_ready"], g * TPS + t + 1)
                        if t >= 1:
                            pe.wait_ge(s["ct_lo"], g * TPS + t)
                        for j in range(BPT * KT):
                            at = (j % KT) * P + (j // KT) * QB
                            ins = nc.tensor.matmul(ps[:, 1, at:at + QB], m.c[:, j], const("fold"), start=True, stop=True)
                        ins.then_inc(s["ct_ready"], 1)

                    pe.wait_ge(s["qk_copied"], g * 2 * KT + 2 * KT)
                    scores(0)
                    for j in range(VF):
                        if j >= 4:
                            pe.wait_ge(s["v_copied"], g * (VF + 2) + j - 3)
                        for w in range(2):
                            at = (2 * j + w) * QB
                            lhs, half = slice(at - 2 * QB, at - 2 * QB + P), slice(0, P)
                            if j == 0:
                                lhs, half = slice(at, at + KB), slice(KB, P)
                            elif j == VF - 1:
                                lhs, half = slice(at - 2 * QB, at - 2 * QB + KB), slice(0, KB)
                            for k in range(KT):
                                c = k * 3 * D + 2 * D
                                ins = mm3(ps[half, 4 + j % 4, w * D:(w + 1) * D], (xt_hi[:, u, k, lhs], xt_lo[:, u, k, lhs]),
                                          both(aqkv, slice(c, c + D)), k == 0, k == KT - 1)
                        ins.then_inc(s["v_ready"], 1)
                    for t in range(TPS):
                        turn(t)
                        if t >= 1:
                            context(t - 1)
                        if t + 1 < TPS:
                            pe.wait_ge(s["sub_ready"], g * TPS + t + 1)
                            scores(t + 1)
                        values(t)
                    context(TPS - 1)
                    pe.wait_ge(s["ct_hi"], g * TPS + TPS)
                    pe.wait_ge(s["ct_lo"], g * TPS + TPS)
                    pe.wait_ge(s["sub_ready"], g * TPS + TPS)
                    transposes(g + N0(n) + 1)
                    for half in range(2):
                        for t in range(2 * half, 2 * half + 2):
                            sl = slice(t * P, (t + 1) * P)
                            for f in range(KT):
                                ins = mm3(ps[:, 2 + half, (t % 2) * D:(t % 2 + 1) * D], (m.c_hi[:, f, sl], m.c_lo[:, f, sl]),
                                          both(ao, slice(f * D, (f + 1) * D)), f == 0, f == KT - 1)
                        ins.then_inc(s["y_ready"], 1)
                each_sequence(pe, body)

            pe.wait_ge(small_loaded, 48)
            pe.wait_ge(ready0, 4)
            pe.wait_ge(tern, 2)
            ones = const("ones")
            nc.tensor.matmul(ps[:, 7, 0:2], ones, tsum[:], start=True, stop=True).then_inc(tern_sum, 1)
            pe.wait_ge(w_lo_done, NCH)
            pe.wait_ge(tern, 10)
            transposes(0)
            for n, kind in enumerate(SUBLAYERS):
                if n:
                    pe.wait_ge(x_updated, N0(n))
                {"ffn0": ffn0, "l1ffn": l1ffn, "gla": gla, "win": win}[kind](n)


def constants(np):
    p = np.arange(P)[:, None]
    f = np.arange(P)[None, :]
    q, kk = p % QB, np.arange(KB)[None, :]
    e, j = np.arange(NE)[:, None], np.arange(NE)[None, :]
    c = {
        "ident": p == f,
        "ones": np.ones((P, P)),
        "causal": f >= p,
        "cumref": ((p <= f) * 1.0 - (p < P // 2)) / GATE_NORM,
        "after": (p > f) / GATE_NORM,
        "ends": np.concatenate([(p < P // 2) * 1.0, np.ones((P, 1))], 1) / GATE_NORM,
        "tri": np.broadcast_to((j < e).reshape(1, NE * NE), (P, NE * NE)),
        "window": np.where((kk >= q) & (kk <= q + 2 * PAD), 0.0, MASKED),
        "fold": q == np.arange(QB)[None, :],
        "hgsum": p // KB == np.arange(2)[None, :],
        "heads": p // AD == np.arange(8)[None, :],
        "edge": np.concatenate([p % KB >= PAD, p % KB < KB - PAD], 1),
    }
    return np.concatenate([np.asarray(c[n], np.float32) for n in CONST_COLS], 1)


def laid_out(np, a):
    def tiles(w):
        k, n = w.shape
        return np.ascontiguousarray(w.reshape(k // P, P, n).transpose(1, 0, 2).reshape(P, -1))

    def down(v):
        return v.reshape(-1, P).T

    qkv = a["L1_attn_w_qkv"].reshape(AH, 3, AD, D).transpose(1, 0, 2, 3).reshape(3 * D, D)
    bqkv = a["L1_attn_b_qkv"].reshape(AH, 3, AD).transpose(1, 0, 2).reshape(3, D)
    rows = np.concatenate([a["L0_attn_bgk2"], a["L1_ffn_b2"], a["L1_attn_b_out"], bqkv[2], bqkv[2],
                           a["L0_ffn_expert_bias"]])
    return {
        "x": a["L0_attn_x"].reshape(-1, D),
        "consts": constants(np),
        "rows": np.ascontiguousarray(np.broadcast_to(rows[None], (P, rows.size))),
        "cols": np.ascontiguousarray(np.concatenate([down(a["L1_ffn_b1"]), down(bqkv[0]), down(bqkv[1]),
                                                     down(a["L0_attn_rms_w"])], 1)),
        "w_sh1": tiles(a["L0_ffn_shared_w1"].T), "w_sh2": tiles(a["L0_ffn_shared_w2"].T),
        "w_sh3": tiles(a["L0_ffn_shared_w3"].T), "w_r": tiles(a["L0_ffn_router_w"].T),
        "w_up": tiles(a["L0_ffn_w12"].reshape(-1, D).T),
        "w_dn": tiles(a["L0_ffn_w3"].transpose(0, 2, 1).reshape(-1, D)),
        "g_qk": tiles(np.concatenate([a["L0_attn_Wq"], a["L0_attn_Wk"]]).T),
        "g_v": tiles(a["L0_attn_Wv"].T), "g_g": tiles(a["L0_attn_Wg"].T),
        "g_k1": tiles(a["L0_attn_Wgk1"].T), "g_k2": np.ascontiguousarray(a["L0_attn_Wgk2"].T),
        "g_o": tiles(a["L0_attn_Wout"].T),
        "a_qkv": tiles(qkv.T), "a_o": tiles(a["L1_attn_w_out"].T),
        "w_1": tiles(a["L1_ffn_W1"].T), "w_2": tiles(a["L1_ffn_W2"].T),
    }


def kernel(**inputs):
    import numpy as np
    import concourse.bacc as bacc
    from concourse.bass_utils import run_bass_kernel_spmd

    nc = bacc.Bacc("TRN2", target_bir_lowering=False, num_devices=1)
    arrays = laid_out(np, {k: np.asarray(v) for k, v in inputs.items()})
    T = {n: nc.dram_tensor(f"in_{n}", v.shape, mybir.dt.from_np(v.dtype), kind="ExternalInput").ap()
         for n, v in arrays.items()}
    out = nc.dram_tensor("out_x", (NSEQ * SEQ, D), F32, kind="ExternalOutput").ap()
    build(nc, T, out)
    r = run_bass_kernel_spmd(nc, [{f"in_{n}": v for n, v in arrays.items()}], core_ids=[0])
    return r.results[0]["out_x"].reshape(NSEQ, SEQ, D)
```

```python
from contextlib import ExitStack

import concourse.bass as bass
from concourse import mybir

P = 128
D = 256
KT = D // P
NSEQ, SEQ = 8, 512
TPS = SEQ // P
EPS = 1e-5
WS = 64.0
HS = 16.0

NE, HE = 8, 256
HSH = 1024
SU, EU = HSH // P, HE // P
TOPK = 2
REGION = NSEQ * SEQ + P
TILES = NSEQ * SEQ * TOPK // P + NE - 1
TILES += -TILES % 4
DUMP = TILES - NSEQ * SEQ * TOPK // P
ROWS = NE * REGION + DUMP * P

FF = 1024
FU = FF // P
PRODS = 4
RELUS = 4

H, DK, DV = 4, 64, 128
GPAIR = H // 2
LOW = 32
GATE_NORM = 32.0

AH, AD = 16, 16
PAD = 16
QB, KB = 32, 64
NB = SEQ // QB
BPT = P // QB
HG = AH // 4
VF = NB // 2 + 1
MASKED = -1e30

ALU = mybir.AluOpType
ACT = mybir.ActivationFunctionType
AX = mybir.AxisListType
F32 = mybir.dt.float32
F16 = mybir.dt.float16
I32 = mybir.dt.int32


class Space:
    pass


SUBLAYERS = ("ffn0", "gla", "ffn0", "l1ffn", "win", "l1ffn")

CONST_COLS = {"ident": 128, "ones": 128, "causal": 128, "cumref": 128, "after": 128, "ends": 2, "tri": NE * NE,
              "window": 64, "fold": 32, "hgsum": 2, "edge": 2, "heads": 8, "iota": TILES, "regions": NE}


def const_at(name):
    at = 0
    for n, w in CONST_COLS.items():
        if n == name:
            return slice(at, at + w)
        at += w


NCONST = sum(CONST_COLS.values())


def ds(at, n):
    return bass.ds(at, n)


def build(nc, T, out):
    ctx = ExitStack()
    with ctx:
        def sb(name, shape, dt=F32):
            return ctx.enter_context(nc.sbuf_tensor(name, shape, dt))

        def sem(name):
            return ctx.enter_context(nc.semaphore(name))

        x = sb("x", [P, NSEQ * TPS, D])
        consts = sb("consts", [P, NCONST])
        window16 = sb("window16", [P, 8, KB], mybir.dt.bfloat16)
        ident16 = sb("ident16", [P, P], mybir.dt.bfloat16)

        def const(name):
            return consts[:, const_at(name)]

        ident = const("ident")

        def pair(name, cols, rows=P):
            return sb(name + "_hi", [rows, cols], F16), sb(name + "_lo", [rows, cols], F16)

        wup = pair("wup", KT * NE * 2 * HE)
        wsh1 = pair("wsh1", KT * HSH)
        wsh2 = pair("wsh2", KT * HSH)
        wsh3 = pair("wsh3", SU * D)
        wdn = pair("wdn", NE * EU * D)
        wr = pair("wr", KT * NE)
        gqk = pair("gqk", KT * 2 * H * DK)
        gv = pair("gv", KT * H * DV)
        gg = pair("gg", KT * H * DV)
        gk1 = pair("gk1", KT * LOW)
        gk2 = pair("gk2", H * DK, LOW)
        go = pair("go", H * D)
        aqkv = pair("aqkv", KT * 3 * D)
        ao = pair("ao", KT * D)
        w1q = sb("w1q", [P, KT * FF], F16)
        w2q = sb("w2q", [P, FU * D], F16)
        rows = sb("rows", [P, 5 * D + NE])
        bgk_row, b2_row, bo_row = (rows[:, n * D:(n + 1) * D] for n in range(3))
        bv_row = rows[:, 3 * D:5 * D]
        ebias_row = rows[:, 5 * D:]
        cols = sb("cols", [P, FU + 2 * KT + 1])
        b1_col, bq_col, bk_col = cols[:, 0:FU], cols[:, FU:FU + KT], cols[:, FU + KT:FU + 2 * KT]
        rms_col = cols[:, FU + 2 * KT:]

        xn = sb("xn", [P, TPS, D + 1])
        expert_rows = sb("expert_rows", [P, TOPK, (NSEQ + 2) * TPS])
        gather_rows = sb("gather_rows", [P, 2, TOPK, TPS], I32)
        yg = sb("yg", [P, TPS, D])
        stats = sb("stats", [P, TPS, 6])
        mv = sb("mv", [P, TPS, 2])
        rstd = sb("rstd", [P, TPS])
        tsum, thr = sb("tsum", [P, 2]), sb("thr", [P, 2, 2])
        eps = sb("eps", [P, TPS])
        neghalf = sb("neghalf", [P, 4 * TPS])
        XW = SEQ + 2 * PAD
        xt_hi = sb("xt_hi", [P, 2, KT, XW], F16)
        xt_lo = sb("xt_lo", [P, 2, KT, XW], F16)
        TOK = slice(PAD, PAD + SEQ)

        WORK = 44416
        work = sb("work", [P, WORK // 4])

        class Carve:
            def __init__(self, base=None):
                self.base = work if base is None else base
                self.room = (4 if base is None else 2) * self.base.shape[1]
                self.at = 0

            def __call__(self, shape, dt=F32):
                n = 1
                for s in shape:
                    n *= s
                size = (2 if dt == F16 else 4) * n
                each = 4 if self.base is work else 2
                a = self.base[:, self.at // each:(self.at + size) // each]
                self.at += size
                assert self.at <= self.room, self.at
                if dt != (F32 if each == 4 else F16):
                    a = a.bitcast(dt)
                names = "abcd"[:len(shape)]
                if len(shape) == 1:
                    return a
                return a.rearrange(f"p ({' '.join(names)}) -> p {' '.join(names)}",
                                   **{n: s for n, s in zip(names[1:], shape[1:])})

        ps = ctx.enter_context(nc.psum_tensor("ps", [P, 8, 512], F32))

        x_loaded = [sem(f"x_loaded{n}") for n in range(2)]
        small_loaded = sem("small_loaded")
        x_stored = sem("x_stored")
        ready0 = sem("constants_ready")
        NST = 4
        staged = [sem(f"staged{n}") for n in range(NST)]
        w_hi_done, w_lo_done = sem("w_hi_done"), sem("w_lo_done")
        tern = sem("ternary_steps")
        tern_sum = sem("ternary_sum")
        mv_ready, rstd_ready, xn_ready = sem("mv_ready"), sem("rstd_ready"), sem("xn_ready")
        ln_step = sem("ln_step")
        pt_ready, xt_hi_ready, xt_lo_ready = sem("pt_ready"), sem("xt_hi_ready"), sem("xt_lo_ready")
        x_updated = sem("x_updated")
        rstd_step = sem("rstd_step")
        pool_stood = sem("pool_wait_stood_alone")
        stood = sem("wait_stood_alone")

        def names(prefix, text):
            return {n: sem(f"{prefix}_{n}") for n in text.split()}

        S = []
        for n, kind in enumerate(SUBLAYERS):
            text = {
                "ffn0": "router_ready scores_ready gate_step mask_ready pos_ready base_set rows_ready gate_set scattered0 "
                        "scattered1 up_ready silu_ready prod_ready h_hi_ready h_lo_ready y_ready y_taken "
                        "zeros_set zero_filled tab_step tab_ready tile_in0 tile_in1 tile_in2 tile_in3 tile_turned "
                        "tile_hi tile_lo tile_up tile_silu tile_prod th_turned th_hi th_lo tile_down tile_y tile_out0 "
                        "tile_out1 tile_out2 tile_out3 rows_step gathered0 gathered1 combined",
                "l1ffn": "up_ready relu_ready h_hi_ready h_lo_ready y_ready y_taken bias_added",
                "gla": "t_ready t_hi t_lo qk_ready qk_copied logits_ready lb_ready soft_step g_ready v_ready v_copied "
                       "kt_ready cum_ready exps_ready q_ready k_ready kdec_ready at_ready masked st_ready s_step "
                       "gate_ready gate_done o_ready sq_ready ss_ready orstd_step orstd_ready og_ready ogt_ready "
                       "ogt_hi ogt_lo y_ready y_taken",
                "win": "zeroed qk_ready qk_copied qz_ready v_ready v_copied sc_ready mx_ready sub_ready "
                       "exp_ready pt_ready pt_copied c_ready rl_ready cn_ready ct_ready ct_hi ct_lo y_ready "
                       "y_taken bias_added",
            }[kind]
            if kind in SUBLAYERS[:n] and kind == "ffn0":
                S.append(S[SUBLAYERS.index(kind)])
            else:
                S.append(names(f"{kind}{n}", text))

        N0 = lambda n: n * NSEQ

        def earlier(n):
            return SUBLAYERS[:n].count("ffn0")


        SPLIT = [("w_sh1", wsh1, KT * HSH, P), ("w_sh2", wsh2, KT * HSH, P), ("w_r", wr, KT * NE, P),
                 ("w_up", wup, KT * NE * 2 * HE, P), ("w_sh3", wsh3, SU * D, P), ("w_dn", wdn, NE * EU * D, P),
                 ("g_qk", gqk, KT * 2 * H * DK, P), ("g_v", gv, KT * H * DV, P), ("g_g", gg, KT * H * DV, P),
                 ("g_k1", gk1, KT * LOW, P), ("g_k2", gk2, H * DK, LOW), ("g_o", go, H * D, P),
                 ("a_qkv", aqkv, KT * 3 * D, P), ("a_o", ao, KT * D, P)]
        CH = 2048
        chunks = [(name, dst, c, min(CH, n - c), r) for name, dst, n, r in SPLIT for c in range(0, n, CH)]
        TERN = [("w_1", w1q), ("w_2", w2q)]
        stage = Carve()([NST, CH])
        NCH = len(chunks)
        loads = [(name, c, n, r) for name, _, c, n, r in chunks] + [(name, 0, CH, P) for name, _ in TERN]

        def load_done(eng, m):
            eng.wait_ge(staged[m % NST], 16 * (m // NST + 1))

        def ffn0_space():
            r, at = Carve(), Carve()
            m = Space()
            m.h_hi, m.h_lo = r([SU, SEQ], F16), r([SU, SEQ], F16)
            m.t_hi, m.t_lo = at([2, KT, P], F16), at([2, KT, P], F16)
            m.t_silu, m.t_prod = at([2, HE]), at([2, HE])
            m.th_hi, m.th_lo = at([2, EU, P], F16), at([2, EU, P], F16)
            m.t_y = at([4, D])
            assert at.at <= r.at
            m.silu, m.prod = r([2, SEQ]), r([PRODS, SEQ])
            m.scores, m.biased, m.mask, m.rank, m.row = (r([TPS, NE]) for _ in range(5))
            m.beats, m.ties = r([TPS, NE, NE]), r([TPS, NE, NE])
            m.onehot, m.picked = r([TOPK, TPS * NE]), r([TOPK, TPS * NE])
            m.gate, m.scatter_rows = r([TOPK, TPS]), r([TOPK, TPS], I32)
            m.base = r([NE])
            m.tile_x, m.zeros = r([4, D + 1]), r([D + 1])
            m.count, m.tiles, m.end, m.jump = (r([NE]) for _ in range(4))
            m.more = r([NE, NSEQ * TPS])
            m.over, m.sums = r([TILES, NE]), r([2, TILES])
            m.before = r([NE, NE])
            m.table = r([2 * TILES + NE], I32)
            return m

        def yg_buffers(n):
            if "ffn0" in SUBLAYERS[n:]:
                return [yg[:, :, :]]
            at = Carve(wup[0])
            return [at([TPS, D]), at([TPS, D])]

        def is_last(g):
            return isinstance(g, int) and g == NSEQ - 1

        def after_ffn0(n):
            return n > 0 and SUBLAYERS[n - 1] == "ffn0"

        def l1ffn_space():
            r = Carve()
            return r([2, FU, SEQ], F16), r([2, FU, SEQ], F16), r([RELUS, SEQ])

        def gla_space():
            r = Carve()
            m = Space()
            m.t_hi, m.t_lo = r([SEQ], F16), r([SEQ], F16)
            m.q = r([GPAIR, SEQ])
            m.states = m.q.rearrange("p a (b c) -> p (a b) c", c=DV).rearrange("p (c a) d -> p c a d", a=GPAIR)
            m.k = r([GPAIR, SEQ])
            m.squares = m.k
            m.v = r([TPS, H * DV])
            m.lb = r([TPS, H * DK])
            m.soft = r([TPS, H * DK])
            at = Carve()
            at.at = r.at - 2 * 4 * TPS * H * DK
            m.gate = at([TPS, H * DV])
            m.up, m.down = r([GPAIR, SEQ]), r([GPAIR, SEQ])
            at.at = r.at - 2 * 4 * GPAIR * SEQ
            m.att = at([TPS, H * P])
            at.at = r.at - 2 * 4 * GPAIR * SEQ
            m.o_hi, m.o_lo = at([TPS, H, P], F16), at([TPS, H, P], F16)
            m.qz = r([GPAIR, 2, SEQ])
            m.ends = r([GPAIR, TPS, 2])
            m.s = r([GPAIR, DV])
            m.ss, m.orstd = r([TPS, H]), r([TPS, H])
            return m

        def win_space():
            r = Carve()
            m = Space()
            m.vz = Carve(wup[0])([NB, KT, P])
            m.qz = Carve(wup[1])([2 * KT, BPT, 8, QB])
            m.q = r([KT, SEQ])
            m.k = r([KT, XW])
            m.p = r([2, BPT * KT * 2, KB])
            m.pt = r([2, BPT * KT, P])
            m.c = r([BPT * KT, P])
            m.c_hi, m.c_lo = r([KT, SEQ], F16), r([KT, SEQ], F16)
            m.mx, m.rl = r([BPT * KT * 2]), r([BPT * KT * 2])
            return m

        STORE_LAG = 6
        expert_x = nc.dram_tensor("expert_x", (ROWS, D + 1), F32, kind="Internal").ap()
        expert_y = nc.dram_tensor("expert_y", (TILES * P, D), F32, kind="Internal").ap()

        GB = (3, 4, 5, 6)
        SB = (0, 1, 2, 7)

        block = ctx.enter_context(nc.Block())

        def each_sequence(eng, body, peel=False):
            with eng.Fori(0, NSEQ // 2 - peel) as i:
                for u in range(2):
                    body(2 * i + u, u)
            if peel:
                for u in range(2):
                    body(NSEQ - 2 + u, u)

        def each_tile(eng, step, depth):
            def has_of(i):
                return lambda back: 0 <= i - back < TILES
            first = 8
            for i in range(first):
                step(i, i // 4, i % 4, has_of(i))
            with eng.Fori(first // 4, TILES // 4) as b:
                for u in range(4):
                    step(4 * b + u, b, u, lambda back: True)
            for i in range(TILES, TILES + depth):
                step(i, i // 4, i % 4, has_of(i))

        def skewed(eng, step):
            step(0, 0, True, False)
            with eng.Fori(0, NSEQ // 2 - 1) as i:
                step(2 * i + 1, 1, True, True)
                step(2 * i + 2, 0, True, True)
            step(NSEQ - 1, 1, True, True)
            step(NSEQ, 0, False, True)

        @block.sync
        def _(sp):
            sp.dma_start(consts[:], T["consts"]).then_inc(small_loaded, 16)
            xd = T["x"].rearrange("(t p) d -> p t d", p=P)
            sp.dma_start(x[:, 0:TPS, :], xd[:, 0:TPS, :]).then_inc(x_loaded[0], 16)
            sp.dma_start(rows[:], T["rows"]).then_inc(small_loaded, 16)
            sp.dma_start(cols[:], T["cols"]).then_inc(small_loaded, 16)
            for m, (name, c, n, r) in enumerate(loads):
                if m >= NST:
                    sp.wait_ge(w_lo_done, m - NST + 1)
                sp.dma_start(stage[0:r, m % NST, 0:n], T[name][:, c:c + n]).then_inc(staged[m % NST], 16)
                if m == 3:
                    sp.dma_start(x[:, TPS:, :], xd[:, TPS:, :]).then_inc(x_loaded[1], 16)
            def ffn0(n):
                s, m = S[n], ffn0_space()
                G0, T0 = earlier(n) * NSEQ, earlier(n) * TILES
                sp.wait_ge(s["zeros_set"], 1 + earlier(n))
                for d in range(DUMP):
                    at = NE * REGION + d * P
                    sp.dma_start(expert_x[at:at + P, :], m.zeros).then_inc(s["zero_filled"], 16)
                sp.wait_ge(s["tab_ready"], 3 * (1 + earlier(n)))
                for e in range(NE):
                    row = sp.value_load(m.table[0:1, 2 * TILES + e:2 * TILES + e + 1], min_val=0, max_val=ROWS - P)
                    sp.dma_start(expert_x[ds(row, P), :], m.zeros).then_inc(s["zero_filled"], 16)
                sp.wait_ge(s["zero_filled"], 16 * (DUMP + NE) * (1 + earlier(n)))
                for r in range(TOPK):
                    sp.wait_ge(s[f"scattered{r}"], 16 * (NSEQ + G0) * TPS)

                def step(i, b, u, has):
                    if has(0):
                        row = sp.value_load(m.table[0:1, ds(i, 1)], min_val=0, max_val=ROWS - P)
                        if not isinstance(i, int) or i >= 4:
                            sp.wait_ge(s["tile_prod"], i - 3 + T0)
                        sp.dma_start(m.tile_x[:, u, :], expert_x[ds(row, P), :]).then_inc(s[f"tile_in{u}"], 16)
                    if has(STORE_LAG):
                        j, v = i - STORE_LAG, (u - STORE_LAG) % 4
                        sp.wait_ge(s["tile_y"], j + 1 + T0)
                        sp.dma_start(expert_y[ds(j * P, P), :], m.t_y[:, v, :]).then_inc(s[f"tile_out{v}"], 16)
                each_tile(sp, step, STORE_LAG)

            for n, kind in enumerate(SUBLAYERS):
                if kind == "ffn0":
                    ffn0(n)
            od = out.rearrange("(t p) d -> p t d", p=P)
            last = len(SUBLAYERS) - 1
            for g in range(NSEQ):
                sp.wait_ge(x_updated, N0(last) + g + 1)
                sp.dma_start(od[:, g * TPS:(g + 1) * TPS, :], x[:, g * TPS:(g + 1) * TPS, :]).then_inc(x_stored, 16)
            sp.wait_ge(x_stored, 16 * NSEQ)

        @block.gpsimd
        def _(pool):
            nc.gpsimd.memset(neghalf[:], -0.5).then_inc(rstd_step, 1)
            nc.gpsimd.memset(eps[:], EPS).then_inc(rstd_step, 1)
            pool.wait_ge(rstd_step, 2)

            def rstd_of(m):
                pool.wait_ge(mv_ready, m + 1)
                nc.gpsimd.tensor_tensor(rstd[:], mv[:, :, 1], eps[:], ALU.add).then_inc(rstd_step, 1)
                pool.wait_ge(rstd_step, m + 3)
                nc.gpsimd.tensor_tensor(rstd[:], rstd[:], neghalf[:, 0:TPS], ALU.pow).then_inc(rstd_ready, 1)

            def work_left(n):
                if n:
                    pool.wait_ge(x_updated, N0(n))
                else:
                    pool.wait_ge(pt_ready, 1)

            def gather(n, q, u, buffers):
                s, G0 = S[n], earlier(n) * NSEQ
                pool.wait_ge(s["rows_step"], q + 1 + G0)
                if not isinstance(q, int) or q >= len(buffers):
                    pool.wait_ge(s["combined"], q + 1 - len(buffers) + G0)
                for r in range(TOPK):
                    if r:
                        pool.wait_ge(s["gathered0"], 16 * TPS * (q + 1 + G0))
                    pool.sem_inc(pool_stood, 1)
                    for t in range(TPS):
                        nc.gpsimd.indirect_dma_start(
                            buffers[u % len(buffers)][:, t, :], None, expert_y[:, :],
                            bass.IndirectOffsetOnAxis(gather_rows[:, u, r, t:t + 1], 0),
                            compute_op=ALU.add if r else ALU.bypass).then_inc(s[f"gathered{r}"], 16)
                pool.wait_ge(s["gathered1"], 16 * TPS * (q + 1 + G0))

            def gathers(n):
                for v in range(4):
                    pool.wait_ge(S[n - 1][f"tile_out{v}"], 4 * TILES * (1 + earlier(n - 1)))
                gather(n - 1, 0, 0, yg_buffers(n))
                rstd_of(N0(n))
                gather(n - 1, 1, 1, yg_buffers(n))

            def more_gathers(n, g, u):
                if after_ffn0(n) and not (isinstance(g, int) and g >= NSEQ - 2):
                    gather(n - 1, g + 2, u, yg_buffers(n))

            def l1ffn(n):
                s = S[n]

                def body(g, u):
                    pool.wait_ge(xn_ready, g + N0(n) + 1)
                    for t in range(TPS):
                        ins = nc.gpsimd.tensor_tensor(x[:, ds(g * TPS + t, 1), :], x[:, ds(g * TPS + t, 1), :],
                                                      b2_row[:, None, :], ALU.add)
                    ins.then_inc(s["bias_added"], 1)
                    rstd_of(g + N0(n) + 1)
                    more_gathers(n, g, u)
                each_sequence(pool, body, after_ffn0(n))

            def ffn0(n):
                s, m = S[n], ffn0_space()
                G0, T0 = earlier(n) * NSEQ, earlier(n) * TILES
                work_left(n)
                nc.gpsimd.memset(m.zeros, 0.0).then_inc(s["zeros_set"], 1)

                def body(g, u):
                    if not is_last(g):
                        rstd_of(g + N0(n) + 1)
                    pool.wait_ge(xn_ready, g + N0(n) + 1)
                    pool.wait_ge(s["rows_ready"], (g + G0) + 2)
                    for r in range(TOPK):
                        if r:
                            pool.wait_ge(s["scattered0"], 16 * TPS * ((g + G0) + 1))
                        nc.gpsimd.tensor_tensor(xn[:, :, D], m.gate[:, r], const("ones")[:, 0:TPS], ALU.mult).then_inc(s["gate_set"], 1)
                        pool.wait_ge(s["gate_set"], (g + G0) * TOPK + r + 1)
                        pool.sem_inc(pool_stood, 1)
                        for t in range(TPS):
                            nc.gpsimd.indirect_dma_start(
                                expert_x[:, :], bass.IndirectOffsetOnAxis(m.scatter_rows[:, r, t:t + 1], 0),
                                xn[:, t, :], None).then_inc(s[f"scattered{r}"], 16)
                    pool.wait_ge(s["scattered1"], 16 * TPS * ((g + G0) + 1))
                each_sequence(pool, body, True)

            def gla(n):
                s, m = S[n], gla_space()
                work_left(n)
                nc.gpsimd.memset(m.qz, 0.0).then_inc(s["q_ready"], 2)

                def body(g, u):
                    rstd_of(g + N0(n) + 1)
                    more_gathers(n, g, u)
                    pool.wait_ge(s["ss_ready"], g * TPS + TPS)
                    nc.gpsimd.tensor_tensor(m.orstd, m.ss, eps[:, None, :].broadcast_to([P, TPS, H]), ALU.add).then_inc(s["orstd_step"], 1)
                    pool.wait_ge(s["orstd_step"], g + 1)
                    nc.gpsimd.tensor_tensor(m.orstd, m.orstd, neghalf.rearrange("p (a b) -> p a b", b=H), ALU.pow).then_inc(s["orstd_ready"], 1)
                each_sequence(pool, body, after_ffn0(n))

            def win(n):
                s, m = S[n], win_space()
                work_left(n)
                for a in (m.vz, m.c, m.k[:, :, 0:PAD]):
                    nc.gpsimd.memset(a, 0.0)
                nc.gpsimd.memset(m.k[:, :, PAD + SEQ:], 0.0).then_inc(s["zeroed"], 1)
                heads = const("heads")

                def body(g, u):
                    pool.wait_ge(xn_ready, g + N0(n) + 1)
                    for t in range(TPS):
                        ins = nc.gpsimd.tensor_tensor(x[:, ds(g * TPS + t, 1), :], x[:, ds(g * TPS + t, 1), :],
                                                      bo_row[:, None, :], ALU.add)
                    ins.then_inc(s["bias_added"], 1)
                    pool.wait_ge(s["qk_copied"], g * 2 * KT + KT)
                    for t in range(TPS):
                        pool.wait_ge(s["sc_ready"], g * TPS + t + 1)
                        for f in range(KT):
                            ins = nc.gpsimd.tensor_tensor(
                                m.qz[:, t % 2 * KT + f],
                                m.q[:, f, t * P:(t + 1) * P].rearrange("p (b q) -> p b q", q=QB)[:, :, None].broadcast_to([P, BPT, 8, QB]),
                                heads[:, None, :, None].broadcast_to([P, BPT, 8, QB]), ALU.mult)
                        ins.then_inc(s["qz_ready"], 1)
                    rstd_of(g + N0(n) + 1)
                each_sequence(pool, body)

            pool.wait_ge(small_loaded, 48)
            nc.gpsimd.tensor_scalar(b2_row, b2_row, 0.5, None, ALU.mult).then_inc(ready0, 1)
            nc.gpsimd.tensor_scalar(rms_col, rms_col, WS, None, ALU.mult).then_inc(ready0, 1)
            pool.wait_ge(ready0, 2)
            for w in (xt_hi, xt_lo):
                nc.gpsimd.memset(w[:, :, :, 0:PAD], 0.0)
                nc.gpsimd.memset(w[:, :, :, PAD + SEQ:], 0.0).then_inc(ready0, 1)
            rstd_of(0)
            for n, kind in enumerate(SUBLAYERS):
                if after_ffn0(n):
                    gathers(n)
                {"ffn0": ffn0, "l1ffn": l1ffn, "gla": gla, "win": win}[kind](n)

        @block.scalar
        def _(act):
            def halves_hi():
                for m, (name, dst, c, n, r) in enumerate(chunks):
                    load_done(act, m)
                    nc.scalar.activation(dst[0][0:r, c:c + n], stage[0:r, m % NST, 0:n], ACT.Copy,
                                         scale=rms_col if name == "g_o" else WS).then_inc(w_hi_done, 1)

            def xt_hi_of(m, u):
                act.wait_ge(pt_ready, m + 1)
                nc.scalar.activation(xt_hi[:, u, :, TOK], ps[:, 0:KT, :], ACT.Copy).then_inc(xt_hi_ready, 1)

            def ffn0(n):
                s, m = S[n], ffn0_space()
                G0, T0 = earlier(n) * NSEQ, earlier(n) * TILES

                def body(g, u):
                    def hi(k):
                        act.wait_ge(s["prod_ready"], (g + G0) * SU + k + 3)
                        if k == 0:
                            act.wait_ge(s["y_ready"], (g + G0) * 2 + 2)
                        nc.scalar.activation(m.h_hi[:, k, :], m.prod[:, k % PRODS, :], ACT.Copy).then_inc(s["h_hi_ready"], 1)

                    act.wait_ge(s["router_ready"], (g + G0) + 1)
                    act.wait_ge(s["rows_ready"], (g + G0) + 1)
                    nc.scalar.activation(m.scores.rearrange("p a b -> p (a b)"), ps[:, 0, 0:TPS * NE], ACT.Sigmoid,
                                         scale=1 / WS).then_inc(s["scores_ready"], 1)
                    for k in range(SU):
                        b = 2 + 2 * (k % 2)
                        act.wait_ge(s["up_ready"], (g + G0) * SU + k + 1)
                        act.wait_ge(s["prod_ready"], (g + G0) * SU + k + 1)
                        nc.scalar.activation(m.silu[:, k % 2, :], ps[:, b, :], ACT.Silu, scale=1 / WS).then_inc(s["silu_ready"], 1)
                        if k >= 1:
                            hi(k - 1)
                    hi(SU - 1)
                    if not is_last(g):
                        xt_hi_of(g + N0(n) + 1, 1 - u)
                each_sequence(act, body, True)

                def step(i, b, u, has):
                    if has(0):
                        act.wait_ge(s["tile_turned"], i + 1 + T0)
                        if not isinstance(i, int) or i >= 2:
                            act.wait_ge(s["tile_up"], i - 1 + T0)
                        nc.scalar.activation(m.t_hi[:, u % 2], ps[:, u % 2, 0:KT * P].rearrange("p (k t) -> p k t", k=KT),
                                             ACT.Copy).then_inc(s["tile_hi"], 1)
                    if has(1):
                        j, v = i - 1, (u - 1) % 2
                        act.wait_ge(s["tile_up"], j + 1 + T0)
                        if not isinstance(j, int) or j >= 2:
                            act.wait_ge(s["tile_prod"], j - 1 + T0)
                        nc.scalar.activation(m.t_silu[:, v], ps[:, 2 + v, 0:HE], ACT.Silu, scale=1 / WS).then_inc(s["tile_silu"], 1)
                    if has(2):
                        j, v = i - 2, u % 2
                        act.wait_ge(s["th_turned"], j + 1 + T0)
                        if not isinstance(j, int) or j >= 2:
                            act.wait_ge(s["tile_down"], j - 1 + T0)
                        nc.scalar.activation(m.th_hi[:, v], ps[:, 4 + v, 0:EU * P].rearrange("p (k t) -> p k t", k=EU),
                                             ACT.Copy).then_inc(s["th_hi"], 1)
                each_tile(act, step, 2)
                xt_hi_of(N0(n + 1), 0)

            def l1ffn(n):
                s = S[n]
                h_hi, h_lo, relu = l1ffn_space()

                def step(g, u, up, down):
                    def hi(k):
                        act.wait_ge(s["relu_ready"], g * FU + k + 1)
                        if k == 0:
                            act.wait_ge(s["y_ready"], g * 2 + 2)
                        nc.scalar.activation(h_hi[:, u, k, :], relu[:, k % RELUS, :], ACT.Copy).then_inc(s["h_hi_ready"], 1)

                    if not up:
                        return
                    for k in range(FU):
                        act.wait_ge(s["up_ready"], g * FU + k + 1)
                        act.wait_ge(s["h_lo_ready"], g * FU + k + 1)
                        nc.scalar.activation(relu[:, k % RELUS, :], ps[:, 2 + k % 4, :], ACT.Relu,
                                             bias=b1_col[:, k:k + 1]).then_inc(s["relu_ready"], 1)
                        if k >= 1:
                            hi(k - 1)
                    hi(FU - 1)
                    xt_hi_of(g + N0(n) + 1, 1 - u)
                skewed(act, step)

            def gla(n):
                s, m = S[n], gla_space()

                def body(g, u):
                    act.wait_ge(s["t_ready"], g + 1)
                    nc.scalar.activation(m.t_hi[0:LOW], ps[0:LOW, 2, :], ACT.Copy, scale=1 / WS).then_inc(s["t_hi"], 1)
                    for j in range(2 * GPAIR):
                        act.wait_ge(s["qk_ready"], g * 2 * GPAIR + j + 1)
                        dst, p = (m.q, j) if j < GPAIR else (m.k, j - GPAIR)
                        nc.scalar.activation(dst[:, p], ps[:, 3 + j, :], ACT.Copy,
                                             scale=(DK ** -0.5 if j < GPAIR else 1.0) / WS).then_inc(s["qk_copied"], 1)
                    act.wait_ge(s["lb_ready"], g * 2 + 2)
                    nc.scalar.activation(m.soft, m.lb, ACT.Abs).then_inc(s["soft_step"], 1)
                    act.wait_ge(s["soft_step"], g * 3 + 1)
                    nc.scalar.activation(m.soft, m.soft, ACT.Exp, scale=-1.0).then_inc(s["soft_step"], 1)
                    act.wait_ge(s["soft_step"], g * 3 + 2)
                    nc.scalar.activation(m.soft, m.soft, ACT.Ln, bias=1.0).then_inc(s["soft_step"], 1)
                    for c in range(TPS):
                        act.wait_ge(s["v_ready"], g * TPS + c + 1)
                        nc.scalar.activation(m.v[:, c], ps[:, GB[c], :], ACT.Copy, scale=1 / WS).then_inc(s["v_copied"], 1)
                    act.wait_ge(s["cum_ready"], g + 1)
                    nc.scalar.activation(m.up, ps[:, 3:5, :], ACT.Exp).then_inc(s["exps_ready"], 1)
                    nc.scalar.activation(m.down, ps[:, 3:5, :], ACT.Exp, scale=-1.0).then_inc(s["exps_ready"], 1)
                    nc.scalar.activation(m.soft.rearrange("p (a b) c -> p a (b c)", a=2), ps[:, 5:7, :], ACT.Exp).then_inc(s["exps_ready"], 1)
                    nc.scalar.activation(m.ends.rearrange("p a b c -> p (a b c)"), ps[:, 0, 0:GPAIR * TPS * 2], ACT.Exp).then_inc(s["exps_ready"], 1)
                    for c in range(TPS):
                        act.wait_ge(s["gate_ready"], g * TPS + c + 1)
                        act.wait_ge(s["st_ready"], g * TPS + TPS)
                        nc.scalar.activation(m.gate[:, c], ps[:, GB[c], :], ACT.Silu, scale=1 / WS).then_inc(s["gate_done"], 1)
                    for c in range(TPS):
                        act.wait_ge(s["o_ready"], g * TPS + c + 1)
                        if c >= 2:
                            act.wait_ge(s["ss_ready"], g * TPS + c - 1)
                        nc.scalar.activation(m.squares[:, c % 2], ps[:, GB[c], :], ACT.Square,
                                             scale=DV ** -0.5).then_inc(s["sq_ready"], 1)
                    for c in range(TPS):
                        act.wait_ge(s["ogt_ready"], g * TPS + c + 1)
                        nc.scalar.activation(m.o_hi[:, c].rearrange("p h t -> p (h t)"), ps[:, SB[c], :], ACT.Copy).then_inc(s["ogt_hi"], 1)
                    xt_hi_of(g + N0(n) + 1, 1 - u)
                each_sequence(act, body)

            def win(n):
                s, m = S[n], win_space()
                act.wait_ge(s["zeroed"], 1)

                def body(g, u):
                    for j in range(2 * KT):
                        act.wait_ge(s["qk_ready"], g * 2 * KT + j + 1)
                        f = j % KT
                        dst, b = (m.q[:, f], bq_col) if j < KT else (m.k[:, f, TOK], bk_col)
                        nc.scalar.activation(dst, ps[:, 2 + j, :], ACT.Identity, bias=b[:, f:f + 1],
                                             scale=1 / WS).then_inc(s["qk_copied"], 1)
                    for t in range(TPS):
                        i = t % 2
                        act.wait_ge(s["sub_ready"], g * TPS + t + 1)
                        nc.scalar.activation(m.p[:, i], m.p[:, i], ACT.Exp, scale=AD ** -0.5).then_inc(s["exp_ready"], 1)
                        act.wait_ge(s["pt_ready"], g * TPS + t + 1)
                        for b in range(2):
                            ins = nc.scalar.activation(m.pt[:, i, 4 * b:4 * b + 4].rearrange("p a b -> p (a b)"),
                                                       ps[:, 4 + b, :], ACT.Copy)
                        ins.then_inc(s["pt_copied"], 1)
                        if t >= 1:
                            ct_hi(s, m, g, t - 1)
                    ct_hi(s, m, g, TPS - 1)
                    xt_hi_of(g + N0(n) + 1, 1 - u)

                def ct_hi(s, m, g, t):
                    act.wait_ge(s["ct_ready"], g * TPS + t + 1)
                    nc.scalar.activation(m.c_hi[:, :, t * P:(t + 1) * P], ps[:, 1, 0:KT * P].rearrange("p (f q) -> p f q", f=KT),
                                         ACT.Copy).then_inc(s["ct_hi"], 1)
                each_sequence(act, body)

            act.wait_ge(small_loaded, 48)
            act.wait_ge(ready0, 4)
            nc.scalar.activation(window16[:], const("window")[:, None, :].broadcast_to([P, 8, KB]), ACT.Copy)
            nc.scalar.activation(ident16[:], ident, ACT.Copy)
            halves_hi()
            xt_hi_of(0, 0)
            for n, kind in enumerate(SUBLAYERS):
                {"ffn0": ffn0, "l1ffn": l1ffn, "gla": gla, "win": win}[kind](n)

        @block.vector
        def _(dve):
            def halves_lo():
                for m, (name, dst, c, n, r) in enumerate(chunks):
                    dve.wait_ge(w_hi_done, m + 1)
                    nc.vector.scalar_tensor_tensor(out=dst[1][0:r, c:c + n], in0=stage[0:r, m % NST, 0:n],
                                                   scalar=rms_col if name == "g_o" else WS,
                                                   in1=dst[0][0:r, c:c + n], op0=ALU.mult,
                                                   op1=ALU.subtract).then_inc(w_lo_done, 1)

            def ternary():
                step = 0
                for k, (name, dst) in enumerate(TERN):
                    load_done(dve, NCH + k)
                    nc.vector.tensor_reduce(tsum[:, k:k + 1], stage[:, (NCH + k) % NST, :], AX.X, ALU.add,
                                            apply_absolute_value=True).then_inc(tern, 1)
                for k, (name, dst) in enumerate(TERN):
                    dve.wait_ge(tern_sum, 1)
                    for sign, c in ((1, 0), (-1, 1)):
                        nc.vector.tensor_scalar(thr[:, k, c:c + 1], ps[:, 7, k:k + 1], sign * 0.5 / (CH * P), sign * 0.5 * EPS,
                                                ALU.mult, ALU.add).then_inc(tern, 1)
                dve.wait_ge(tern, 6)
                for k, (name, dst) in enumerate(TERN):
                    w = stage[:, (NCH + k) % NST, :]
                    nc.vector.tensor_scalar(dst[:], w, thr[:, k, 1:2], None, ALU.is_lt).then_inc(tern, 1)
                    dve.wait_ge(tern, 7 + 2 * k)
                    nc.vector.scalar_tensor_tensor(out=dst[:], in0=w, scalar=thr[:, k, 0:1], in1=dst[:],
                                                   op0=ALU.is_gt, op1=ALU.subtract).then_inc(tern, 1)
                dve.wait_ge(tern, 10)

            def ln_stats(m, at):
                for t in range(TPS):
                    ins = nc.vector.bn_stats(stats[:, t, :], x[:, ds(at + t, 1), :].rearrange("p a d -> p (a d)"))
                ins.then_inc(ln_step, 1)
                dve.wait_ge(ln_step, m + 1)
                dve.sem_inc(stood, 1)
                for t in range(TPS):
                    ins = nc.vector.bn_aggr(mv[:, t, :], stats[:, t, :])
                ins.then_inc(mv_ready, 1)

            def ln_scale(m, at, first=False):
                dve.wait_ge(mv_ready, m + 1)
                dve.wait_ge(rstd_ready, m + 1)
                if not first:
                    dve.wait_ge(pt_ready, m)
                for t in range(TPS):
                    ins = nc.vector.tensor_scalar(xn[:, t, 0:D], x[:, ds(at + t, 1), :].rearrange("p a d -> p (a d)"),
                                                  mv[:, t, 0:1], rstd[:, t:t + 1], ALU.subtract, ALU.mult)
                ins.then_inc(xn_ready, 1)

            def xt_lo_of(m, u):
                dve.wait_ge(xt_hi_ready, m + 1)
                nc.vector.tensor_tensor(xt_lo[:, u, :, TOK], ps[:, 0:KT, :], xt_hi[:, u, :, TOK], ALU.subtract).then_inc(xt_lo_ready, 1)

            def next_at(g):
                return ((g + 1) % NSEQ) * TPS

            def integer_rows(n, q, u):
                nc.vector.tensor_scalar(gather_rows[:, u], expert_rows[:, :, ds(q * TPS, TPS)], 0.0, None,
                                        ALU.add).then_inc(S[n]["rows_step"], 1)

            def combine(n, q, u):
                s, G0 = S[n], earlier(n) * NSEQ
                dve.wait_ge(s["gathered0"], 16 * TPS * (q + 1 + G0))
                dve.wait_ge(s["gathered1"], 16 * TPS * (q + 1 + G0))
                integer_rows(n, q + 2, u)
                b = yg_buffers(n + 1)
                xs = x[:, ds(q * TPS, TPS), :]
                nc.vector.tensor_tensor(xs, xs, b[u % len(b)], ALU.add).then_inc(s["combined"], 1)
                dve.wait_ge(s["combined"], q + 1 + G0)
                dve.sem_inc(stood, 1)

            def next_stats(n, g, u):
                if after_ffn0(n) and not is_last(g):
                    combine(n - 1, g + 1, 1 - u)
                ln_stats(g + N0(n) + 1, next_at(g))

            def ffn0(n):
                s, m = S[n], ffn0_space()
                G0, T0 = earlier(n) * NSEQ, earlier(n) * TILES
                tri = const("tri").rearrange("p (e j) -> p e j", e=NE)
                iota = const("iota")
                GSTEPS, TAB_STEPS = 13, 20
                if not earlier(n):
                    dve.sem_inc(s["h_lo_ready"], PRODS)
                if not earlier(n):
                    dve.sem_inc(s["prod_ready"], 2)
                if not earlier(n):
                    dve.sem_inc(s["y_taken"], 2)
                if not earlier(n):
                    dve.sem_inc(s["rows_ready"], 1)
                nc.vector.tensor_scalar(m.base, const("regions"), -1.0, None, ALU.add).then_inc(s["base_set"], 1)
                dve.wait_ge(s["base_set"], 1 + earlier(n))

                def body(g, u):
                    step = [0]

                    def link(ins):
                        step[0] += 1
                        ins.then_inc(s["gate_step"], 1)
                        dve.wait_ge(s["gate_step"], (g + G0) * GSTEPS + step[0])

                    def choose():
                        dve.wait_ge(s["scores_ready"], (g + G0) + 1)
                        link(nc.vector.tensor_tensor(m.biased, m.scores, ebias_row[:, None, :].broadcast_to([P, TPS, NE]), ALU.add))
                        other = m.biased[:, :, None, :].broadcast_to([P, TPS, NE, NE])
                        own = m.biased[:, :, :, None].broadcast_to([P, TPS, NE, NE])
                        nc.vector.tensor_tensor(m.beats, other, own, ALU.is_gt)
                        link(nc.vector.tensor_tensor(m.ties, other, own, ALU.is_equal))
                        link(nc.vector.tensor_tensor(m.ties, m.ties, tri[:, None].broadcast_to([P, TPS, NE, NE]), ALU.mult))
                        link(nc.vector.tensor_tensor(m.beats, m.beats, m.ties, ALU.add))
                        link(nc.vector.tensor_reduce(m.rank, m.beats, AX.X, ALU.add))
                        nc.vector.tensor_scalar(m.mask, m.rank, float(TOPK), None, ALU.is_lt).then_inc(s["mask_ready"], 1)
                        for r in range(TOPK):
                            ins = nc.vector.tensor_scalar(m.onehot[:, r], m.rank.rearrange("p t e -> p (t e)"), float(r), None,
                                                          ALU.is_equal)
                        link(ins)
                        link(nc.vector.scalar_tensor_tensor(
                            out=m.picked, in0=m.onehot, scalar=HS / WS,
                            in1=m.scores.rearrange("p t e -> p (t e)")[:, None, :].broadcast_to([P, TOPK, TPS * NE]),
                            op0=ALU.mult, op1=ALU.mult))
                        link(nc.vector.tensor_reduce(m.gate.rearrange("p r t -> p (r t)"),
                                                     m.picked.rearrange("p r (t e) -> p (r t) e", e=NE), AX.X, ALU.add))

                    def place():
                        dve.wait_ge(s["pos_ready"], (g + G0) + 1)
                        link(nc.vector.tensor_tensor(m.row, ps[:, 0, 64:64 + TPS * NE].rearrange("p (t e) -> p t e", e=NE),
                                                     m.base[:, None, :].broadcast_to([P, TPS, NE]), ALU.add))
                        link(nc.vector.tensor_tensor(m.base, m.base, ps[:, 0, 96:96 + NE], ALU.add))
                        link(nc.vector.tensor_tensor(
                            m.picked, m.onehot, m.row.rearrange("p t e -> p (t e)")[:, None, :].broadcast_to([P, TOPK, TPS * NE]), ALU.mult))
                        link(nc.vector.tensor_reduce(m.rank.rearrange("p t e -> p (t e)")[:, 0:TOPK * TPS],
                                                     m.picked.rearrange("p r (t e) -> p (r t) e", e=NE), AX.X, ALU.add))
                        rows_ = m.rank.rearrange("p t e -> p (t e)")[:, 0:TOPK * TPS].rearrange("p (r t) -> p r t", r=TOPK)
                        nc.vector.tensor_scalar(expert_rows[:, :, ds(g * TPS, TPS)], rows_, 0.0, None, ALU.add)
                        link(nc.vector.tensor_scalar(m.scatter_rows, rows_, 0.0, None, ALU.add))
                        dve.sem_inc(s["rows_ready"], 1)

                    def lo(k):
                        dve.wait_ge(s["h_hi_ready"], (g + G0) * SU + k + 1)
                        nc.vector.tensor_tensor(m.h_lo[:, k, :], m.prod[:, k % PRODS, :], m.h_hi[:, k, :],
                                                ALU.subtract).then_inc(s["h_lo_ready"], 1)

                    def take(half):
                        dve.wait_ge(s["y_ready"], (g + G0) * 2 + half + 3)
                        xs = x[:, ds(g * TPS + 2 * half, 2), :]
                        nc.vector.scalar_tensor_tensor(out=xs, in0=ps[:, 6 + half, :].rearrange("p (t d) -> p t d", t=2),
                                                       scalar=0.5 / (WS * HS), in1=xs, op0=ALU.mult,
                                                       op1=ALU.add).then_inc(s["y_taken"], 1)

                    choose()
                    for k in range(SU):
                        b = 3 + 2 * (k % 2)
                        dve.wait_ge(s["silu_ready"], (g + G0) * SU + k + 1)
                        dve.wait_ge(s["h_lo_ready"], (g + G0) * SU + k + 1)
                        nc.vector.scalar_tensor_tensor(out=m.prod[:, k % PRODS, :], in0=ps[:, b, :], scalar=HS / WS,
                                                       in1=m.silu[:, k % 2, :], op0=ALU.mult, op1=ALU.mult).then_inc(s["prod_ready"], 1)
                        if k >= 1:
                            lo(k - 1)
                        if k == 1:
                            place()
                        if k == 2 and not is_last(g):
                            ln_stats(g + N0(n) + 1, next_at(g))
                        if k == 2 and is_last(g):
                            tabulate()
                    lo(SU - 1)
                    if not is_last(g):
                        for r in range(TOPK):
                            dve.wait_ge(s[f"scattered{r}"], 16 * TPS * ((g + G0) + 1))
                        ln_scale(g + N0(n) + 1, next_at(g))
                    take(0)
                    if not is_last(g):
                        xt_lo_of(g + N0(n) + 1, 1 - u)
                    take(1)
                    dve.wait_ge(s["y_taken"], (g + G0) * 2 + 4)

                def tabulate():
                    done = [0]

                    def link(ins):
                        done[0] += 1
                        ins.then_inc(s["tab_step"], 1)
                        dve.wait_ge(s["tab_step"], done[0] + earlier(n) * TAB_STEPS)

                    link(nc.vector.tensor_tensor(m.count, m.base, const("regions"), ALU.subtract))
                    nc.vector.tensor_scalar(m.table[:, 2 * TILES:], m.base, 1.0, None, ALU.add).then_inc(s["tab_ready"], 1)
                    link(nc.vector.tensor_scalar(m.count, m.count, 1.0, 1.0 / P, ALU.add, ALU.mult))
                    nt = NSEQ * TPS
                    link(nc.vector.tensor_tensor(m.more, m.count[:, :, None].broadcast_to([P, NE, nt]),
                                                 iota[:, None, 0:nt].broadcast_to([P, NE, nt]), ALU.is_gt))
                    link(nc.vector.tensor_reduce(m.tiles, m.more, AX.X, ALU.add))
                    link(nc.vector.tensor_tensor(m.before, tri, m.tiles[:, None, :].broadcast_to([P, NE, NE]), ALU.mult))
                    link(nc.vector.tensor_reduce(m.end, m.before, AX.X, ALU.add))
                    nc.vector.tensor_scalar(m.jump, m.tiles, -float(P), float(REGION), ALU.mult, ALU.add)
                    link(nc.vector.tensor_tensor(m.end, m.end, m.tiles, ALU.add))
                    link(nc.vector.tensor_tensor(m.over, iota[:, :, None].broadcast_to([P, TILES, NE]),
                                                 m.end[:, None, :].broadcast_to([P, TILES, NE]), ALU.is_ge))
                    link(nc.vector.tensor_reduce(m.sums[:, 0], m.over, AX.X, ALU.add))
                    link(nc.vector.tensor_tensor(m.over, m.over, m.jump[:, None, :].broadcast_to([P, TILES, NE]), ALU.mult))
                    link(nc.vector.tensor_reduce(m.sums[:, 1], m.over, AX.X, ALU.add))
                    nc.vector.tensor_scalar(m.table[:, TILES:2 * TILES], m.sums[:, 0], NE - 1.0, 2.0 * HE, ALU.min,
                                            ALU.mult).then_inc(s["tab_ready"], 1)
                    dve.wait_ge(s["tab_ready"], 2 + 3 * earlier(n))
                    link(nc.vector.tensor_scalar(m.count, const("regions"), float(REGION), None, ALU.add))
                    nc.vector.scalar_tensor_tensor(out=m.table[:, 0:TILES], in0=iota, scalar=float(P), in1=m.sums[:, 1],
                                                   op0=ALU.mult, op1=ALU.add).then_inc(s["tab_ready"], 1)
                    nr = NSEQ * TPS
                    for r in range(TOPK):
                        beyond = m.over[:, 0:nr]
                        link(nc.vector.tensor_tensor(beyond, expert_rows[:, r, 0:nr, None].broadcast_to([P, nr, NE]),
                                                     m.count[:, None, :].broadcast_to([P, nr, NE]), ALU.is_ge))
                        link(nc.vector.tensor_tensor(beyond, beyond, m.jump[:, None, :].broadcast_to([P, nr, NE]), ALU.mult))
                        link(nc.vector.tensor_reduce(m.sums[:, 0, 0:nr], beyond, AX.X, ALU.add))
                        link(nc.vector.tensor_tensor(expert_rows[:, r, 0:nr], expert_rows[:, r, 0:nr], m.sums[:, 0, 0:nr], ALU.subtract))
                    assert done[0] == TAB_STEPS

                each_sequence(dve, body, True)
                dve.wait_ge(s["gate_step"], (NSEQ + G0) * GSTEPS)
                for q in range(2):
                    integer_rows(n, q, q)

                def step(i, b, u, has):
                    if has(0):
                        dve.wait_ge(s["tile_hi"], i + 1 + T0)
                        nc.vector.tensor_tensor(m.t_lo[:, u % 2], ps[:, u % 2, 0:KT * P].rearrange("p (k t) -> p k t", k=KT),
                                                m.t_hi[:, u % 2], ALU.subtract).then_inc(s["tile_lo"], 1)
                    if has(1):
                        j, v = i - 1, (u - 1) % 2
                        dve.wait_ge(s["tile_silu"], j + 1 + T0)
                        if not isinstance(j, int) or j >= 2:
                            dve.wait_ge(s["th_turned"], j - 1 + T0)
                        nc.vector.scalar_tensor_tensor(out=m.t_prod[:, v], in0=ps[:, 2 + v, HE:2 * HE],
                                                       scalar=m.tile_x[:, (u - 1) % 4, D:D + 1], in1=m.t_silu[:, v],
                                                       op0=ALU.mult, op1=ALU.mult).then_inc(s["tile_prod"], 1)
                    if has(2):
                        j, v = i - 2, u % 2
                        dve.wait_ge(s["th_hi"], j + 1 + T0)
                        nc.vector.tensor_tensor(m.th_lo[:, v], ps[:, 4 + v, 0:EU * P].rearrange("p (k t) -> p k t", k=EU),
                                                m.th_hi[:, v], ALU.subtract).then_inc(s["th_lo"], 1)
                    if has(3):
                        j, v = i - 3, (u - 3) % 4
                        dve.wait_ge(s["tile_down"], j + 1 + T0)
                        if not isinstance(j, int) or j >= 4:
                            dve.wait_ge(s[f"tile_out{v}"], 16 * (b - (1 if u < 3 else 0)) + 4 * T0)
                        nc.vector.tensor_scalar(m.t_y[:, v], ps[:, 6 + v % 2, 0:D], 0.5 / (WS * HS), None,
                                                ALU.mult).then_inc(s["tile_y"], 1)
                each_tile(dve, step, 3)
                dve.wait_ge(s["tile_y"], TILES + T0)
                dve.sem_inc(x_updated, NSEQ)
                combine(n, 0, 0)
                ln_stats(N0(n + 1), 0)
                ln_scale(N0(n + 1), 0)
                xt_lo_of(N0(n + 1), 0)

            def l1ffn(n):
                s = S[n]
                h_hi, h_lo, relu = l1ffn_space()
                dve.sem_inc(s["h_lo_ready"], RELUS)
                dve.sem_inc(s["y_taken"], 2)

                def step(g, u, up, down):
                    if up:
                        up_part(g, u)
                    if down:
                        down_part(g - 1, u, up)
                    else:
                        xt_lo_of(g + N0(n) + 1, 1 - u)

                def up_part(g, u):
                    for k in range(FU):
                        dve.wait_ge(s["h_hi_ready"], g * FU + k + 1)
                        nc.vector.tensor_tensor(h_lo[:, u, k, :], relu[:, k % RELUS, :], h_hi[:, u, k, :],
                                                ALU.subtract).then_inc(s["h_lo_ready"], 1)
                        if k == 0:
                            next_stats(n, g, u)
                        if k == 4:
                            ln_scale(g + N0(n) + 1, next_at(g))

                def down_part(g, u, next_one):
                    for half in range(2):
                        if half and next_one:
                            xt_lo_of(g + N0(n) + 2, 1 - u)
                        dve.wait_ge(s["y_ready"], g * 2 + half + 5)
                        dve.wait_ge(s["bias_added"], g + 1)
                        xs = x[:, ds(g * TPS + 2 * half, 2), :]
                        nc.vector.scalar_tensor_tensor(out=xs, in0=ps[:, 6 + half, :].rearrange("p (t d) -> p t d", t=2),
                                                       scalar=0.5, in1=xs, op0=ALU.mult, op1=ALU.add).then_inc(s["y_taken"], 1)
                    dve.wait_ge(s["y_taken"], g * 2 + 4)
                    dve.sem_inc(x_updated, 1)
                skewed(dve, step)

            def gla(n):
                s, m = S[n], gla_space()
                dve.sem_inc(s["y_taken"], 2)

                def body(g, u):
                    step = [0]

                    def link(ins):
                        step[0] += 1
                        ins.then_inc(s["s_step"], 1)
                        dve.wait_ge(s["s_step"], g * (1 + 2 * TPS) + step[0])

                    dve.wait_ge(s["t_hi"], g + 1)
                    nc.vector.scalar_tensor_tensor(out=m.t_lo[0:LOW], in0=ps[0:LOW, 2, :], scalar=1 / WS, in1=m.t_hi[0:LOW],
                                                   op0=ALU.mult, op1=ALU.subtract).then_inc(s["t_lo"], 1)
                    for j, b in enumerate((2, 7)):
                        dve.wait_ge(s["logits_ready"], g * 2 + j + 1)
                        nc.vector.scalar_tensor_tensor(
                            out=m.lb[:, 2 * j:2 * j + 2], in0=ps[:, b, :].rearrange("p (t d) -> p t d", t=2), scalar=1 / WS,
                            in1=bgk_row[:, None, :].broadcast_to([P, 2, H * DK]), op0=ALU.mult, op1=ALU.add).then_inc(s["lb_ready"], 1)
                    next_stats(n, g, u)
                    dve.wait_ge(s["soft_step"], g * 3 + 3)
                    nc.vector.scalar_tensor_tensor(out=m.lb, in0=m.lb, scalar=0.0, in1=m.soft, op0=ALU.min,
                                                   op1=ALU.subtract).then_inc(s["g_ready"], 1)
                    ln_scale(g + N0(n) + 1, next_at(g))
                    dve.wait_ge(s["exps_ready"], g * 4 + 1)
                    for h in range(2):
                        sl = slice(h * DK, (h + 1) * DK)
                        nc.vector.tensor_tensor(m.qz[sl, :, h], m.q[sl], m.up[sl], ALU.mult).then_inc(s["q_ready"], 1)
                    dve.wait_ge(s["exps_ready"], g * 4 + 2)
                    nc.vector.tensor_tensor(m.k, m.k, m.down, ALU.mult).then_inc(s["k_ready"], 1)
                    dve.wait_ge(s["exps_ready"], g * 4 + 4)
                    for j, b in enumerate((2, 7)):
                        dve.wait_ge(s["kt_ready"], g * 2 + j + 1)
                        sl = m.soft[:, 2 * j:2 * j + 2]
                        nc.vector.scalar_tensor_tensor(out=sl, in0=ps[:, b, :].rearrange("p (t d) -> p t d", t=2), scalar=1 / WS,
                                                       in1=sl, op0=ALU.mult, op1=ALU.mult).then_inc(s["kdec_ready"], 1)
                    dve.wait_ge(s["q_ready"], g * 2 + 4)
                    link(nc.vector.memset(m.s, 0.0))
                    for c in range(TPS):
                        for p in range(GPAIR):
                            ins = nc.vector.tensor_scalar(m.states[:, c, p], m.s[:, p], m.ends[:, p, c, 0:1], None, ALU.mult)
                        link(ins)
                        dve.wait_ge(s["st_ready"], g * TPS + c + 1)
                        for p in range(GPAIR):
                            for h in range(2):
                                sl = slice(h * DK, (h + 1) * DK)
                                at = (2 * p + h) * DV
                                ins = nc.vector.scalar_tensor_tensor(
                                    out=m.s[sl, p], in0=m.s[sl, p], scalar=m.ends[sl, p, c, 1:2],
                                    in1=ps[sl, SB[c], at:at + DV], op0=ALU.mult, op1=ALU.add)
                        link(ins)
                        dve.wait_ge(s["at_ready"], g * TPS + c + 1)
                        nc.vector.tensor_tensor(m.att[:, c].rearrange("p (h t) -> p h t", h=H), ps[:, GB[c], :].rearrange("p (h t) -> p h t", h=H),
                                                const("causal")[:, None, :].broadcast_to([P, H, P]), ALU.mult).then_inc(s["masked"], 1)
                    for c in range(TPS):
                        dve.wait_ge(s["sq_ready"], g * TPS + c + 1)
                        nc.vector.tensor_reduce(m.ss[:, c], m.squares[:, c % 2].rearrange("p (h e) -> p h e", h=H), AX.X,
                                                ALU.add).then_inc(s["ss_ready"], 1)
                    dve.wait_ge(s["orstd_ready"], g + 1)
                    dve.wait_ge(s["gate_done"], g * TPS + TPS)
                    for c in range(TPS):
                        for h in range(H):
                            sl = slice(h * DV, (h + 1) * DV)
                            ins = nc.vector.scalar_tensor_tensor(out=m.gate[:, c, sl], in0=ps[:, GB[c], sl],
                                                                 scalar=m.orstd[:, c, h:h + 1], in1=m.gate[:, c, sl],
                                                                 op0=ALU.mult, op1=ALU.mult)
                        ins.then_inc(s["og_ready"], 1)
                    for c in range(TPS):
                        dve.wait_ge(s["ogt_hi"], g * TPS + c + 1)
                        nc.vector.tensor_tensor(m.o_lo[:, c].rearrange("p h t -> p (h t)"), ps[:, SB[c], :],
                                                m.o_hi[:, c].rearrange("p h t -> p (h t)"), ALU.subtract).then_inc(s["ogt_lo"], 1)
                    xt_lo_of(g + N0(n) + 1, 1 - u)
                    for half in range(2):
                        dve.wait_ge(s["y_ready"], g * 2 + half + 1)
                        xs = x[:, ds(g * TPS + 2 * half, 2), :]
                        nc.vector.scalar_tensor_tensor(out=xs, in0=ps[:, 3 + half, :].rearrange("p (t d) -> p t d", t=2),
                                                       scalar=1 / WS, in1=xs, op0=ALU.mult, op1=ALU.add).then_inc(s["y_taken"], 1)
                    dve.wait_ge(s["y_taken"], g * 2 + 4)
                    dve.sem_inc(x_updated, 1)
                each_sequence(dve, body, after_ffn0(n))

            def win(n):
                s, m = S[n], win_space()
                dve.wait_ge(s["zeroed"], 1)
                dve.sem_inc(s["y_taken"], 2)

                def body(g, u):
                    def softmax(t):
                        i = t % 2
                        sc = ps[:, 2:4, :].rearrange("p a (b k) -> p (a b) k", k=KB)
                        dve.wait_ge(s["sc_ready"], g * TPS + t + 3)
                        nc.vector.tensor_reduce(m.mx, sc, AX.X, ALU.max).then_inc(s["mx_ready"], 1)
                        dve.wait_ge(s["mx_ready"], g * TPS + t + 1)
                        nc.vector.tensor_tensor(m.p[:, i], sc, m.mx[:, :, None].broadcast_to([P, BPT * KT * 2, KB]),
                                                ALU.subtract).then_inc(s["sub_ready"], 1)

                    def normalize(t):
                        dve.wait_ge(s["c_ready"], g * TPS + t + 1)
                        nc.vector.reciprocal(m.rl, ps[:, 0, 0:BPT * KT * 2]).then_inc(s["rl_ready"], 1)
                        dve.wait_ge(s["rl_ready"], g * TPS + t + 1)
                        for h in range(4):
                            sl = slice(h * QB, (h + 1) * QB)
                            c = ps[sl, 6:8, :].rearrange("p a (b k) -> p (a b) k", k=4 * AD)
                            ins = nc.vector.tensor_tensor(
                                m.c[sl].rearrange("p a (b k) -> p (a b) k", k=4 * AD)[:, :, h * AD:(h + 1) * AD],
                                c[:, :, h * AD:(h + 1) * AD], m.rl[sl, :, None].broadcast_to([QB, BPT * KT * 2, AD]), ALU.mult)
                        ins.then_inc(s["cn_ready"], 1)

                    def ct_lo(t):
                        dve.wait_ge(s["ct_hi"], g * TPS + t + 1)
                        sl = slice(t * P, (t + 1) * P)
                        nc.vector.tensor_tensor(m.c_lo[:, :, sl], ps[:, 1, 0:KT * P].rearrange("p (f q) -> p f q", f=KT),
                                                m.c_hi[:, :, sl], ALU.subtract).then_inc(s["ct_lo"], 1)

                    softmax(0)
                    for j in range(VF):
                        dve.wait_ge(s["v_ready"], g * VF + j + 1)
                        for h in range(2):
                            w = 2 * (j - 1 + h)
                            if not 0 <= w < NB:
                                continue
                            sl = slice(h * KB, (h + 1) * KB)
                            ins = nc.vector.scalar_tensor_tensor(
                                out=m.vz[sl, w:w + 2].rearrange("p w f d -> p (w f) d")[:, :, sl],
                                in0=ps[sl, 4 + j % 4, :].rearrange("p (w d) -> p w d", d=P)[:, :, sl], scalar=1 / WS,
                                in1=bv_row[sl].rearrange("p (w d) -> p w d", d=P)[:, :, sl], op0=ALU.mult, op1=ALU.add)
                        ins.then_inc(s["v_copied"], 1)
                    dve.wait_ge(s["v_copied"], g * (VF + 2) + VF)
                    for e, w in enumerate((0, NB - 1)):
                        nc.vector.tensor_scalar(m.vz[:, w], m.vz[:, w], const("edge")[:, e:e + 1], None,
                                                ALU.mult).then_inc(s["v_copied"], 1)
                    ln_stats(g + N0(n) + 1, next_at(g))
                    for t in range(TPS):
                        if t + 1 < TPS:
                            softmax(t + 1)
                        if t == 1:
                            ln_scale(g + N0(n) + 1, next_at(g))
                        normalize(t)
                        if t >= 1:
                            ct_lo(t - 1)
                    ct_lo(TPS - 1)
                    xt_lo_of(g + N0(n) + 1, 1 - u)
                    for half in range(2):
                        dve.wait_ge(s["y_ready"], g * 2 + half + 1)
                        dve.wait_ge(s["bias_added"], g + 1)
                        xs = x[:, ds(g * TPS + 2 * half, 2), :]
                        nc.vector.scalar_tensor_tensor(out=xs, in0=ps[:, 2 + half, :].rearrange("p (t d) -> p t d", t=2),
                                                       scalar=1 / WS, in1=xs, op0=ALU.mult, op1=ALU.add).then_inc(s["y_taken"], 1)
                    dve.wait_ge(s["y_taken"], g * 2 + 4)
                    dve.sem_inc(x_updated, 1)
                each_sequence(dve, body)

            dve.wait_ge(small_loaded, 48)
            dve.wait_ge(ready0, 4)
            dve.wait_ge(x_loaded[0], 16)
            nc.vector.memset(expert_rows[:, :, NSEQ * TPS:], 0.0)
            ln_stats(0, 0)
            halves_lo()
            ternary()
            dve.wait_ge(x_loaded[1], 16)
            ln_scale(0, 0, first=True)
            xt_lo_of(0, 0)
            for n, kind in enumerate(SUBLAYERS):
                {"ffn0": ffn0, "l1ffn": l1ffn, "gla": gla, "win": win}[kind](n)

        @block.tensor
        def _(pe):
            def mm3(out_, a, b, start, stop):
                nc.tensor.matmul(out_, a[0], b[0], start=start, stop=False)
                nc.tensor.matmul(out_, a[0], b[1], start=False, stop=False)
                return nc.tensor.matmul(out_, a[1], b[0], start=False, stop=stop)

            def both(w, sl):
                return w[0][:, sl], w[1][:, sl]

            def xt(u, k, sl=slice(0, SEQ)):
                sl = slice(PAD + sl.start, PAD + sl.stop)
                return xt_hi[:, u, k, sl], xt_lo[:, u, k, sl]

            def transposes(m):
                pe.wait_ge(xn_ready, m + 1)
                for k in range(KT):
                    for t in range(TPS):
                        ins = nc.tensor.transpose(ps[:, k, t * P:(t + 1) * P], xn[:, t, k * P:(k + 1) * P], ident)
                ins.then_inc(pt_ready, 1)

            def xt_ready(m):
                pe.wait_ge(xt_hi_ready, m + 1)
                pe.wait_ge(xt_lo_ready, m + 1)

            def ffn0(n):
                s, m = S[n], ffn0_space()
                G0, T0 = earlier(n) * NSEQ, earlier(n) * TILES
                h = m.h_hi, m.h_lo
                if not earlier(n):
                    pe.sem_inc(s["y_ready"], 2)

                def router(g, u):
                    xt_ready(g + N0(n))
                    for t in range(TPS):
                        for k in range(KT):
                            ins = mm3(ps[:, 0, t * NE:(t + 1) * NE], xt(u, k, slice(t * P, (t + 1) * P)),
                                      both(wr, slice(k * NE, (k + 1) * NE)), k == 0, k == KT - 1)
                    ins.then_inc(s["router_ready"], 1)

                def positions(g):
                    pe.wait_ge(s["mask_ready"], (g + G0) + 1)
                    pos, total = ps[:, 0, 64:64 + TPS * NE], ps[:, 0, 96:96 + NE]
                    nc.tensor.matmul(pos, const("causal"), m.mask.rearrange("p t e -> p (t e)"), start=True, stop=False,
                                     skip_group_check=True)
                    for t in range(TPS - 1):
                        nc.tensor.matmul(pos[:, (t + 1) * NE:].rearrange("p (t e) -> p t e", e=NE), const("ones"),
                                         m.mask[:, t:t + 1].broadcast_to([P, TPS - 1 - t, NE]), start=False, stop=(t == TPS - 2),
                                         skip_group_check=True)
                    for t in range(TPS):
                        ins = nc.tensor.matmul(total, const("ones"), m.mask[:, t], start=(t == 0), stop=(t == TPS - 1),
                                               skip_group_check=True)
                    ins.then_inc(s["pos_ready"], 1)

                def body(g, u):
                    def up(q):
                        b = 2 + 2 * (q % 2)
                        pe.wait_ge(s["prod_ready"], (g + G0) * SU + q + 1)
                        for half in range(2):
                            for k in range(KT):
                                w = both((wsh1, wsh2)[half], slice(k * HSH + q * P, k * HSH + (q + 1) * P))
                                ins = mm3(ps[:, b + half, :], w, xt(u, k), k == 0, k == KT - 1)
                        ins.then_inc(s["up_ready"], 1)

                    def down(half):
                        pe.wait_ge(s["y_taken"], (g + G0) * 2 + half + 1)
                        for t in range(2 * half, 2 * half + 2):
                            sl = slice(t * P, (t + 1) * P)
                            for q in range(SU):
                                ins = mm3(ps[:, 6 + half, (t % 2) * D:(t % 2 + 1) * D], (h[0][:, q, sl], h[1][:, q, sl]),
                                          both(wsh3, slice(q * D, (q + 1) * D)), q == 0, q == SU - 1)
                        ins.then_inc(s["y_ready"], 1)

                    for q in range(SU):
                        up(q)
                        if q == 1:
                            positions(g)
                    pe.wait_ge(s["h_hi_ready"], (g + G0) * SU + SU)
                    pe.wait_ge(s["h_lo_ready"], (g + G0) * SU + SU + PRODS)
                    down(0)
                    if not is_last(g):
                        pe.wait_ge(s["rows_ready"], (g + G0) + 2)
                        transposes(g + N0(n) + 1)
                    down(1)
                    if not is_last(g):
                        router(g + 1, 1 - u)

                router(0, 0)
                each_sequence(pe, body, True)

                pe.wait_ge(s["tab_ready"], 3 * (1 + earlier(n)))
                pe.wait_ge(s["y_taken"], 2 * (NSEQ + G0) + 2)
                pe.wait_ge(s["rows_ready"], (NSEQ + G0) + 1)

                def columns(j):
                    return pe.value_load(m.table[0:1, ds(TILES + j, 1)], min_val=0, max_val=(NE - 1) * 2 * HE)

                def step(i, b, u, has):
                    if has(0):
                        pe.wait_ge(s[f"tile_in{u}"], 16 * (b + 1) + 4 * T0)
                        for k in range(KT):
                            ins = nc.tensor.transpose(ps[:, u % 2, k * P:(k + 1) * P], m.tile_x[:, u, k * P:(k + 1) * P], ident)
                        ins.then_inc(s["tile_turned"], 1)
                    if has(1):
                        j, v = i - 1, (u - 1) % 2
                        at = columns(j)
                        pe.wait_ge(s["tile_hi"], j + 1 + T0)
                        pe.wait_ge(s["tile_lo"], j + 1 + T0)
                        if not isinstance(j, int) or j >= 2:
                            pe.wait_ge(s["tile_prod"], j - 1 + T0)
                        for k in range(KT):
                            ins = mm3(ps[:, 2 + v, :], (m.t_hi[:, v, k], m.t_lo[:, v, k]),
                                      both(wup, ds(at + k * NE * 2 * HE, 2 * HE)), k == 0, k == KT - 1)
                        ins.then_inc(s["tile_up"], 1)
                    if has(2):
                        j, v = i - 2, u % 2
                        pe.wait_ge(s["tile_prod"], j + 1 + T0)
                        for k in range(EU):
                            ins = nc.tensor.transpose(ps[:, 4 + v, k * P:(k + 1) * P], m.t_prod[:, v, k * P:(k + 1) * P], ident)
                        ins.then_inc(s["th_turned"], 1)
                    if has(3):
                        j, v = i - 3, (u - 3) % 2
                        at = columns(j)
                        pe.wait_ge(s["th_hi"], j + 1 + T0)
                        pe.wait_ge(s["th_lo"], j + 1 + T0)
                        if not isinstance(j, int) or j >= 2:
                            pe.wait_ge(s["tile_y"], j - 1 + T0)
                        for k in range(EU):
                            ins = mm3(ps[:, 6 + v, 0:D], (m.th_hi[:, v, k], m.th_lo[:, v, k]), both(wdn, ds(at + k * D, D)),
                                      k == 0, k == EU - 1)
                        ins.then_inc(s["tile_down"], 1)
                each_tile(pe, step, 3)
                transposes(N0(n + 1))

            def l1ffn(n):
                s = S[n]
                h_hi, h_lo, _ = l1ffn_space()
                pe.sem_inc(s["y_ready"], 4)

                def step(g, u, up, down):
                    if up:
                        up_part(g, u)
                    if down:
                        down_part(g - 1, 1 - u, up)
                    else:
                        transposes(g + N0(n) + 1)

                def up_part(g, u):
                    xt_ready(g + N0(n))
                    for q in range(FU):
                        if q >= 4 or not isinstance(g, int) or g:
                            pe.wait_ge(s["relu_ready"], g * FU + q - 3)
                        for k in range(KT):
                            w = w1q[:, k * FF + q * P:k * FF + (q + 1) * P]
                            nc.tensor.matmul(ps[:, 2 + q % 4, :], w, xt_hi[:, u, k, TOK], start=(k == 0), stop=False)
                            ins = nc.tensor.matmul(ps[:, 2 + q % 4, :], w, xt_lo[:, u, k, TOK], start=False, stop=(k == KT - 1))
                        ins.then_inc(s["up_ready"], 1)

                def down_part(g, u, next_one):
                    pe.wait_ge(s["h_hi_ready"], g * FU + FU)
                    pe.wait_ge(s["h_lo_ready"], g * FU + FU + RELUS)
                    for half in range(2):
                        if half and next_one:
                            transposes(g + N0(n) + 2)
                        pe.wait_ge(s["y_taken"], g * 2 + half + 1)
                        for t in range(2 * half, 2 * half + 2):
                            sl = slice(t * P, (t + 1) * P)
                            for q in range(FU):
                                o = ps[:, 6 + half, (t % 2) * D:(t % 2 + 1) * D]
                                w = w2q[:, q * D:(q + 1) * D]
                                nc.tensor.matmul(o, h_hi[:, u, q, sl], w, start=(q == 0), stop=False)
                                ins = nc.tensor.matmul(o, h_lo[:, u, q, sl], w, start=False, stop=(q == FU - 1))
                        ins.then_inc(s["y_ready"], 1)
                skewed(pe, step)

            def gla(n):
                s, m = S[n], gla_space()

                def body(g, u):
                    def project(out_, w, c, n_, transposed=None):
                        for k in range(KT):
                            wk = both(w, slice(k * (w[0].shape[1] // KT) + c, k * (w[0].shape[1] // KT) + c + n_))
                            if transposed is None:
                                ins = mm3(out_, wk, xt(u, k), k == 0, k == KT - 1)
                            else:
                                ins = mm3(out_, xt(u, k, slice(transposed * P, (transposed + 1) * P)), wk, k == 0, k == KT - 1)
                        return ins

                    xt_ready(g + N0(n))
                    pe.wait_ge(s["y_taken"], g * 2 + 2)
                    project(ps[0:LOW, 2, :], gk1, 0, LOW).then_inc(s["t_ready"], 1)
                    for j in range(2 * GPAIR):
                        project(ps[:, 3 + j, :], gqk, j * P, P).then_inc(s["qk_ready"], 1)
                    pe.wait_ge(s["t_hi"], g + 1)
                    pe.wait_ge(s["t_lo"], g + 1)
                    for j, b in enumerate((2, 7)):
                        for t in range(2):
                            sl = slice((2 * j + t) * P, (2 * j + t + 1) * P)
                            ins = mm3(ps[:, b, t * H * DK:(t + 1) * H * DK], (m.t_hi[0:LOW, sl], m.t_lo[0:LOW, sl]),
                                      (gk2[0][:, :], gk2[1][:, :]), True, True)
                        ins.then_inc(s["logits_ready"], 1)
                    for c in range(TPS):
                        pe.wait_ge(s["qk_copied"], g * 2 * GPAIR + c + 1)
                        project(ps[:, GB[c], :], gv, 0, H * DV, c).then_inc(s["v_ready"], 1)
                    for j, b in enumerate((2, 7)):
                        pe.wait_ge(s["lb_ready"], g * 2 + j + 1)
                        for t in range(2):
                            ins = project(ps[:, b, t * H * DK:(t + 1) * H * DK], gqk, H * DK, H * DK, 2 * j + t)
                        ins.then_inc(s["kt_ready"], 1)
                    pe.wait_ge(s["g_ready"], g + 1)
                    pe.wait_ge(s["v_copied"], g * TPS + TPS)
                    for p in range(GPAIR):
                        for c in range(TPS):
                            gp = m.lb[:, c, p * P:(p + 1) * P]
                            nc.tensor.matmul(ps[:, 3 + p, c * P:(c + 1) * P], gp, const("cumref"), start=True, stop=True)
                            at = (p * TPS + c) * 2
                            nc.tensor.matmul(ps[:, 0, at:at + 2], gp, const("ends"), start=True, stop=True)
                    for c in range(TPS):
                        ins = nc.tensor.matmul(ps[:, 5 + c // 2, (c % 2) * 256:(c % 2 + 1) * 256], const("after"), m.lb[:, c],
                                               start=True, stop=True)
                    ins.then_inc(s["cum_ready"], 1)
                    pe.wait_ge(s["kdec_ready"], g * 2 + 2)
                    for c in range(TPS):
                        for p in range(GPAIR):
                            ins = nc.tensor.matmul(ps[:, SB[c], p * 256:(p + 1) * 256], m.soft[:, c, p * P:(p + 1) * P],
                                                   m.v[:, c, p * 256:(p + 1) * 256], start=True, stop=True)
                        ins.then_inc(s["st_ready"], 1)
                    pe.wait_ge(s["q_ready"], g * 2 + 4)
                    pe.wait_ge(s["k_ready"], g + 1)
                    for c in range(TPS):
                        sl = slice(c * P, (c + 1) * P)
                        for p in range(GPAIR):
                            ins = nc.tensor.matmul(ps[:, GB[c], p * 256:(p + 1) * 256], m.k[:, p, sl], m.qz[:, p, :, sl],
                                                   start=True, stop=True)
                        ins.then_inc(s["at_ready"], 1)
                    for c in range(TPS):
                        pe.wait_ge(s["masked"], g * TPS + c + 1)
                        project(ps[:, GB[c], :], gg, 0, H * DV, c).then_inc(s["gate_ready"], 1)
                    for c in range(TPS):
                        pe.wait_ge(s["gate_done"], g * TPS + c + 1)
                        for h in range(H):
                            o = ps[:, GB[c], h * DV:(h + 1) * DV]
                            nc.tensor.matmul(o, m.att[:, c, h * P:(h + 1) * P], m.v[:, c, h * DV:(h + 1) * DV],
                                             start=True, stop=False)
                            ins = nc.tensor.matmul(o, m.qz[:, h // 2, h % 2, c * P:(c + 1) * P], m.states[:, c, h // 2],
                                                   start=False, stop=True)
                        ins.then_inc(s["o_ready"], 1)
                    for c in range(TPS):
                        pe.wait_ge(s["og_ready"], g * TPS + c + 1)
                        for h in range(H):
                            ins = nc.tensor.transpose(ps[:, SB[c], h * P:(h + 1) * P], m.gate[:, c, h * DV:(h + 1) * DV], ident)
                        ins.then_inc(s["ogt_ready"], 1)
                    for half in range(2):
                        pe.wait_ge(s["ogt_hi"], g * TPS + 2 * half + 2)
                        pe.wait_ge(s["ogt_lo"], g * TPS + 2 * half + 2)
                        for t in range(2):
                            c = 2 * half + t
                            for h in range(H):
                                ins = mm3(ps[:, 3 + half, t * D:(t + 1) * D], (m.o_hi[:, c, h], m.o_lo[:, c, h]),
                                          both(go, slice(h * D, (h + 1) * D)), h == 0, h == H - 1)
                        ins.then_inc(s["y_ready"], 1)
                    transposes(g + N0(n) + 1)
                each_sequence(pe, body)

            def win(n):
                s, m = S[n], win_space()
                pe.sem_inc(s["sc_ready"], 2)
                pe.wait_ge(s["zeroed"], 1)

                def body(g, u):
                    xt_ready(g + N0(n))
                    for j in range(2 * KT):
                        if j < 2:
                            pe.wait_ge(s["y_taken"], g * 2 + j + 1)
                        for k in range(KT):
                            c = k * 3 * D + j * P
                            ins = mm3(ps[:, 2 + j, :], both(aqkv, slice(c, c + P)), xt(u, k), k == 0, k == KT - 1)
                        ins.then_inc(s["qk_ready"], 1)

                    def scores(t):
                        pe.wait_ge(s["qz_ready"], g * TPS + t + 1)
                        for b in range(2):
                            nc.tensor.matmul(ps[:, 2 + b, :], ident16[:], window16[:], start=True, stop=False, skip_group_check=True)
                            for w in range(2):
                                for f in range(KT):
                                    for hg in range(2):
                                        blk = 2 * b + w
                                        at = ((w * KT + f) * 2 + hg) * KB
                                        key = (t * BPT + blk) * QB
                                        ins = nc.tensor.matmul(
                                            ps[:, 2 + b, at:at + KB], m.qz[:, t % 2 * KT + f, blk, 4 * hg:4 * hg + 4].rearrange("p h q -> p (h q)"),
                                            m.k[:, f, key:key + KB], start=False, stop=True, skip_group_check=True)
                        ins.then_inc(s["sc_ready"], 1)

                    def turn(t):
                        pe.wait_ge(s["exp_ready"], g * TPS + t + 1)
                        if t == 0:
                            pe.wait_ge(s["v_copied"], g * (VF + 2) + VF + 2)
                        for j in range(BPT * KT):
                            ins = nc.tensor.transpose(ps[:, 4 + j // 4, (j % 4) * P:(j % 4 + 1) * P],
                                                      m.p[:, t % 2, 2 * j:2 * j + 2].rearrange("p a b -> p (a b)"), ident)
                        ins.then_inc(s["pt_ready"], 1)

                    def values(t):
                        pe.wait_ge(s["pt_copied"], g * TPS + t + 1)
                        if t >= 1:
                            pe.wait_ge(s["cn_ready"], g * TPS + t)
                        for j in range(BPT * KT):
                            w = m.pt[:, t % 2, j]
                            nc.tensor.matmul(ps[:, 6 + j // 4, (j % 4) * P:(j % 4 + 1) * P], w,
                                             m.vz[:, t * BPT + j // KT, j % KT], start=True, stop=True)
                            ins = nc.tensor.matmul(ps[:, 0, 2 * j:2 * j + 2], w, const("hgsum"), start=True, stop=True)
                        ins.then_inc(s["c_ready"], 1)

                    def context(t):
                        pe.wait_ge(s["cn_ready"], g * TPS + t + 1)
                        if t >= 1:
                            pe.wait_ge(s["ct_lo"], g * TPS + t)
                        for j in range(BPT * KT):
                            at = (j % KT) * P + (j // KT) * QB
                            ins = nc.tensor.matmul(ps[:, 1, at:at + QB], m.c[:, j], const("fold"), start=True, stop=True)
                        ins.then_inc(s["ct_ready"], 1)

                    pe.wait_ge(s["qk_copied"], g * 2 * KT + 2 * KT)
                    scores(0)
                    for j in range(VF):
                        if j >= 4:
                            pe.wait_ge(s["v_copied"], g * (VF + 2) + j - 3)
                        for w in range(2):
                            at = (2 * j + w) * QB
                            lhs, half = slice(at - 2 * QB, at - 2 * QB + P), slice(0, P)
                            if j == 0:
                                lhs, half = slice(at, at + KB), slice(KB, P)
                            elif j == VF - 1:
                                lhs, half = slice(at - 2 * QB, at - 2 * QB + KB), slice(0, KB)
                            for k in range(KT):
                                c = k * 3 * D + 2 * D
                                ins = mm3(ps[half, 4 + j % 4, w * D:(w + 1) * D], (xt_hi[:, u, k, lhs], xt_lo[:, u, k, lhs]),
                                          both(aqkv, slice(c, c + D)), k == 0, k == KT - 1)
                        ins.then_inc(s["v_ready"], 1)
                    for t in range(TPS):
                        turn(t)
                        if t >= 1:
                            context(t - 1)
                        if t + 1 < TPS:
                            pe.wait_ge(s["sub_ready"], g * TPS + t + 1)
                            scores(t + 1)
                        values(t)
                    context(TPS - 1)
                    pe.wait_ge(s["ct_hi"], g * TPS + TPS)
                    pe.wait_ge(s["ct_lo"], g * TPS + TPS)
                    pe.wait_ge(s["sub_ready"], g * TPS + TPS)
                    transposes(g + N0(n) + 1)
                    for half in range(2):
                        for t in range(2 * half, 2 * half + 2):
                            sl = slice(t * P, (t + 1) * P)
                            for f in range(KT):
                                ins = mm3(ps[:, 2 + half, (t % 2) * D:(t % 2 + 1) * D], (m.c_hi[:, f, sl], m.c_lo[:, f, sl]),
                                          both(ao, slice(f * D, (f + 1) * D)), f == 0, f == KT - 1)
                        ins.then_inc(s["y_ready"], 1)
                each_sequence(pe, body)

            pe.wait_ge(small_loaded, 48)
            pe.wait_ge(ready0, 4)
            pe.wait_ge(tern, 2)
            ones = const("ones")
            nc.tensor.matmul(ps[:, 7, 0:2], ones, tsum[:], start=True, stop=True).then_inc(tern_sum, 1)
            pe.wait_ge(w_lo_done, NCH)
            pe.wait_ge(tern, 10)
            transposes(0)
            for n, kind in enumerate(SUBLAYERS):
                if n:
                    pe.wait_ge(x_updated, N0(n))
                {"ffn0": ffn0, "l1ffn": l1ffn, "gla": gla, "win": win}[kind](n)


def constants(np):
    p = np.arange(P)[:, None]
    f = np.arange(P)[None, :]
    q, kk = p % QB, np.arange(KB)[None, :]
    e, j = np.arange(NE)[:, None], np.arange(NE)[None, :]
    c = {
        "ident": p == f,
        "ones": np.ones((P, P)),
        "causal": f >= p,
        "cumref": ((p <= f) * 1.0 - (p < P // 2)) / GATE_NORM,
        "after": (p > f) / GATE_NORM,
        "ends": np.concatenate([(p < P // 2) * 1.0, np.ones((P, 1))], 1) / GATE_NORM,
        "tri": np.broadcast_to((j < e).reshape(1, NE * NE), (P, NE * NE)),
        "window": np.where((kk >= q) & (kk <= q + 2 * PAD), 0.0, MASKED),
        "fold": q == np.arange(QB)[None, :],
        "hgsum": p // KB == np.arange(2)[None, :],
        "heads": p // AD == np.arange(8)[None, :],
        "iota": np.broadcast_to(np.arange(TILES)[None], (P, TILES)),
        "regions": np.broadcast_to(np.arange(NE)[None] * REGION, (P, NE)),
        "edge": np.concatenate([p % KB >= PAD, p % KB < KB - PAD], 1),
    }
    return np.concatenate([np.asarray(c[n], np.float32) for n in CONST_COLS], 1)


def laid_out(np, a):
    def tiles(w):
        k, n = w.shape
        return np.ascontiguousarray(w.reshape(k // P, P, n).transpose(1, 0, 2).reshape(P, -1))

    def down(v):
        return v.reshape(-1, P).T

    qkv = a["L1_attn_w_qkv"].reshape(AH, 3, AD, D).transpose(1, 0, 2, 3).reshape(3 * D, D)
    bqkv = a["L1_attn_b_qkv"].reshape(AH, 3, AD).transpose(1, 0, 2).reshape(3, D)
    rows = np.concatenate([a["L0_attn_bgk2"], a["L1_ffn_b2"], a["L1_attn_b_out"], bqkv[2], bqkv[2],
                           a["L0_ffn_expert_bias"]])
    return {
        "x": a["L0_attn_x"].reshape(-1, D),
        "consts": constants(np),
        "rows": np.ascontiguousarray(np.broadcast_to(rows[None], (P, rows.size))),
        "cols": np.ascontiguousarray(np.concatenate([down(a["L1_ffn_b1"]), down(bqkv[0]), down(bqkv[1]),
                                                     down(a["L0_attn_rms_w"])], 1)),
        "w_sh1": tiles(a["L0_ffn_shared_w1"].T), "w_sh2": tiles(a["L0_ffn_shared_w2"].T),
        "w_sh3": tiles(a["L0_ffn_shared_w3"].T), "w_r": tiles(a["L0_ffn_router_w"].T),
        "w_up": tiles(a["L0_ffn_w12"].reshape(-1, D).T),
        "w_dn": tiles(a["L0_ffn_w3"].transpose(0, 2, 1).reshape(-1, D)),
        "g_qk": tiles(np.concatenate([a["L0_attn_Wq"], a["L0_attn_Wk"]]).T),
        "g_v": tiles(a["L0_attn_Wv"].T), "g_g": tiles(a["L0_attn_Wg"].T),
        "g_k1": tiles(a["L0_attn_Wgk1"].T), "g_k2": np.ascontiguousarray(a["L0_attn_Wgk2"].T),
        "g_o": tiles(a["L0_attn_Wout"].T),
        "a_qkv": tiles(qkv.T), "a_o": tiles(a["L1_attn_w_out"].T),
        "w_1": tiles(a["L1_ffn_W1"].T), "w_2": tiles(a["L1_ffn_W2"].T),
    }


def kernel(**inputs):
    import numpy as np
    import concourse.bacc as bacc
    from concourse.bass_utils import run_bass_kernel_spmd

    nc = bacc.Bacc("TRN2", target_bir_lowering=False, num_devices=1)
    arrays = laid_out(np, {k: np.asarray(v) for k, v in inputs.items()})
    T = {n: nc.dram_tensor(f"in_{n}", v.shape, mybir.dt.from_np(v.dtype), kind="ExternalInput").ap()
         for n, v in arrays.items()}
    out = nc.dram_tensor("out_x", (NSEQ * SEQ, D), F32, kind="ExternalOutput").ap()
    build(nc, T, out)
    r = run_bass_kernel_spmd(nc, [{f"in_{n}": v for n, v in arrays.items()}], core_ids=[0])
    return r.results[0]["out_x"].reshape(NSEQ, SEQ, D)
```

```python
from contextlib import ExitStack

import concourse.bass as bass
from concourse import mybir

P = 128
D = 256
KT = D // P
NSEQ, SEQ = 8, 512
TPS = SEQ // P
EPS = 1e-5
WS = 64.0
HS = 16.0

NE, HE = 8, 256
HSH = 1024
SU, EU = HSH // P, HE // P
TOPK = 2
REGION = NSEQ * SEQ + P
TILES = NSEQ * SEQ * TOPK // P + NE - 1
TILES += -TILES % 4
DUMP = TILES - NSEQ * SEQ * TOPK // P
ROWS = NE * REGION + DUMP * P

FF = 1024
FU = FF // P
PRODS = 4
RELUS = 4

H, DK, DV = 4, 64, 128
GPAIR = H // 2
LOW = 32
GATE_NORM = 32.0

AH, AD = 16, 16
PAD = 16
QB, KB = 32, 64
NB = SEQ // QB
BPT = P // QB
HG = AH // 4
VF = NB // 2 + 1
VF_FIRST = 5
MASKED = -1e30

ALU = mybir.AluOpType
ACT = mybir.ActivationFunctionType
AX = mybir.AxisListType
F32 = mybir.dt.float32
F16 = mybir.dt.float16
I32 = mybir.dt.int32


LATER = {"w_up": KT * NE * 2 * HE, "w_dn": NE * EU * D, "g_qk": KT * 2 * H * DK, "g_v": KT * H * DV,
         "g_g": KT * H * DV, "g_k1": KT * LOW, "g_k2": H * DK, "a_o": KT * D}
LPS = 2
LCH = sum(LATER.values()) // (NSEQ * LPS)
assert LCH * NSEQ * LPS == sum(LATER.values()) and LCH <= TPS * D


class Space:
    pass


SUBLAYERS = ("ffn0", "gla", "ffn0", "l1ffn", "win", "l1ffn")

CONST_COLS = {"ident": 128, "ones": 128, "causal": 128, "cumref": 128, "after": 128, "ends": 2, "tri": NE * NE,
              "window": 64, "edge": 2, "heads": 8, "iota": TILES, "regions": NE}


def const_at(name):
    at = 0
    for n, w in CONST_COLS.items():
        if n == name:
            return slice(at, at + w)
        at += w


NCONST = sum(CONST_COLS.values())


def ds(at, n):
    return bass.ds(at, n)


def build(nc, T, out):
    ctx = ExitStack()
    with ctx:
        def sb(name, shape, dt=F32):
            return ctx.enter_context(nc.sbuf_tensor(name, shape, dt))

        def sem(name):
            return ctx.enter_context(nc.semaphore(name))

        x = sb("x", [P, NSEQ * TPS, D])
        consts = sb("consts", [P, NCONST])
        window16 = sb("window16", [P, 8, KB], mybir.dt.bfloat16)
        ident16 = sb("ident16", [P, P], mybir.dt.bfloat16)

        def const(name):
            return consts[:, const_at(name)]

        ident = const("ident")

        def pair(name, cols, rows=P):
            return sb(name + "_hi", [rows, cols], F16), sb(name + "_lo", [rows, cols], F16)

        wsh1 = pair("wsh1", KT * HSH)
        wsh2 = pair("wsh2", KT * HSH)
        wsh3 = pair("wsh3", SU * D)
        wr = pair("wr", KT * NE)
        go = pair("go", H * D)
        aqkv = pair("aqkv", KT * 3 * D)
        later = pair("later", sum(LATER.values()))

        def later_at(name, rows=P):
            at = 0
            for n, w in LATER.items():
                if n == name:
                    return later[0][0:rows, at:at + w], later[1][0:rows, at:at + w]
                at += w

        wup, wdn = later_at("w_up"), later_at("w_dn")
        gqk, gv, gg = later_at("g_qk"), later_at("g_v"), later_at("g_g")
        gk1, gk2 = later_at("g_k1"), later_at("g_k2", LOW)
        ao = later_at("a_o")
        w1q = sb("w1q", [P, KT * FF], F16)
        w2q = sb("w2q", [P, FU * D], F16)
        rows = sb("rows", [P, 5 * D + NE])
        bgk_row, b2_row, bo_row = (rows[:, n * D:(n + 1) * D] for n in range(3))
        bv_row = rows[:, 3 * D:5 * D]
        ebias_row = rows[:, 5 * D:]
        cols = sb("cols", [P, FU + 2 * KT + 1])
        b1_col, bq_col, bk_col = cols[:, 0:FU], cols[:, FU:FU + KT], cols[:, FU + KT:FU + 2 * KT]
        rms_col = cols[:, FU + 2 * KT:]

        xn = sb("xn", [P, TPS, D + 1])
        expert_rows = sb("expert_rows", [P, TOPK, (NSEQ + 2) * TPS])
        gather_rows = sb("gather_rows", [P, 2, TOPK, TPS], I32)
        yg = sb("yg", [P, TPS, D])
        stats = sb("stats", [P, TPS, 6])
        mv = sb("mv", [P, TPS, 2])
        rstd = sb("rstd", [P, TPS])
        tsum, thr = sb("tsum", [P, 2]), sb("thr", [P, 2, 2])
        eps = sb("eps", [P, TPS])
        neghalf = sb("neghalf", [P, 4 * TPS])
        XW = SEQ + 2 * PAD
        xt_hi = sb("xt_hi", [P, 2, KT, XW], F16)
        xt_lo = sb("xt_lo", [P, 2, KT, XW], F16)
        TOK = slice(PAD, PAD + SEQ)

        WORK = 44416
        work = sb("work", [P, WORK // 4])

        class Carve:
            def __init__(self, base=None):
                self.base = work if base is None else base
                self.room = (4 if base is None else 2) * self.base.shape[1]
                self.at = 0

            def __call__(self, shape, dt=F32):
                n = 1
                for s in shape:
                    n *= s
                size = (2 if dt == F16 else 4) * n
                each = 4 if self.base is work else 2
                a = self.base[:, self.at // each:(self.at + size) // each]
                self.at += size
                assert self.at <= self.room, self.at
                if dt != (F32 if each == 4 else F16):
                    a = a.bitcast(dt)
                names = "abcd"[:len(shape)]
                if len(shape) == 1:
                    return a
                return a.rearrange(f"p ({' '.join(names)}) -> p {' '.join(names)}",
                                   **{n: s for n, s in zip(names[1:], shape[1:])})

        ps = ctx.enter_context(nc.psum_tensor("ps", [P, 8, 512], F32))

        x_loaded = [sem(f"x_loaded{n}") for n in range(2)]
        small_loaded = sem("small_loaded")
        x_stored = sem("x_stored")
        ready0 = sem("constants_ready")
        NST = 4
        staged = [sem(f"staged{n}") for n in range(NST)]
        w_hi_done, w_lo_done = sem("w_hi_done"), sem("w_lo_done")
        later_in = [sem(f"later_in{v}") for v in range(LPS)]
        later_hi_done, later_lo_done = sem("later_hi_done"), sem("later_lo_done")
        tern = sem("ternary_steps")
        tern_sum = sem("ternary_sum")
        mv_ready, rstd_ready, xn_ready = sem("mv_ready"), sem("rstd_ready"), sem("xn_ready")
        ln_step = sem("ln_step")
        pt_ready, xt_hi_ready, xt_lo_ready = sem("pt_ready"), sem("xt_hi_ready"), sem("xt_lo_ready")
        x_updated = sem("x_updated")
        rstd_step = sem("rstd_step")
        pool_stood = sem("pool_wait_stood_alone")
        stood = sem("wait_stood_alone")

        def names(prefix, text):
            return {n: sem(f"{prefix}_{n}") for n in text.split()}

        S = []
        for n, kind in enumerate(SUBLAYERS):
            text = {
                "ffn0": "router_ready scores_ready gate_step mask_ready pos_ready base_set rows_ready gate_set scattered0 "
                        "scattered1 up_ready silu_ready prod_ready h_hi_ready h_lo_ready y_ready y_taken "
                        "zeros_set zero_filled tab_step tab_ready tile_in0 tile_in1 tile_in2 tile_in3 tile_turned "
                        "tile_hi tile_lo tile_up tile_silu tile_prod th_turned th_hi th_lo tile_down tile_y tile_out0 "
                        "tile_out1 tile_out2 tile_out3 rows_step gathered0 gathered1 combined",
                "l1ffn": "up_ready relu_ready h_hi_ready h_lo_ready y_ready y_taken bias_added",
                "gla": "t_ready t_hi t_lo qk_ready qk_copied logits_ready lb_ready soft_step g_ready v_ready v_copied "
                       "kt_ready cum_ready exps_ready q_ready k_ready kdec_ready at_ready masked st_ready s_step "
                       "gate_ready gate_done o_ready sq_ready ss_ready orstd_step orstd_ready og_ready ogt_ready "
                       "ogt_hi ogt_lo y_ready y_taken",
                "win": "zeroed qk_ready qk_copied qz_ready v_ready v_copied sc_ready mx_ready sub_ready "
                       "exp_ready pt_ready pt_copied c_ready sum_ready rl_ready cn_ready ct_ready ct_hi ct_lo y_ready "
                       "y_taken bias_added",
            }[kind]
            if kind in SUBLAYERS[:n] and kind == "ffn0":
                S.append(S[SUBLAYERS.index(kind)])
            else:
                S.append(names(f"{kind}{n}", text))

        N0 = lambda n: n * NSEQ

        def earlier(n):
            return SUBLAYERS[:n].count("ffn0")


        SPLIT = [("w_sh1", wsh1, KT * HSH), ("w_sh2", wsh2, KT * HSH), ("w_r", wr, KT * NE), ("w_sh3", wsh3, SU * D),
                 ("g_o", go, H * D), ("a_qkv", aqkv, KT * 3 * D)]
        FIRST = 4
        CH = 2048
        TERN = [("w_1", w1q), ("w_2", w2q)]
        stage = Carve()([NST, CH])
        loads = [(name, n) for name, _, n in SPLIT[:FIRST]] + [(name, CH) for name, _ in TERN] + \
                [(name, n) for name, _, n in SPLIT[FIRST:]]

        def load_of(m):
            return m if m < FIRST else m + len(TERN)

        def load_done(eng, m):
            eng.wait_ge(staged[m % NST], 16 * (m // NST + 1))

        def staging_left(eng):
            eng.wait_ge(w_lo_done, len(SPLIT))
            eng.wait_ge(tern, 10)

        def ffn0_space():
            r, at = Carve(), Carve()
            m = Space()
            m.h_hi, m.h_lo = r([SU, SEQ], F16), r([SU, SEQ], F16)
            m.t_hi, m.t_lo = at([2, KT, P], F16), at([2, KT, P], F16)
            m.t_silu, m.t_prod = at([2, HE]), at([2, HE])
            m.th_hi, m.th_lo = at([2, EU, P], F16), at([2, EU, P], F16)
            m.t_y = at([4, D])
            assert at.at <= r.at
            m.silu, m.prod = r([2, SEQ]), r([PRODS, SEQ])
            m.scores, m.biased, m.mask, m.rank, m.row = (r([TPS, NE]) for _ in range(5))
            m.beats, m.ties = r([TPS, NE, NE]), r([TPS, NE, NE])
            m.onehot, m.picked = r([TOPK, TPS * NE]), r([TOPK, TPS * NE])
            m.gate, m.scatter_rows = r([TOPK, TPS]), r([TOPK, TPS], I32)
            m.base = r([NE])
            m.tile_x, m.zeros = r([4, D + 1]), r([D + 1])
            m.count, m.tiles, m.end, m.jump = (r([NE]) for _ in range(4))
            m.more = r([NE, NSEQ * TPS])
            m.over, m.sums = r([TILES, NE]), r([2, TILES])
            m.before = r([NE, NE])
            m.table = r([2 * TILES + NE], I32)
            return m

        def later_stage(m):
            return yg[:, :, :].rearrange("p t d -> p (t d)")[:, 0:LCH], m.tile_x.rearrange("p v d -> p (v d)")[:, 0:LCH]

        def yg_buffers(n):
            if "ffn0" in SUBLAYERS[n:]:
                return [yg[:, :, :]]
            at = Carve(wup[0])
            return [at([TPS, D]), at([TPS, D])]

        def is_last(g):
            return isinstance(g, int) and g == NSEQ - 1

        def after_ffn0(n):
            return n > 0 and SUBLAYERS[n - 1] == "ffn0"

        def l1ffn_space():
            r = Carve()
            return r([2, FU, SEQ], F16), r([2, FU, SEQ], F16), r([RELUS, SEQ])

        def gla_space():
            r = Carve()
            m = Space()
            m.t_hi, m.t_lo = r([SEQ], F16), r([SEQ], F16)
            m.q = r([GPAIR, SEQ])
            m.states = m.q.rearrange("p a (b c) -> p (a b) c", c=DV).rearrange("p (c a) d -> p c a d", a=GPAIR)
            m.k = r([GPAIR, SEQ])
            m.squares = m.k
            m.v = r([TPS, H * DV])
            m.lb = r([TPS, H * DK])
            m.soft = r([TPS, H * DK])
            at = Carve()
            at.at = r.at - 2 * 4 * TPS * H * DK
            m.gate = at([TPS, H * DV])
            m.up, m.down = r([GPAIR, SEQ]), r([GPAIR, SEQ])
            at.at = r.at - 2 * 4 * GPAIR * SEQ
            m.att = at([TPS, H * P])
            at.at = r.at - 2 * 4 * GPAIR * SEQ
            m.o_hi, m.o_lo = at([TPS, H, P], F16), at([TPS, H, P], F16)
            m.qz = r([GPAIR, 2, SEQ])
            m.ends = r([GPAIR, TPS, 2])
            m.s = r([GPAIR, DV])
            m.ss, m.orstd = r([TPS, H]), r([TPS, H])
            return m

        def win_space():
            r = Carve()
            m = Space()
            m.vz = Carve(wup[0])([NB, KT, P])
            m.qz = Carve(wup[1])([2 * KT, BPT, 8, QB])
            m.q = r([KT, SEQ])
            m.k = r([KT, XW])
            m.p = r([2, BPT * KT * 2, KB])
            m.pt = r([2, BPT * KT, P])
            m.ctx = r([2, D])
            m.c_hi, m.c_lo = r([KT, SEQ], F16), r([KT, SEQ], F16)
            m.mx, m.sum, m.rl = (r([BPT * KT * 2]) for _ in range(3))
            return m

        STORE_LAG = 6
        expert_x = nc.dram_tensor("expert_x", (ROWS, D + 1), F32, kind="Internal").ap()
        expert_y = nc.dram_tensor("expert_y", (TILES * P, D), F32, kind="Internal").ap()

        GB = (3, 4, 5, 6)
        QKB = (0, 1, 2, 7)
        SB = (2, 7, 0, 1)

        block = ctx.enter_context(nc.Block())

        def each_sequence(eng, body, peel=False):
            with eng.Fori(0, NSEQ // 2 - peel) as i:
                for u in range(2):
                    body(2 * i + u, u)
            if peel:
                for u in range(2):
                    body(NSEQ - 2 + u, u)

        def each_tile(eng, step, depth):
            def has_of(i):
                return lambda back: 0 <= i - back < TILES
            first = 8
            for i in range(first):
                step(i, i // 4, i % 4, has_of(i))
            with eng.Fori(first // 4, TILES // 4) as b:
                for u in range(4):
                    step(4 * b + u, b, u, lambda back: True)
            for i in range(TILES, TILES + depth):
                step(i, i // 4, i % 4, has_of(i))

        def skewed(eng, step):
            step(0, 0, True, False)
            with eng.Fori(0, NSEQ // 2 - 1) as i:
                step(2 * i + 1, 1, True, True)
                step(2 * i + 2, 0, True, True)
            step(NSEQ - 1, 1, True, True)
            step(NSEQ, 0, False, True)

        @block.sync
        def _(sp):
            sp.dma_start(consts[:], T["consts"]).then_inc(small_loaded, 16)
            xd = T["x"].rearrange("(t p) d -> p t d", p=P)
            sp.dma_start(x[:, 0:TPS, :], xd[:, 0:TPS, :]).then_inc(x_loaded[0], 16)
            sp.dma_start(rows[:], T["rows"]).then_inc(small_loaded, 16)
            sp.dma_start(cols[:], T["cols"]).then_inc(small_loaded, 16)
            for m, (name, n) in enumerate(loads):
                if m >= NST:
                    sp.wait_ge(w_lo_done, m - NST + 1)
                sp.dma_start(stage[:, m % NST, 0:n], T[name]).then_inc(staged[m % NST], 16)
                if m == FIRST + 1:
                    sp.dma_start(x[:, TPS:, :], xd[:, TPS:, :]).then_inc(x_loaded[1], 16)
            def ffn0(n):
                s, m = S[n], ffn0_space()
                G0, T0 = earlier(n) * NSEQ, earlier(n) * TILES
                sp.wait_ge(s["zeros_set"], 1 + earlier(n))
                for d in range(DUMP):
                    at = NE * REGION + d * P
                    sp.dma_start(expert_x[at:at + P, :], m.zeros).then_inc(s["zero_filled"], 16)
                if not earlier(n):
                    staging_left(sp)
                    with sp.Fori(0, NSEQ) as g:
                        for v in range(LPS):
                            sp.wait_ge(later_lo_done, g * LPS + v + 1)
                            sp.dma_start(later_stage(m)[v], T["w_later"][:, ds((g * LPS + v) * LCH, LCH)]).then_inc(later_in[v], 16)
                sp.wait_ge(s["tab_ready"], 3 * (1 + earlier(n)))
                for e in range(NE):
                    row = sp.value_load(m.table[0:1, 2 * TILES + e:2 * TILES + e + 1], min_val=0, max_val=ROWS - P)
                    sp.dma_start(expert_x[ds(row, P), :], m.zeros).then_inc(s["zero_filled"], 16)
                sp.wait_ge(s["zero_filled"], 16 * (DUMP + NE) * (1 + earlier(n)))
                sp.wait_ge(later_lo_done, LPS * (NSEQ + 1))
                for r in range(TOPK):
                    sp.wait_ge(s[f"scattered{r}"], 16 * (NSEQ + G0) * TPS)

                def step(i, b, u, has):
                    if has(0):
                        row = sp.value_load(m.table[0:1, ds(i, 1)], min_val=0, max_val=ROWS - P)
                        if not isinstance(i, int) or i >= 4:
                            sp.wait_ge(s["tile_prod"], i - 3 + T0)
                        sp.dma_start(m.tile_x[:, u, :], expert_x[ds(row, P), :]).then_inc(s[f"tile_in{u}"], 16)
                    if has(STORE_LAG):
                        j, v = i - STORE_LAG, (u - STORE_LAG) % 4
                        sp.wait_ge(s["tile_y"], j + 1 + T0)
                        sp.dma_start(expert_y[ds(j * P, P), :], m.t_y[:, v, :]).then_inc(s[f"tile_out{v}"], 16)
                each_tile(sp, step, STORE_LAG)

            for n, kind in enumerate(SUBLAYERS):
                if kind == "ffn0":
                    ffn0(n)
            od = out.rearrange("(t p) d -> p t d", p=P)
            last = len(SUBLAYERS) - 1
            for g in range(NSEQ):
                sp.wait_ge(x_updated, N0(last) + g + 1)
                sp.dma_start(od[:, g * TPS:(g + 1) * TPS, :], x[:, g * TPS:(g + 1) * TPS, :]).then_inc(x_stored, 16)
            sp.wait_ge(x_stored, 16 * NSEQ)

        @block.gpsimd
        def _(pool):
            nc.gpsimd.memset(neghalf[:], -0.5).then_inc(rstd_step, 1)
            nc.gpsimd.memset(eps[:], EPS).then_inc(rstd_step, 1)
            pool.wait_ge(rstd_step, 2)

            def rstd_of(m):
                pool.wait_ge(mv_ready, m + 1)
                nc.gpsimd.tensor_tensor(rstd[:], mv[:, :, 1], eps[:], ALU.add).then_inc(rstd_step, 1)
                pool.wait_ge(rstd_step, m + 3)
                nc.gpsimd.tensor_tensor(rstd[:], rstd[:], neghalf[:, 0:TPS], ALU.pow).then_inc(rstd_ready, 1)

            def work_left(n):
                if n:
                    pool.wait_ge(x_updated, N0(n))
                else:
                    staging_left(pool)

            def gather_first(n, q, u, buffers):
                s, G0 = S[n], earlier(n) * NSEQ
                pool.wait_ge(s["rows_step"], q + 1 + G0)
                if not isinstance(q, int) or q >= len(buffers):
                    pool.wait_ge(s["combined"], q + 1 - len(buffers) + G0)
                gather_one(n, q, u, buffers, 0)

            def gather_second(n, q, u, buffers):
                s, G0 = S[n], earlier(n) * NSEQ
                pool.wait_ge(s["gathered0"], 16 * TPS * (q + 1 + G0))
                if not isinstance(q, int) or q + G0 > 0:
                    pool.wait_ge(s["gathered1"], 16 * TPS * (q + G0))
                gather_one(n, q, u, buffers, 1)

            def gather_one(n, q, u, buffers, r):
                pool.sem_inc(pool_stood, 1)
                for t in range(TPS):
                    nc.gpsimd.indirect_dma_start(
                        buffers[u % len(buffers)][:, t, :], None, expert_y[:, :],
                        bass.IndirectOffsetOnAxis(gather_rows[:, u, r, t:t + 1], 0),
                        compute_op=ALU.add if r else ALU.bypass).then_inc(S[n][f"gathered{r}"], 16)

            def gathers(n):
                for v in range(4):
                    pool.wait_ge(S[n - 1][f"tile_out{v}"], 4 * TILES * (1 + earlier(n - 1)))
                for stage_ in (gather_first, gather_second):
                    stage_(n - 1, 0, 0, yg_buffers(n))
                rstd_of(N0(n))
                for stage_ in (gather_first, gather_second):
                    stage_(n - 1, 1, 1, yg_buffers(n))

            def more_gathers(n, g, u, stage_):
                if after_ffn0(n) and not (isinstance(g, int) and g >= NSEQ - 2):
                    stage_(n - 1, g + 2, u, yg_buffers(n))

            def l1ffn(n):
                s = S[n]

                def body(g, u):
                    more_gathers(n, g, u, gather_first)
                    rstd_of(g + N0(n) + 1)
                    pool.wait_ge(xn_ready, g + N0(n) + 1)
                    for t in range(TPS):
                        ins = nc.gpsimd.tensor_tensor(x[:, ds(g * TPS + t, 1), :], x[:, ds(g * TPS + t, 1), :],
                                                      b2_row[:, None, :], ALU.add)
                    ins.then_inc(s["bias_added"], 1)
                    more_gathers(n, g, u, gather_second)
                each_sequence(pool, body, after_ffn0(n))

            def ffn0(n):
                s, m = S[n], ffn0_space()
                G0, T0 = earlier(n) * NSEQ, earlier(n) * TILES
                work_left(n)
                nc.gpsimd.memset(m.zeros, 0.0).then_inc(s["zeros_set"], 1)

                def body(g, u):
                    if not is_last(g):
                        rstd_of(g + N0(n) + 1)
                    pool.wait_ge(xn_ready, g + N0(n) + 1)
                    pool.wait_ge(s["rows_ready"], (g + G0) + 2)
                    for r in range(TOPK):
                        if r:
                            pool.wait_ge(s["scattered0"], 16 * TPS * ((g + G0) + 1))
                        nc.gpsimd.tensor_tensor(xn[:, :, D], m.gate[:, r], const("ones")[:, 0:TPS], ALU.mult).then_inc(s["gate_set"], 1)
                        pool.wait_ge(s["gate_set"], (g + G0) * TOPK + r + 1)
                        pool.sem_inc(pool_stood, 1)
                        for t in range(TPS):
                            nc.gpsimd.indirect_dma_start(
                                expert_x[:, :], bass.IndirectOffsetOnAxis(m.scatter_rows[:, r, t:t + 1], 0),
                                xn[:, t, :], None).then_inc(s[f"scattered{r}"], 16)
                    pool.wait_ge(s["scattered1"], 16 * TPS * ((g + G0) + 1))
                each_sequence(pool, body, True)

            def gla(n):
                s, m = S[n], gla_space()
                work_left(n)
                nc.gpsimd.memset(m.qz, 0.0).then_inc(s["q_ready"], 2)

                def body(g, u):
                    rstd_of(g + N0(n) + 1)
                    more_gathers(n, g, u, gather_first)
                    more_gathers(n, g, u, gather_second)
                    pool.wait_ge(s["ss_ready"], g * TPS + TPS)
                    nc.gpsimd.tensor_tensor(m.orstd, m.ss, eps[:, None, :].broadcast_to([P, TPS, H]), ALU.add).then_inc(s["orstd_step"], 1)
                    pool.wait_ge(s["orstd_step"], g + 1)
                    nc.gpsimd.tensor_tensor(m.orstd, m.orstd, neghalf.rearrange("p (a b) -> p a b", b=H), ALU.pow).then_inc(s["orstd_ready"], 1)
                each_sequence(pool, body, after_ffn0(n))

            def win(n):
                s, m = S[n], win_space()
                work_left(n)
                for a in (m.vz, m.k[:, :, 0:PAD]):
                    nc.gpsimd.memset(a, 0.0)
                nc.gpsimd.memset(m.k[:, :, PAD + SEQ:], 0.0).then_inc(s["zeroed"], 1)
                heads = const("heads")

                def body(g, u):
                    pool.wait_ge(s["qk_copied"], g * 2 * KT + KT)
                    for t in range(TPS):
                        pool.wait_ge(s["sc_ready"], g * TPS + t + 1)
                        for f in range(KT):
                            ins = nc.gpsimd.tensor_tensor(
                                m.qz[:, t % 2 * KT + f],
                                m.q[:, f, t * P:(t + 1) * P].rearrange("p (b q) -> p b q", q=QB)[:, :, None].broadcast_to([P, BPT, 8, QB]),
                                heads[:, None, :, None].broadcast_to([P, BPT, 8, QB]), ALU.mult)
                        ins.then_inc(s["qz_ready"], 1)
                        if t == 1:
                            rstd_of(g + N0(n) + 1)
                    pool.wait_ge(xn_ready, g + N0(n) + 1)
                    for t in range(TPS):
                        ins = nc.gpsimd.tensor_tensor(x[:, ds(g * TPS + t, 1), :], x[:, ds(g * TPS + t, 1), :],
                                                      bo_row[:, None, :], ALU.add)
                    ins.then_inc(s["bias_added"], 1)
                each_sequence(pool, body)

            pool.wait_ge(small_loaded, 48)
            nc.gpsimd.tensor_scalar(b2_row, b2_row, 0.5, None, ALU.mult).then_inc(ready0, 1)
            nc.gpsimd.tensor_scalar(rms_col, rms_col, WS, None, ALU.mult).then_inc(ready0, 1)
            pool.wait_ge(ready0, 2)
            for w in (xt_hi, xt_lo):
                nc.gpsimd.memset(w[:, :, :, 0:PAD], 0.0)
                nc.gpsimd.memset(w[:, :, :, PAD + SEQ:], 0.0).then_inc(ready0, 1)
            rstd_of(0)
            for n, kind in enumerate(SUBLAYERS):
                if after_ffn0(n):
                    gathers(n)
                {"ffn0": ffn0, "l1ffn": l1ffn, "gla": gla, "win": win}[kind](n)

        @block.scalar
        def _(act):
            def halves_hi(which):
                for m in which:
                    name, dst, n = SPLIT[m]
                    load_done(act, load_of(m))
                    nc.scalar.activation(dst[0][:, 0:n], stage[:, load_of(m) % NST, 0:n], ACT.Copy,
                                         scale=rms_col if name == "g_o" else WS).then_inc(w_hi_done, 1)

            def later_hi(m, g, v):
                act.wait_ge(later_in[v], 16 * (g + 1))
                nc.scalar.activation(later[0][:, ds((g * LPS + v) * LCH, LCH)], later_stage(m)[v], ACT.Copy,
                                     scale=WS).then_inc(later_hi_done, 1)

            def xt_hi_of(m, u):
                act.wait_ge(pt_ready, m + 1)
                nc.scalar.activation(xt_hi[:, u, :, TOK], ps[:, 0:KT, :], ACT.Copy).then_inc(xt_hi_ready, 1)

            def ffn0(n):
                s, m = S[n], ffn0_space()
                G0, T0 = earlier(n) * NSEQ, earlier(n) * TILES

                def body(g, u):
                    def hi(k):
                        act.wait_ge(s["prod_ready"], (g + G0) * SU + k + 3)
                        if k == 0:
                            act.wait_ge(s["y_ready"], (g + G0) * 2 + 2)
                        nc.scalar.activation(m.h_hi[:, k, :], m.prod[:, k % PRODS, :], ACT.Copy).then_inc(s["h_hi_ready"], 1)

                    act.wait_ge(s["router_ready"], (g + G0) + 1)
                    act.wait_ge(s["rows_ready"], (g + G0) + 1)
                    nc.scalar.activation(m.scores.rearrange("p a b -> p (a b)"), ps[:, 0, 0:TPS * NE], ACT.Sigmoid,
                                         scale=1 / WS).then_inc(s["scores_ready"], 1)
                    for k in range(SU):
                        b = 2 + 2 * (k % 2)
                        act.wait_ge(s["up_ready"], (g + G0) * SU + k + 1)
                        act.wait_ge(s["prod_ready"], (g + G0) * SU + k + 1)
                        nc.scalar.activation(m.silu[:, k % 2, :], ps[:, b, :], ACT.Silu, scale=1 / WS).then_inc(s["silu_ready"], 1)
                        if k >= 1:
                            hi(k - 1)
                        if k in (3, 5) and not earlier(n):
                            later_hi(m, g, (k - 3) // 2)
                    hi(SU - 1)
                    if not is_last(g):
                        xt_hi_of(g + N0(n) + 1, 1 - u)
                each_sequence(act, body, True)

                def step(i, b, u, has):
                    if has(0):
                        act.wait_ge(s["tile_turned"], i + 1 + T0)
                        if not isinstance(i, int) or i >= 2:
                            act.wait_ge(s["tile_up"], i - 1 + T0)
                        nc.scalar.activation(m.t_hi[:, u % 2], ps[:, u % 2, 0:KT * P].rearrange("p (k t) -> p k t", k=KT),
                                             ACT.Copy).then_inc(s["tile_hi"], 1)
                    if has(1):
                        j, v = i - 1, (u - 1) % 2
                        act.wait_ge(s["tile_up"], j + 1 + T0)
                        if not isinstance(j, int) or j >= 2:
                            act.wait_ge(s["tile_prod"], j - 1 + T0)
                        nc.scalar.activation(m.t_silu[:, v], ps[:, 2 + v, 0:HE], ACT.Silu, scale=1 / WS).then_inc(s["tile_silu"], 1)
                    if has(2):
                        j, v = i - 2, u % 2
                        act.wait_ge(s["th_turned"], j + 1 + T0)
                        if not isinstance(j, int) or j >= 2:
                            act.wait_ge(s["tile_down"], j - 1 + T0)
                        nc.scalar.activation(m.th_hi[:, v], ps[:, 4 + v, 0:EU * P].rearrange("p (k t) -> p k t", k=EU),
                                             ACT.Copy).then_inc(s["th_hi"], 1)
                each_tile(act, step, 2)
                xt_hi_of(N0(n + 1), 0)

            def l1ffn(n):
                s = S[n]
                h_hi, h_lo, relu = l1ffn_space()

                def step(g, u, up, down):
                    def hi(k):
                        act.wait_ge(s["relu_ready"], g * FU + k + 1)
                        if k == 0:
                            act.wait_ge(s["y_ready"], g * 2 + 2)
                        nc.scalar.activation(h_hi[:, u, k, :], relu[:, k % RELUS, :], ACT.Copy).then_inc(s["h_hi_ready"], 1)

                    if not up:
                        return
                    for k in range(FU):
                        act.wait_ge(s["up_ready"], g * FU + k + 1)
                        act.wait_ge(s["h_lo_ready"], g * FU + k + 1)
                        nc.scalar.activation(relu[:, k % RELUS, :], ps[:, 2 + k % 4, :], ACT.Relu,
                                             bias=b1_col[:, k:k + 1]).then_inc(s["relu_ready"], 1)
                        if k >= 1:
                            hi(k - 1)
                    hi(FU - 1)
                    xt_hi_of(g + N0(n) + 1, 1 - u)
                skewed(act, step)

            def gla(n):
                s, m = S[n], gla_space()

                def low_queries_keys(g, first=False):
                    act.wait_ge(s["t_ready"], g + 1)
                    nc.scalar.activation(m.t_hi[0:LOW], ps[0:LOW, 2, :], ACT.Copy, scale=1 / WS).then_inc(s["t_hi"], 1)
                    for j in range(2 * GPAIR):
                        act.wait_ge(s["qk_ready"], g * 2 * GPAIR + j + 1)
                        if j == GPAIR and not first:
                            act.wait_ge(s["ss_ready"], g * TPS)
                        dst, p = (m.q, j) if j < GPAIR else (m.k, j - GPAIR)
                        nc.scalar.activation(dst[:, p], ps[:, QKB[j], :], ACT.Copy,
                                             scale=(DK ** -0.5 if j < GPAIR else 1.0) / WS).then_inc(s["qk_copied"], 1)

                def body(g, u):
                    act.wait_ge(s["lb_ready"], g * 2 + 2)
                    nc.scalar.activation(m.soft, m.lb, ACT.Abs).then_inc(s["soft_step"], 1)
                    act.wait_ge(s["soft_step"], g * 3 + 1)
                    nc.scalar.activation(m.soft, m.soft, ACT.Exp, scale=-1.0).then_inc(s["soft_step"], 1)
                    act.wait_ge(s["soft_step"], g * 3 + 2)
                    nc.scalar.activation(m.soft, m.soft, ACT.Ln, bias=1.0).then_inc(s["soft_step"], 1)
                    for c in range(TPS):
                        act.wait_ge(s["v_ready"], g * TPS + c + 1)
                        nc.scalar.activation(m.v[:, c], ps[:, GB[c], :], ACT.Copy, scale=1 / WS).then_inc(s["v_copied"], 1)
                    act.wait_ge(s["cum_ready"], g + 1)
                    nc.scalar.activation(m.ends.rearrange("p a b c -> p (a b c)"), ps[:, 0, 0:GPAIR * TPS * 2], ACT.Exp).then_inc(s["exps_ready"], 1)
                    nc.scalar.activation(m.soft.rearrange("p (a b) c -> p a (b c)", a=2), ps[:, 5:7, :], ACT.Exp).then_inc(s["exps_ready"], 1)
                    xt_hi_of(g + N0(n) + 1, 1 - u)
                    nc.scalar.activation(m.up, ps[:, 3:5, :], ACT.Exp).then_inc(s["exps_ready"], 1)
                    nc.scalar.activation(m.down, ps[:, 3:5, :], ACT.Exp, scale=-1.0).then_inc(s["exps_ready"], 1)
                    for c in range(TPS):
                        act.wait_ge(s["gate_ready"], g * TPS + c + 1)
                        act.wait_ge(s["st_ready"], g * TPS + TPS)
                        nc.scalar.activation(m.gate[:, c], ps[:, GB[c], :], ACT.Silu, scale=1 / WS).then_inc(s["gate_done"], 1)
                    for c in range(TPS):
                        act.wait_ge(s["o_ready"], g * TPS + c + 1)
                        if c >= 2:
                            act.wait_ge(s["ss_ready"], g * TPS + c - 1)
                        nc.scalar.activation(m.squares[:, c % 2], ps[:, GB[c], :], ACT.Square,
                                             scale=DV ** -0.5).then_inc(s["sq_ready"], 1)
                    if not is_last(g):
                        low_queries_keys(g + 1)
                    for c in range(TPS):
                        act.wait_ge(s["ogt_ready"], g * TPS + c + 1)
                        nc.scalar.activation(m.o_hi[:, c].rearrange("p h t -> p (h t)"), ps[:, SB[c], :], ACT.Copy).then_inc(s["ogt_hi"], 1)

                low_queries_keys(0, True)
                each_sequence(act, body, True)

            def win(n):
                s, m = S[n], win_space()
                act.wait_ge(s["zeroed"], 1)

                def queries_keys(g):
                    for j in range(2 * KT):
                        act.wait_ge(s["qk_ready"], g * 2 * KT + j + 1)
                        f = j % KT
                        dst, b = (m.q[:, f], bq_col) if j < KT else (m.k[:, f, TOK], bk_col)
                        nc.scalar.activation(dst, ps[:, 2 + j, :], ACT.Identity, bias=b[:, f:f + 1],
                                             scale=1 / WS).then_inc(s["qk_copied"], 1)

                def body(g, u):
                    for t in range(TPS):
                        i = t % 2
                        act.wait_ge(s["sub_ready"], g * TPS + t + 1)
                        nc.scalar.activation(m.p[:, i], m.p[:, i], ACT.Exp, scale=AD ** -0.5).then_inc(s["exp_ready"], 1)
                        for b in range(2):
                            act.wait_ge(s["pt_ready"], (g * TPS + t) * 2 + b + 1)
                            nc.scalar.activation(m.pt[:, i, 4 * b:4 * b + 4].rearrange("p a b -> p (a b)"),
                                                 ps[:, 4 + b, :], ACT.Copy).then_inc(s["pt_copied"], 1)
                        if t >= 1:
                            ct_hi(s, m, g, t - 1)
                        if t == 1:
                            xt_hi_of(g + N0(n) + 1, 1 - u)
                    if not is_last(g):
                        act.wait_ge(s["qz_ready"], g * TPS + TPS)
                        queries_keys(g + 1)
                    ct_hi(s, m, g, TPS - 1)

                def ct_hi(s, m, g, t):
                    act.wait_ge(s["ct_ready"], g * TPS + t + 3)
                    nc.scalar.activation(m.c_hi[:, :, t * P:(t + 1) * P], ps[:, 1, 0:KT * P].rearrange("p (f q) -> p f q", f=KT),
                                         ACT.Copy).then_inc(s["ct_hi"], 1)
                queries_keys(0)
                each_sequence(act, body, True)

            act.wait_ge(small_loaded, 48)
            act.wait_ge(ready0, 4)
            nc.scalar.activation(window16[:], const("window")[:, None, :].broadcast_to([P, 8, KB]), ACT.Copy)
            nc.scalar.activation(ident16[:], ident, ACT.Copy)
            halves_hi(range(FIRST))
            xt_hi_of(0, 0)
            halves_hi(range(FIRST, len(SPLIT)))
            staging_left(act)
            for n, kind in enumerate(SUBLAYERS):
                {"ffn0": ffn0, "l1ffn": l1ffn, "gla": gla, "win": win}[kind](n)

        @block.vector
        def _(dve):
            def halves_lo(which):
                for m in which:
                    name, dst, n = SPLIT[m]
                    dve.wait_ge(w_hi_done, m + 1)
                    nc.vector.scalar_tensor_tensor(out=dst[1][:, 0:n], in0=stage[:, load_of(m) % NST, 0:n],
                                                   scalar=rms_col if name == "g_o" else WS, in1=dst[0][:, 0:n],
                                                   op0=ALU.mult, op1=ALU.subtract).then_inc(w_lo_done, 1)

            def later_lo(m, g, v):
                at = ds((g * LPS + v) * LCH, LCH)
                dve.wait_ge(later_hi_done, g * LPS + v + 1)
                nc.vector.scalar_tensor_tensor(out=later[1][:, at], in0=later_stage(m)[v], scalar=WS, in1=later[0][:, at],
                                               op0=ALU.mult, op1=ALU.subtract).then_inc(later_lo_done, 1)

            def ternary():
                for k, (name, dst) in enumerate(TERN):
                    load_done(dve, FIRST + k)
                    nc.vector.tensor_reduce(tsum[:, k:k + 1], stage[:, (FIRST + k) % NST, :], AX.X, ALU.add,
                                            apply_absolute_value=True).then_inc(tern, 1)
                for k, (name, dst) in enumerate(TERN):
                    dve.wait_ge(tern_sum, 1)
                    for sign, c in ((1, 0), (-1, 1)):
                        nc.vector.tensor_scalar(thr[:, k, c:c + 1], ps[:, 7, k:k + 1], sign * 0.5 / (CH * P), sign * 0.5 * EPS,
                                                ALU.mult, ALU.add).then_inc(tern, 1)
                dve.wait_ge(tern, 6)
                for k, (name, dst) in enumerate(TERN):
                    w = stage[:, (FIRST + k) % NST, :]
                    nc.vector.tensor_scalar(dst[:], w, thr[:, k, 1:2], None, ALU.is_lt).then_inc(tern, 1)
                    dve.wait_ge(tern, 7 + 2 * k)
                    nc.vector.scalar_tensor_tensor(out=dst[:], in0=w, scalar=thr[:, k, 0:1], in1=dst[:],
                                                   op0=ALU.is_gt, op1=ALU.subtract).then_inc(tern, 1)
                dve.wait_ge(tern, 10)

            def ln_stats(m, at):
                for t in range(TPS):
                    ins = nc.vector.bn_stats(stats[:, t, :], x[:, ds(at + t, 1), :].rearrange("p a d -> p (a d)"))
                ins.then_inc(ln_step, 1)
                dve.wait_ge(ln_step, m + 1)
                dve.sem_inc(stood, 1)
                for t in range(TPS):
                    ins = nc.vector.bn_aggr(mv[:, t, :], stats[:, t, :])
                ins.then_inc(mv_ready, 1)

            def ln_scale(m, at, first=False):
                dve.wait_ge(mv_ready, m + 1)
                dve.wait_ge(rstd_ready, m + 1)
                if not first:
                    dve.wait_ge(pt_ready, m)
                for t in range(TPS):
                    ins = nc.vector.tensor_scalar(xn[:, t, 0:D], x[:, ds(at + t, 1), :].rearrange("p a d -> p (a d)"),
                                                  mv[:, t, 0:1], rstd[:, t:t + 1], ALU.subtract, ALU.mult)
                ins.then_inc(xn_ready, 1)

            def xt_lo_of(m, u):
                dve.wait_ge(xt_hi_ready, m + 1)
                nc.vector.tensor_tensor(xt_lo[:, u, :, TOK], ps[:, 0:KT, :], xt_hi[:, u, :, TOK], ALU.subtract).then_inc(xt_lo_ready, 1)

            def next_at(g):
                return ((g + 1) % NSEQ) * TPS

            def integer_rows(n, q, u):
                nc.vector.tensor_scalar(gather_rows[:, u], expert_rows[:, :, ds(q * TPS, TPS)], 0.0, None,
                                        ALU.add).then_inc(S[n]["rows_step"], 1)

            def combine(n, q, u):
                s, G0 = S[n], earlier(n) * NSEQ
                dve.wait_ge(s["gathered0"], 16 * TPS * (q + 1 + G0))
                dve.wait_ge(s["gathered1"], 16 * TPS * (q + 1 + G0))
                integer_rows(n, q + 2, u)
                b = yg_buffers(n + 1)
                xs = x[:, ds(q * TPS, TPS), :]
                nc.vector.tensor_tensor(xs, xs, b[u % len(b)], ALU.add).then_inc(s["combined"], 1)
                dve.wait_ge(s["combined"], q + 1 + G0)
                dve.sem_inc(stood, 1)

            def next_stats(n, g, u):
                if after_ffn0(n) and not is_last(g):
                    combine(n - 1, g + 1, 1 - u)
                ln_stats(g + N0(n) + 1, next_at(g))

            def ffn0(n):
                s, m = S[n], ffn0_space()
                G0, T0 = earlier(n) * NSEQ, earlier(n) * TILES
                tri = const("tri").rearrange("p (e j) -> p e j", e=NE)
                iota = const("iota")
                GSTEPS, TAB_STEPS = 13, 20
                if not earlier(n):
                    dve.sem_inc(s["h_lo_ready"], PRODS)
                if not earlier(n):
                    dve.sem_inc(s["prod_ready"], 2)
                if not earlier(n):
                    dve.sem_inc(s["y_taken"], 2)
                if not earlier(n):
                    dve.sem_inc(s["rows_ready"], 1)
                nc.vector.tensor_scalar(m.base, const("regions"), -1.0, None, ALU.add).then_inc(s["base_set"], 1)
                dve.wait_ge(s["base_set"], 1 + earlier(n))

                def body(g, u):
                    step = [0]

                    def link(ins):
                        step[0] += 1
                        ins.then_inc(s["gate_step"], 1)
                        dve.wait_ge(s["gate_step"], (g + G0) * GSTEPS + step[0])

                    def choose():
                        dve.wait_ge(s["scores_ready"], (g + G0) + 1)
                        link(nc.vector.tensor_tensor(m.biased, m.scores, ebias_row[:, None, :].broadcast_to([P, TPS, NE]), ALU.add))
                        other = m.biased[:, :, None, :].broadcast_to([P, TPS, NE, NE])
                        own = m.biased[:, :, :, None].broadcast_to([P, TPS, NE, NE])
                        nc.vector.tensor_tensor(m.beats, other, own, ALU.is_gt)
                        link(nc.vector.tensor_tensor(m.ties, other, own, ALU.is_equal))
                        link(nc.vector.tensor_tensor(m.ties, m.ties, tri[:, None].broadcast_to([P, TPS, NE, NE]), ALU.mult))
                        link(nc.vector.tensor_tensor(m.beats, m.beats, m.ties, ALU.add))
                        link(nc.vector.tensor_reduce(m.rank, m.beats, AX.X, ALU.add))
                        nc.vector.tensor_scalar(m.mask, m.rank, float(TOPK), None, ALU.is_lt).then_inc(s["mask_ready"], 1)
                        for r in range(TOPK):
                            ins = nc.vector.tensor_scalar(m.onehot[:, r], m.rank.rearrange("p t e -> p (t e)"), float(r), None,
                                                          ALU.is_equal)
                        link(ins)
                        link(nc.vector.scalar_tensor_tensor(
                            out=m.picked, in0=m.onehot, scalar=HS / WS,
                            in1=m.scores.rearrange("p t e -> p (t e)")[:, None, :].broadcast_to([P, TOPK, TPS * NE]),
                            op0=ALU.mult, op1=ALU.mult))
                        link(nc.vector.tensor_reduce(m.gate.rearrange("p r t -> p (r t)"),
                                                     m.picked.rearrange("p r (t e) -> p (r t) e", e=NE), AX.X, ALU.add))

                    def place():
                        dve.wait_ge(s["pos_ready"], (g + G0) + 1)
                        link(nc.vector.tensor_tensor(m.row, ps[:, 0, 64:64 + TPS * NE].rearrange("p (t e) -> p t e", e=NE),
                                                     m.base[:, None, :].broadcast_to([P, TPS, NE]), ALU.add))
                        link(nc.vector.tensor_tensor(m.base, m.base, ps[:, 0, 96:96 + NE], ALU.add))
                        link(nc.vector.tensor_tensor(
                            m.picked, m.onehot, m.row.rearrange("p t e -> p (t e)")[:, None, :].broadcast_to([P, TOPK, TPS * NE]), ALU.mult))
                        link(nc.vector.tensor_reduce(m.rank.rearrange("p t e -> p (t e)")[:, 0:TOPK * TPS],
                                                     m.picked.rearrange("p r (t e) -> p (r t) e", e=NE), AX.X, ALU.add))
                        rows_ = m.rank.rearrange("p t e -> p (t e)")[:, 0:TOPK * TPS].rearrange("p (r t) -> p r t", r=TOPK)
                        nc.vector.tensor_scalar(expert_rows[:, :, ds(g * TPS, TPS)], rows_, 0.0, None, ALU.add)
                        link(nc.vector.tensor_scalar(m.scatter_rows, rows_, 0.0, None, ALU.add))
                        dve.sem_inc(s["rows_ready"], 1)

                    def lo(k):
                        dve.wait_ge(s["h_hi_ready"], (g + G0) * SU + k + 1)
                        nc.vector.tensor_tensor(m.h_lo[:, k, :], m.prod[:, k % PRODS, :], m.h_hi[:, k, :],
                                                ALU.subtract).then_inc(s["h_lo_ready"], 1)

                    def take(half):
                        dve.wait_ge(s["y_ready"], (g + G0) * 2 + half + 3)
                        xs = x[:, ds(g * TPS + 2 * half, 2), :]
                        nc.vector.scalar_tensor_tensor(out=xs, in0=ps[:, 6 + half, :].rearrange("p (t d) -> p t d", t=2),
                                                       scalar=0.5 / (WS * HS), in1=xs, op0=ALU.mult,
                                                       op1=ALU.add).then_inc(s["y_taken"], 1)

                    if not is_last(g):
                        ln_stats(g + N0(n) + 1, next_at(g))
                    choose()
                    for k in range(SU):
                        b = 3 + 2 * (k % 2)
                        dve.wait_ge(s["silu_ready"], (g + G0) * SU + k + 1)
                        dve.wait_ge(s["h_lo_ready"], (g + G0) * SU + k + 1)
                        nc.vector.scalar_tensor_tensor(out=m.prod[:, k % PRODS, :], in0=ps[:, b, :], scalar=HS / WS,
                                                       in1=m.silu[:, k % 2, :], op0=ALU.mult, op1=ALU.mult).then_inc(s["prod_ready"], 1)
                        if k >= 1:
                            lo(k - 1)
                        if k == 1:
                            place()
                        if k in (4, 6) and not earlier(n):
                            later_lo(m, g, (k - 4) // 2)
                        if k >= 2 and is_last(g):
                            tabulate(k - 2)
                    lo(SU - 1)
                    if not is_last(g):
                        for r in range(TOPK):
                            dve.wait_ge(s[f"scattered{r}"], 16 * TPS * ((g + G0) + 1))
                        ln_scale(g + N0(n) + 1, next_at(g))
                    take(0)
                    if not is_last(g):
                        xt_lo_of(g + N0(n) + 1, 1 - u)
                    take(1)
                    dve.wait_ge(s["y_taken"], (g + G0) * 2 + 4)

                done = [0]

                def tabulate(part):
                    nt = NSEQ * TPS

                    def link(ins):
                        done[0] += 1
                        ins.then_inc(s["tab_step"], 1)
                        dve.wait_ge(s["tab_step"], done[0] + earlier(n) * TAB_STEPS)

                    if part == 0:
                        link(nc.vector.tensor_tensor(m.count, m.base, const("regions"), ALU.subtract))
                        nc.vector.tensor_scalar(m.table[:, 2 * TILES:], m.base, 1.0, None, ALU.add).then_inc(s["tab_ready"], 1)
                        link(nc.vector.tensor_scalar(m.count, m.count, 1.0, 1.0 / P, ALU.add, ALU.mult))
                        link(nc.vector.tensor_tensor(m.more, m.count[:, :, None].broadcast_to([P, NE, nt]),
                                                     iota[:, None, 0:nt].broadcast_to([P, NE, nt]), ALU.is_gt))
                        link(nc.vector.tensor_reduce(m.tiles, m.more, AX.X, ALU.add))
                    if part == 1:
                        link(nc.vector.tensor_tensor(m.before, tri, m.tiles[:, None, :].broadcast_to([P, NE, NE]), ALU.mult))
                        link(nc.vector.tensor_reduce(m.end, m.before, AX.X, ALU.add))
                        nc.vector.tensor_scalar(m.jump, m.tiles, -float(P), float(REGION), ALU.mult, ALU.add)
                        link(nc.vector.tensor_tensor(m.end, m.end, m.tiles, ALU.add))
                        link(nc.vector.tensor_tensor(m.over, iota[:, :, None].broadcast_to([P, TILES, NE]),
                                                     m.end[:, None, :].broadcast_to([P, TILES, NE]), ALU.is_ge))
                    if part == 2:
                        link(nc.vector.tensor_reduce(m.sums[:, 0], m.over, AX.X, ALU.add))
                        link(nc.vector.tensor_tensor(m.over, m.over, m.jump[:, None, :].broadcast_to([P, TILES, NE]), ALU.mult))
                    if part == 3:
                        link(nc.vector.tensor_reduce(m.sums[:, 1], m.over, AX.X, ALU.add))
                        nc.vector.tensor_scalar(m.table[:, TILES:2 * TILES], m.sums[:, 0], NE - 1.0, 2.0 * HE, ALU.min,
                                                ALU.mult).then_inc(s["tab_ready"], 1)
                        dve.wait_ge(s["tab_ready"], 2 + 3 * earlier(n))
                        link(nc.vector.tensor_scalar(m.count, const("regions"), float(REGION), None, ALU.add))
                        nc.vector.scalar_tensor_tensor(out=m.table[:, 0:TILES], in0=iota, scalar=float(P), in1=m.sums[:, 1],
                                                       op0=ALU.mult, op1=ALU.add).then_inc(s["tab_ready"], 1)
                    for r in range(TOPK):
                        if part == 4 + r:
                            beyond = m.over[:, 0:nt]
                            link(nc.vector.tensor_tensor(beyond, expert_rows[:, r, 0:nt, None].broadcast_to([P, nt, NE]),
                                                         m.count[:, None, :].broadcast_to([P, nt, NE]), ALU.is_ge))
                            link(nc.vector.tensor_tensor(beyond, beyond, m.jump[:, None, :].broadcast_to([P, nt, NE]), ALU.mult))
                            link(nc.vector.tensor_reduce(m.sums[:, 0, 0:nt], beyond, AX.X, ALU.add))
                            link(nc.vector.tensor_tensor(expert_rows[:, r, 0:nt], expert_rows[:, r, 0:nt], m.sums[:, 0, 0:nt],
                                                         ALU.subtract))

                each_sequence(dve, body, True)
                assert done[0] == TAB_STEPS
                dve.wait_ge(s["gate_step"], (NSEQ + G0) * GSTEPS)
                for q in range(2):
                    integer_rows(n, q, q)

                def step(i, b, u, has):
                    if has(0):
                        dve.wait_ge(s["tile_hi"], i + 1 + T0)
                        nc.vector.tensor_tensor(m.t_lo[:, u % 2], ps[:, u % 2, 0:KT * P].rearrange("p (k t) -> p k t", k=KT),
                                                m.t_hi[:, u % 2], ALU.subtract).then_inc(s["tile_lo"], 1)
                    if has(1):
                        j, v = i - 1, (u - 1) % 2
                        dve.wait_ge(s["tile_silu"], j + 1 + T0)
                        if not isinstance(j, int) or j >= 2:
                            dve.wait_ge(s["th_turned"], j - 1 + T0)
                        nc.vector.scalar_tensor_tensor(out=m.t_prod[:, v], in0=ps[:, 2 + v, HE:2 * HE],
                                                       scalar=m.tile_x[:, (u - 1) % 4, D:D + 1], in1=m.t_silu[:, v],
                                                       op0=ALU.mult, op1=ALU.mult).then_inc(s["tile_prod"], 1)
                    if has(2):
                        j, v = i - 2, u % 2
                        dve.wait_ge(s["th_hi"], j + 1 + T0)
                        nc.vector.tensor_tensor(m.th_lo[:, v], ps[:, 4 + v, 0:EU * P].rearrange("p (k t) -> p k t", k=EU),
                                                m.th_hi[:, v], ALU.subtract).then_inc(s["th_lo"], 1)
                    if has(3):
                        j, v = i - 3, (u - 3) % 4
                        dve.wait_ge(s["tile_down"], j + 1 + T0)
                        if not isinstance(j, int) or j >= 4:
                            dve.wait_ge(s[f"tile_out{v}"], 16 * (b - (1 if u < 3 else 0)) + 4 * T0)
                        nc.vector.tensor_scalar(m.t_y[:, v], ps[:, 6 + v % 2, 0:D], 0.5 / (WS * HS), None,
                                                ALU.mult).then_inc(s["tile_y"], 1)
                each_tile(dve, step, 3)
                dve.wait_ge(s["tile_y"], TILES + T0)
                dve.sem_inc(x_updated, NSEQ)
                combine(n, 0, 0)
                ln_stats(N0(n + 1), 0)
                ln_scale(N0(n + 1), 0)
                xt_lo_of(N0(n + 1), 0)

            def l1ffn(n):
                s = S[n]
                h_hi, h_lo, relu = l1ffn_space()
                dve.sem_inc(s["h_lo_ready"], RELUS)
                dve.sem_inc(s["y_taken"], 2)

                def step(g, u, up, down):
                    if up:
                        up_part(g, u)
                    if down:
                        down_part(g - 1, u, up)
                    else:
                        xt_lo_of(g + N0(n) + 1, 1 - u)

                def up_part(g, u):
                    for k in range(FU):
                        dve.wait_ge(s["h_hi_ready"], g * FU + k + 1)
                        nc.vector.tensor_tensor(h_lo[:, u, k, :], relu[:, k % RELUS, :], h_hi[:, u, k, :],
                                                ALU.subtract).then_inc(s["h_lo_ready"], 1)
                        if k == 0:
                            next_stats(n, g, u)
                        if k == 4:
                            ln_scale(g + N0(n) + 1, next_at(g))

                def down_part(g, u, next_one):
                    for half in range(2):
                        if half and next_one:
                            xt_lo_of(g + N0(n) + 2, 1 - u)
                        dve.wait_ge(s["y_ready"], g * 2 + half + 5)
                        dve.wait_ge(s["bias_added"], g + 1)
                        xs = x[:, ds(g * TPS + 2 * half, 2), :]
                        nc.vector.scalar_tensor_tensor(out=xs, in0=ps[:, 6 + half, :].rearrange("p (t d) -> p t d", t=2),
                                                       scalar=0.5, in1=xs, op0=ALU.mult, op1=ALU.add).then_inc(s["y_taken"], 1)
                    dve.wait_ge(s["y_taken"], g * 2 + 4)
                    dve.sem_inc(x_updated, 1)
                skewed(dve, step)

            def gla(n):
                s, m = S[n], gla_space()
                dve.sem_inc(s["y_taken"], 2)

                def low(g):
                    dve.wait_ge(s["t_hi"], g + 1)
                    nc.vector.scalar_tensor_tensor(out=m.t_lo[0:LOW], in0=ps[0:LOW, 2, :], scalar=1 / WS, in1=m.t_hi[0:LOW],
                                                   op0=ALU.mult, op1=ALU.subtract).then_inc(s["t_lo"], 1)

                def body(g, u):
                    step = [0]

                    def link(ins):
                        step[0] += 1
                        ins.then_inc(s["s_step"], 1)
                        dve.wait_ge(s["s_step"], g * (1 + 2 * TPS) + step[0])

                    for j, b in enumerate((2, 7)):
                        dve.wait_ge(s["logits_ready"], g * 2 + j + 1)
                        nc.vector.scalar_tensor_tensor(
                            out=m.lb[:, 2 * j:2 * j + 2], in0=ps[:, b, :].rearrange("p (t d) -> p t d", t=2), scalar=1 / WS,
                            in1=bgk_row[:, None, :].broadcast_to([P, 2, H * DK]), op0=ALU.mult, op1=ALU.add).then_inc(s["lb_ready"], 1)
                    next_stats(n, g, u)
                    dve.wait_ge(s["soft_step"], g * 3 + 3)
                    nc.vector.scalar_tensor_tensor(out=m.lb, in0=m.lb, scalar=0.0, in1=m.soft, op0=ALU.min,
                                                   op1=ALU.subtract).then_inc(s["g_ready"], 1)
                    ln_scale(g + N0(n) + 1, next_at(g))
                    dve.wait_ge(s["exps_ready"], g * 4 + 2)
                    for j, b in enumerate((2, 7)):
                        dve.wait_ge(s["kt_ready"], g * 2 + j + 1)
                        sl = m.soft[:, 2 * j:2 * j + 2]
                        nc.vector.scalar_tensor_tensor(out=sl, in0=ps[:, b, :].rearrange("p (t d) -> p t d", t=2), scalar=1 / WS,
                                                       in1=sl, op0=ALU.mult, op1=ALU.mult).then_inc(s["kdec_ready"], 1)
                    xt_lo_of(g + N0(n) + 1, 1 - u)
                    dve.wait_ge(s["exps_ready"], g * 4 + 3)
                    for h in range(2):
                        sl = slice(h * DK, (h + 1) * DK)
                        nc.vector.tensor_tensor(m.qz[sl, :, h], m.q[sl], m.up[sl], ALU.mult).then_inc(s["q_ready"], 1)
                    dve.wait_ge(s["exps_ready"], g * 4 + 4)
                    nc.vector.tensor_tensor(m.k, m.k, m.down, ALU.mult).then_inc(s["k_ready"], 1)
                    dve.wait_ge(s["q_ready"], g * 2 + 4)
                    link(nc.vector.memset(m.s, 0.0))

                    def state(c):
                        for p in range(GPAIR):
                            ins = nc.vector.tensor_scalar(m.states[:, c, p], m.s[:, p], m.ends[:, p, c, 0:1], None, ALU.mult)
                        link(ins)
                        dve.wait_ge(s["st_ready"], g * TPS + c + 1)
                        for p in range(GPAIR):
                            for h in range(2):
                                sl = slice(h * DK, (h + 1) * DK)
                                at = (2 * p + h) * DV
                                ins = nc.vector.scalar_tensor_tensor(
                                    out=m.s[sl, p], in0=m.s[sl, p], scalar=m.ends[sl, p, c, 1:2],
                                    in1=ps[sl, SB[c], at:at + DV], op0=ALU.mult, op1=ALU.add)
                        link(ins)

                    def mask(c):
                        dve.wait_ge(s["at_ready"], g * TPS + c + 1)
                        nc.vector.tensor_tensor(m.att[:, c].rearrange("p (h t) -> p h t", h=H), ps[:, GB[c], :].rearrange("p (h t) -> p h t", h=H),
                                                const("causal")[:, None, :].broadcast_to([P, H, P]), ALU.mult).then_inc(s["masked"], 1)

                    state(0)
                    state(1)
                    mask(0)
                    mask(1)
                    state(2)
                    mask(2)
                    mask(3)
                    state(3)
                    for c in range(TPS):
                        dve.wait_ge(s["sq_ready"], g * TPS + c + 1)
                        nc.vector.tensor_reduce(m.ss[:, c], m.squares[:, c % 2].rearrange("p (h e) -> p h e", h=H), AX.X,
                                                ALU.add).then_inc(s["ss_ready"], 1)
                    if not is_last(g):
                        low(g + 1)
                    dve.wait_ge(s["orstd_ready"], g + 1)
                    dve.wait_ge(s["gate_done"], g * TPS + TPS)
                    for c in range(TPS):
                        for h in range(H):
                            sl = slice(h * DV, (h + 1) * DV)
                            ins = nc.vector.scalar_tensor_tensor(out=m.gate[:, c, sl], in0=ps[:, GB[c], sl],
                                                                 scalar=m.orstd[:, c, h:h + 1], in1=m.gate[:, c, sl],
                                                                 op0=ALU.mult, op1=ALU.mult)
                        ins.then_inc(s["og_ready"], 1)
                    for c in range(TPS):
                        dve.wait_ge(s["ogt_hi"], g * TPS + c + 1)
                        nc.vector.tensor_tensor(m.o_lo[:, c].rearrange("p h t -> p (h t)"), ps[:, SB[c], :],
                                                m.o_hi[:, c].rearrange("p h t -> p (h t)"), ALU.subtract).then_inc(s["ogt_lo"], 1)
                    for half in range(2):
                        dve.wait_ge(s["y_ready"], g * 2 + half + 1)
                        xs = x[:, ds(g * TPS + 2 * half, 2), :]
                        nc.vector.scalar_tensor_tensor(out=xs, in0=ps[:, 3 + half, :].rearrange("p (t d) -> p t d", t=2),
                                                       scalar=1 / WS, in1=xs, op0=ALU.mult, op1=ALU.add).then_inc(s["y_taken"], 1)
                    dve.wait_ge(s["y_taken"], g * 2 + 4)
                    dve.sem_inc(x_updated, 1)
                low(0)
                each_sequence(dve, body, True)

            def win(n):
                s, m = S[n], win_space()
                dve.wait_ge(s["zeroed"], 1)
                dve.sem_inc(s["y_taken"], 2)

                def body(g, u):
                    def softmax(t):
                        i = t % 2
                        sc = ps[:, 2:4, :].rearrange("p a (b k) -> p (a b) k", k=KB)
                        dve.wait_ge(s["sc_ready"], g * TPS + t + 3)
                        nc.vector.tensor_reduce(m.mx, sc, AX.X, ALU.max).then_inc(s["mx_ready"], 1)
                        dve.wait_ge(s["mx_ready"], g * TPS + t + 1)
                        nc.vector.tensor_tensor(m.p[:, i], sc, m.mx[:, :, None].broadcast_to([P, BPT * KT * 2, KB]),
                                                ALU.subtract).then_inc(s["sub_ready"], 1)

                    def sums(t):
                        dve.wait_ge(s["exp_ready"], g * TPS + t + 1)
                        nc.vector.tensor_reduce(m.sum, m.p[:, t % 2], AX.X, ALU.add).then_inc(s["sum_ready"], 1)
                        dve.wait_ge(s["sum_ready"], g * TPS + t + 1)
                        nc.vector.reciprocal(m.rl, m.sum).then_inc(s["rl_ready"], 1)

                    def normalize(t):
                        dve.wait_ge(s["c_ready"], g * TPS + t + 1)
                        dve.wait_ge(s["rl_ready"], g * TPS + t + 1)
                        dve.wait_ge(s["ct_ready"], g * TPS + t + 1)
                        for b in range(BPT):
                            to = slice(b * QB, (b + 1) * QB)
                            for h in range(4):
                                sl = slice(h * QB, (h + 1) * QB)
                                own = slice(h * AD, (h + 1) * AD)
                                c = ps[sl, 6 + b // 2, b % 2 * D:(b % 2 + 1) * D].rearrange("p (a k) -> p a k", k=4 * AD)
                                ins = nc.vector.tensor_tensor(
                                    m.ctx[to, t % 2].rearrange("p (a k) -> p a k", k=4 * AD)[:, :, own], c[:, :, own],
                                    m.rl[sl, 4 * b:4 * b + 4, None].broadcast_to([QB, 4, AD]), ALU.mult)
                        ins.then_inc(s["cn_ready"], 1)

                    def ct_lo(t):
                        dve.wait_ge(s["ct_hi"], g * TPS + t + 1)
                        sl = slice(t * P, (t + 1) * P)
                        nc.vector.tensor_tensor(m.c_lo[:, :, sl], ps[:, 1, 0:KT * P].rearrange("p (f q) -> p f q", f=KT),
                                                m.c_hi[:, :, sl], ALU.subtract).then_inc(s["ct_lo"], 1)

                    ln_stats(g + N0(n) + 1, next_at(g))
                    for j in range(VF):
                        if j == VF_FIRST:
                            softmax(0)
                        dve.wait_ge(s["v_ready"], g * VF + j + 1)
                        for h in range(2):
                            w = 2 * (j - 1 + h)
                            if not 0 <= w < NB:
                                continue
                            sl = slice(h * KB, (h + 1) * KB)
                            ins = nc.vector.scalar_tensor_tensor(
                                out=m.vz[sl, w:w + 2].rearrange("p w f d -> p (w f) d")[:, :, sl],
                                in0=ps[sl, 4 + j % 4, :].rearrange("p (w d) -> p w d", d=P)[:, :, sl], scalar=1 / WS,
                                in1=bv_row[sl].rearrange("p (w d) -> p w d", d=P)[:, :, sl], op0=ALU.mult, op1=ALU.add)
                        ins.then_inc(s["v_copied"], 1)
                    dve.wait_ge(s["v_copied"], g * (VF + 2) + VF)
                    for e, w in enumerate((0, NB - 1)):
                        nc.vector.tensor_scalar(m.vz[:, w], m.vz[:, w], const("edge")[:, e:e + 1], None,
                                                ALU.mult).then_inc(s["v_copied"], 1)
                    ln_scale(g + N0(n) + 1, next_at(g))
                    for t in range(TPS):
                        sums(t)
                        if t + 1 < TPS:
                            softmax(t + 1)
                        if t >= 1:
                            ct_lo(t - 1)
                        normalize(t)
                        if t == 1:
                            xt_lo_of(g + N0(n) + 1, 1 - u)
                    ct_lo(TPS - 1)
                    for half in range(2):
                        dve.wait_ge(s["y_ready"], g * 2 + half + 1)
                        dve.wait_ge(s["bias_added"], g + 1)
                        xs = x[:, ds(g * TPS + 2 * half, 2), :]
                        nc.vector.scalar_tensor_tensor(out=xs, in0=ps[:, 6 + half, :].rearrange("p (t d) -> p t d", t=2),
                                                       scalar=1 / WS, in1=xs, op0=ALU.mult, op1=ALU.add).then_inc(s["y_taken"], 1)
                    dve.wait_ge(s["y_taken"], g * 2 + 4)
                    dve.sem_inc(x_updated, 1)
                each_sequence(dve, body)

            dve.wait_ge(small_loaded, 48)
            dve.wait_ge(ready0, 4)
            dve.wait_ge(x_loaded[0], 16)
            nc.vector.memset(expert_rows[:, :, NSEQ * TPS:], 0.0)
            ln_stats(0, 0)
            ln_scale(0, 0, first=True)
            halves_lo(range(FIRST))
            xt_lo_of(0, 0)
            ternary()
            halves_lo(range(FIRST, len(SPLIT)))
            dve.sem_inc(later_lo_done, LPS)
            dve.wait_ge(x_loaded[1], 16)
            for n, kind in enumerate(SUBLAYERS):
                {"ffn0": ffn0, "l1ffn": l1ffn, "gla": gla, "win": win}[kind](n)

        @block.tensor
        def _(pe):
            def mm3(out_, a, b, start, stop):
                nc.tensor.matmul(out_, a[0], b[0], start=start, stop=False)
                nc.tensor.matmul(out_, a[0], b[1], start=False, stop=False)
                return nc.tensor.matmul(out_, a[1], b[0], start=False, stop=stop)

            def both(w, sl):
                return w[0][:, sl], w[1][:, sl]

            def xt(u, k, sl=slice(0, SEQ)):
                sl = slice(PAD + sl.start, PAD + sl.stop)
                return xt_hi[:, u, k, sl], xt_lo[:, u, k, sl]

            def transposes(m):
                pe.wait_ge(xn_ready, m + 1)
                for k in range(KT):
                    for t in range(TPS):
                        ins = nc.tensor.transpose(ps[:, k, t * P:(t + 1) * P], xn[:, t, k * P:(k + 1) * P], ident)
                ins.then_inc(pt_ready, 1)

            def xt_ready(m):
                pe.wait_ge(xt_hi_ready, m + 1)
                pe.wait_ge(xt_lo_ready, m + 1)

            def ffn0(n):
                s, m = S[n], ffn0_space()
                G0, T0 = earlier(n) * NSEQ, earlier(n) * TILES
                h = m.h_hi, m.h_lo
                if not earlier(n):
                    pe.sem_inc(s["y_ready"], 2)

                def router(g, u):
                    xt_ready(g + N0(n))
                    for t in range(TPS):
                        for k in range(KT):
                            ins = mm3(ps[:, 0, t * NE:(t + 1) * NE], xt(u, k, slice(t * P, (t + 1) * P)),
                                      both(wr, slice(k * NE, (k + 1) * NE)), k == 0, k == KT - 1)
                    ins.then_inc(s["router_ready"], 1)

                def positions(g):
                    pe.wait_ge(s["mask_ready"], (g + G0) + 1)
                    pos, total = ps[:, 0, 64:64 + TPS * NE], ps[:, 0, 96:96 + NE]
                    nc.tensor.matmul(pos, const("causal"), m.mask.rearrange("p t e -> p (t e)"), start=True, stop=False,
                                     skip_group_check=True)
                    for t in range(TPS - 1):
                        nc.tensor.matmul(pos[:, (t + 1) * NE:].rearrange("p (t e) -> p t e", e=NE), const("ones"),
                                         m.mask[:, t:t + 1].broadcast_to([P, TPS - 1 - t, NE]), start=False, stop=(t == TPS - 2),
                                         skip_group_check=True)
                    for t in range(TPS):
                        ins = nc.tensor.matmul(total, const("ones"), m.mask[:, t], start=(t == 0), stop=(t == TPS - 1),
                                               skip_group_check=True)
                    ins.then_inc(s["pos_ready"], 1)

                def body(g, u):
                    def up(q):
                        b = 2 + 2 * (q % 2)
                        pe.wait_ge(s["prod_ready"], (g + G0) * SU + q + 1)
                        for half in range(2):
                            for k in range(KT):
                                w = both((wsh1, wsh2)[half], slice(k * HSH + q * P, k * HSH + (q + 1) * P))
                                ins = mm3(ps[:, b + half, :], w, xt(u, k), k == 0, k == KT - 1)
                        ins.then_inc(s["up_ready"], 1)

                    def down(half):
                        pe.wait_ge(s["y_taken"], (g + G0) * 2 + half + 1)
                        for t in range(2 * half, 2 * half + 2):
                            sl = slice(t * P, (t + 1) * P)
                            for q in range(SU):
                                if t == 0 and q >= SU - 2:
                                    pe.wait_ge(s["h_hi_ready"], (g + G0) * SU + q + 1)
                                    pe.wait_ge(s["h_lo_ready"], (g + G0) * SU + q + 1 + PRODS)
                                ins = mm3(ps[:, 6 + half, (t % 2) * D:(t % 2 + 1) * D], (h[0][:, q, sl], h[1][:, q, sl]),
                                          both(wsh3, slice(q * D, (q + 1) * D)), q == 0, q == SU - 1)
                        ins.then_inc(s["y_ready"], 1)

                    for q in range(SU):
                        up(q)
                        if q == 1:
                            positions(g)
                    pe.wait_ge(s["h_hi_ready"], (g + G0) * SU + SU - 2)
                    pe.wait_ge(s["h_lo_ready"], (g + G0) * SU + SU - 2 + PRODS)
                    down(0)
                    if not is_last(g):
                        pe.wait_ge(s["rows_ready"], (g + G0) + 2)
                        transposes(g + N0(n) + 1)
                    down(1)
                    if not is_last(g):
                        router(g + 1, 1 - u)

                router(0, 0)
                each_sequence(pe, body, True)

                pe.wait_ge(s["tab_ready"], 3 * (1 + earlier(n)))
                pe.wait_ge(s["rows_ready"], (NSEQ + G0) + 1)
                if not earlier(n):
                    staging_left(pe)
                    pe.wait_ge(later_lo_done, LPS * (NSEQ + 1))

                now, past = ([pe.alloc_register(f"{name}_columns{n}_{v}") for v in range(4)] for name in ("now", "past"))

                def columns(u, back):
                    return pe.snap((now if u >= back else past)[(u - back) % 4], min_val=0, max_val=(NE - 1) * 2 * HE)

                def step(i, b, u, has):
                    if u == 0:
                        for v in range(4):
                            if has(1):
                                pe.reg_mov(past[v], now[v])
                        if has(0):
                            pe.load(now, m.table[0:1, ds(TILES + i, 4)])
                    if has(0):
                        pe.wait_ge(s[f"tile_in{u}"], 16 * (b + 1) + 4 * T0)
                        for k in range(KT):
                            ins = nc.tensor.transpose(ps[:, u % 2, k * P:(k + 1) * P], m.tile_x[:, u, k * P:(k + 1) * P], ident)
                        ins.then_inc(s["tile_turned"], 1)
                    if has(1):
                        j, v = i - 1, (u - 1) % 2
                        at = columns(u, 1)
                        pe.wait_ge(s["tile_hi"], j + 1 + T0)
                        pe.wait_ge(s["tile_lo"], j + 1 + T0)
                        if not isinstance(j, int) or j >= 2:
                            pe.wait_ge(s["tile_prod"], j - 1 + T0)
                        for k in range(KT):
                            ins = mm3(ps[:, 2 + v, :], (m.t_hi[:, v, k], m.t_lo[:, v, k]),
                                      both(wup, ds(at + k * NE * 2 * HE, 2 * HE)), k == 0, k == KT - 1)
                        ins.then_inc(s["tile_up"], 1)
                    if has(2):
                        j, v = i - 2, u % 2
                        pe.wait_ge(s["tile_prod"], j + 1 + T0)
                        for k in range(EU):
                            ins = nc.tensor.transpose(ps[:, 4 + v, k * P:(k + 1) * P], m.t_prod[:, v, k * P:(k + 1) * P], ident)
                        ins.then_inc(s["th_turned"], 1)
                    if has(3):
                        j, v = i - 3, (u - 3) % 2
                        at = columns(u, 3)
                        pe.wait_ge(s["th_hi"], j + 1 + T0)
                        pe.wait_ge(s["th_lo"], j + 1 + T0)
                        if not isinstance(j, int) or j >= 2:
                            pe.wait_ge(s["tile_y"], j - 1 + T0)
                        else:
                            pe.wait_ge(s["y_taken"], 2 * (NSEQ + G0) + 1 + j)
                        for k in range(EU):
                            ins = mm3(ps[:, 6 + v, 0:D], (m.th_hi[:, v, k], m.th_lo[:, v, k]), both(wdn, ds(at + k * D, D)),
                                      k == 0, k == EU - 1)
                        ins.then_inc(s["tile_down"], 1)
                each_tile(pe, step, 3)
                transposes(N0(n + 1))

            def l1ffn(n):
                s = S[n]
                h_hi, h_lo, _ = l1ffn_space()
                pe.sem_inc(s["y_ready"], 4)

                def step(g, u, up, down):
                    if up:
                        up_part(g, u)
                    if down:
                        down_part(g - 1, 1 - u, up)
                    else:
                        transposes(g + N0(n) + 1)

                def up_part(g, u):
                    xt_ready(g + N0(n))
                    for q in range(FU):
                        if q >= 4 or not isinstance(g, int) or g:
                            pe.wait_ge(s["relu_ready"], g * FU + q - 3)
                        for k in range(KT):
                            w = w1q[:, k * FF + q * P:k * FF + (q + 1) * P]
                            nc.tensor.matmul(ps[:, 2 + q % 4, :], w, xt_hi[:, u, k, TOK], start=(k == 0), stop=False)
                            ins = nc.tensor.matmul(ps[:, 2 + q % 4, :], w, xt_lo[:, u, k, TOK], start=False, stop=(k == KT - 1))
                        ins.then_inc(s["up_ready"], 1)

                def down_part(g, u, next_one):
                    pe.wait_ge(s["h_hi_ready"], g * FU + FU)
                    pe.wait_ge(s["h_lo_ready"], g * FU + FU + RELUS)
                    for half in range(2):
                        if half and next_one:
                            transposes(g + N0(n) + 2)
                        pe.wait_ge(s["y_taken"], g * 2 + half + 1)
                        for t in range(2 * half, 2 * half + 2):
                            sl = slice(t * P, (t + 1) * P)
                            for q in range(FU):
                                o = ps[:, 6 + half, (t % 2) * D:(t % 2 + 1) * D]
                                w = w2q[:, q * D:(q + 1) * D]
                                nc.tensor.matmul(o, h_hi[:, u, q, sl], w, start=(q == 0), stop=False)
                                ins = nc.tensor.matmul(o, h_lo[:, u, q, sl], w, start=False, stop=(q == FU - 1))
                        ins.then_inc(s["y_ready"], 1)
                skewed(pe, step)

            def gla(n):
                s, m = S[n], gla_space()

                def project(u, out_, w, c, n_, transposed=None):
                    for k in range(KT):
                        wk = both(w, slice(k * (w[0].shape[1] // KT) + c, k * (w[0].shape[1] // KT) + c + n_))
                        if transposed is None:
                            ins = mm3(out_, wk, xt(u, k), k == 0, k == KT - 1)
                        else:
                            ins = mm3(out_, xt(u, k, slice(transposed * P, (transposed + 1) * P)), wk, k == 0, k == KT - 1)
                    return ins

                def low_queries_keys(g, u):
                    xt_ready(g + N0(n))
                    project(u, ps[0:LOW, 2, :], gk1, 0, LOW).then_inc(s["t_ready"], 1)
                    for j in range(2 * GPAIR):
                        if j == GPAIR:
                            pe.wait_ge(s["t_hi"], g + 1)
                            pe.wait_ge(s["t_lo"], g + 1)
                        project(u, ps[:, QKB[j], :], gqk, j * P, P).then_inc(s["qk_ready"], 1)

                def body(g, u):
                    pe.wait_ge(s["qk_copied"], (g + 1) * 2 * GPAIR)
                    for j, b in enumerate((2, 7)):
                        for t in range(2):
                            sl = slice((2 * j + t) * P, (2 * j + t + 1) * P)
                            ins = mm3(ps[:, b, t * H * DK:(t + 1) * H * DK], (m.t_hi[0:LOW, sl], m.t_lo[0:LOW, sl]),
                                      (gk2[0][:, :], gk2[1][:, :]), True, True)
                        ins.then_inc(s["logits_ready"], 1)
                    for c in range(TPS):
                        if c < 2:
                            pe.wait_ge(s["y_taken"], g * 2 + c + 1)
                        project(u, ps[:, GB[c], :], gv, 0, H * DV, c).then_inc(s["v_ready"], 1)
                    for j, b in enumerate((2, 7)):
                        pe.wait_ge(s["lb_ready"], g * 2 + j + 1)
                        for t in range(2):
                            ins = project(u, ps[:, b, t * H * DK:(t + 1) * H * DK], gqk, H * DK, H * DK, 2 * j + t)
                        ins.then_inc(s["kt_ready"], 1)
                    pe.wait_ge(s["g_ready"], g + 1)
                    pe.wait_ge(s["v_copied"], g * TPS + TPS)
                    for p in range(GPAIR):
                        for c in range(TPS):
                            gp = m.lb[:, c, p * P:(p + 1) * P]
                            nc.tensor.matmul(ps[:, 3 + p, c * P:(c + 1) * P], gp, const("cumref"), start=True, stop=True)
                            at = (p * TPS + c) * 2
                            nc.tensor.matmul(ps[:, 0, at:at + 2], gp, const("ends"), start=True, stop=True)
                    for c in range(TPS):
                        ins = nc.tensor.matmul(ps[:, 5 + c // 2, (c % 2) * 256:(c % 2 + 1) * 256], const("after"), m.lb[:, c],
                                               start=True, stop=True)
                    ins.then_inc(s["cum_ready"], 1)
                    pe.wait_ge(s["exps_ready"], g * 4 + 1)
                    transposes(g + N0(n) + 1)
                    pe.wait_ge(s["kdec_ready"], g * 2 + 2)
                    for c in range(TPS):
                        if c == 2:
                            xt_ready(g + N0(n) + 1)
                        for p in range(GPAIR):
                            ins = nc.tensor.matmul(ps[:, SB[c], p * 256:(p + 1) * 256], m.soft[:, c, p * P:(p + 1) * P],
                                                   m.v[:, c, p * 256:(p + 1) * 256], start=True, stop=True)
                        ins.then_inc(s["st_ready"], 1)
                    pe.wait_ge(s["q_ready"], g * 2 + 4)
                    pe.wait_ge(s["k_ready"], g + 1)
                    for c in range(TPS):
                        sl = slice(c * P, (c + 1) * P)
                        for p in range(GPAIR):
                            ins = nc.tensor.matmul(ps[:, GB[c], p * 256:(p + 1) * 256], m.k[:, p, sl], m.qz[:, p, :, sl],
                                                   start=True, stop=True)
                        ins.then_inc(s["at_ready"], 1)
                    for c in range(TPS):
                        pe.wait_ge(s["masked"], g * TPS + c + 1)
                        project(u, ps[:, GB[c], :], gg, 0, H * DV, c).then_inc(s["gate_ready"], 1)
                    for c in range(TPS):
                        pe.wait_ge(s["gate_done"], g * TPS + c + 1)
                        pe.wait_ge(s["s_step"], g * (1 + 2 * TPS) + 2 + 2 * c)
                        for h in range(H):
                            o = ps[:, GB[c], h * DV:(h + 1) * DV]
                            nc.tensor.matmul(o, m.att[:, c, h * P:(h + 1) * P], m.v[:, c, h * DV:(h + 1) * DV],
                                             start=True, stop=False)
                            ins = nc.tensor.matmul(o, m.qz[:, h // 2, h % 2, c * P:(c + 1) * P], m.states[:, c, h // 2],
                                                   start=False, stop=True)
                        ins.then_inc(s["o_ready"], 1)
                    pe.wait_ge(s["s_step"], (g + 1) * (1 + 2 * TPS))
                    if not is_last(g):
                        low_queries_keys(g + 1, 1 - u)
                        pe.wait_ge(s["qk_copied"], (g + 2) * 2 * GPAIR)
                    for c in range(TPS):
                        pe.wait_ge(s["og_ready"], g * TPS + c + 1)
                        for h in range(H):
                            ins = nc.tensor.transpose(ps[:, SB[c], h * P:(h + 1) * P], m.gate[:, c, h * DV:(h + 1) * DV], ident)
                        ins.then_inc(s["ogt_ready"], 1)
                    for half in range(2):
                        pe.wait_ge(s["ogt_hi"], g * TPS + 2 * half + 2)
                        pe.wait_ge(s["ogt_lo"], g * TPS + 2 * half + 2)
                        for t in range(2):
                            c = 2 * half + t
                            for h in range(H):
                                ins = mm3(ps[:, 3 + half, t * D:(t + 1) * D], (m.o_hi[:, c, h], m.o_lo[:, c, h]),
                                          both(go, slice(h * D, (h + 1) * D)), h == 0, h == H - 1)
                        ins.then_inc(s["y_ready"], 1)

                low_queries_keys(0, 0)
                each_sequence(pe, body, True)

            def win(n):
                s, m = S[n], win_space()
                pe.sem_inc(s["sc_ready"], 2)
                pe.sem_inc(s["ct_ready"], 2)
                pe.wait_ge(s["zeroed"], 1)

                def queries_keys(g, u):
                    xt_ready(g + N0(n))
                    for j in range(2 * KT):
                        for k in range(KT):
                            c = k * 3 * D + j * P
                            ins = mm3(ps[:, 2 + j, :], both(aqkv, slice(c, c + P)), xt(u, k), k == 0, k == KT - 1)
                        ins.then_inc(s["qk_ready"], 1)

                def body(g, u):
                    def scores(t):
                        pe.wait_ge(s["qz_ready"], g * TPS + t + 1)
                        for b in range(2):
                            nc.tensor.matmul(ps[:, 2 + b, :], ident16[:], window16[:], start=True, stop=False, skip_group_check=True)
                            for w in range(2):
                                for f in range(KT):
                                    for hg in range(2):
                                        blk = 2 * b + w
                                        at = ((w * KT + f) * 2 + hg) * KB
                                        key = (t * BPT + blk) * QB
                                        ins = nc.tensor.matmul(
                                            ps[:, 2 + b, at:at + KB], m.qz[:, t % 2 * KT + f, blk, 4 * hg:4 * hg + 4].rearrange("p h q -> p (h q)"),
                                            m.k[:, f, key:key + KB], start=False, stop=True, skip_group_check=True)
                        ins.then_inc(s["sc_ready"], 1)

                    def turn(t):
                        pe.wait_ge(s["exp_ready"], g * TPS + t + 1)
                        if t == 0:
                            pe.wait_ge(s["v_copied"], g * (VF + 2) + VF + 2)
                        for j in range(BPT * KT):
                            ins = nc.tensor.transpose(ps[:, 4 + j // 4, (j % 4) * P:(j % 4 + 1) * P],
                                                      m.p[:, t % 2, 2 * j:2 * j + 2].rearrange("p a b -> p (a b)"), ident)
                            if j % 4 == 3:
                                ins.then_inc(s["pt_ready"], 1)

                    def values(t):
                        if t >= 1:
                            pe.wait_ge(s["cn_ready"], g * TPS + t)
                        for j in range(BPT * KT):
                            if j % 4 == 0:
                                pe.wait_ge(s["pt_copied"], (g * TPS + t) * 2 + j // 4 + 1)
                            w = m.pt[:, t % 2, j]
                            ins = nc.tensor.matmul(ps[:, 6 + j // 4, (j % 4) * P:(j % 4 + 1) * P], w,
                                                   m.vz[:, t * BPT + j // KT, j % KT], start=True, stop=True)
                        ins.then_inc(s["c_ready"], 1)

                    def context(t):
                        pe.wait_ge(s["cn_ready"], g * TPS + t + 1)
                        if t >= 1:
                            pe.wait_ge(s["ct_lo"], g * TPS + t)
                        for f in range(KT):
                            ins = nc.tensor.transpose(ps[:, 1, f * P:(f + 1) * P], m.ctx[:, t % 2, f * P:(f + 1) * P], ident)
                        ins.then_inc(s["ct_ready"], 1)

                    for j in range(VF):
                        if j == VF_FIRST:
                            pe.wait_ge(s["qk_copied"], g * 2 * KT + 2 * KT)
                            scores(0)
                        if j in (2, 3):
                            pe.wait_ge(s["y_taken"], g * 2 + j - 1)
                        if j < 2:
                            pe.wait_ge(s["qk_copied"], g * 2 * KT + KT + j + 1)
                        if j >= 4:
                            pe.wait_ge(s["v_copied"], g * (VF + 2) + j - 3)
                        for w in range(2):
                            at = (2 * j + w) * QB
                            lhs, half = slice(at - 2 * QB, at - 2 * QB + P), slice(0, P)
                            if j == 0:
                                lhs, half = slice(at, at + KB), slice(KB, P)
                            elif j == VF - 1:
                                lhs, half = slice(at - 2 * QB, at - 2 * QB + KB), slice(0, KB)
                            for k in range(KT):
                                c = k * 3 * D + 2 * D
                                ins = mm3(ps[half, 4 + j % 4, w * D:(w + 1) * D], (xt_hi[:, u, k, lhs], xt_lo[:, u, k, lhs]),
                                          both(aqkv, slice(c, c + D)), k == 0, k == KT - 1)
                        ins.then_inc(s["v_ready"], 1)
                    for t in range(TPS):
                        if t + 1 < TPS:
                            pe.wait_ge(s["sub_ready"], g * TPS + t + 1)
                            scores(t + 1)
                        turn(t)
                        if t >= 1:
                            if t == 2:
                                xt_ready(g + N0(n) + 1)
                            context(t - 1)
                        values(t)
                        if t == 1:
                            pe.wait_ge(s["ct_hi"], g * TPS + t)
                            pe.wait_ge(s["ct_lo"], g * TPS + t)
                            transposes(g + N0(n) + 1)
                    pe.wait_ge(s["sub_ready"], g * TPS + TPS)
                    if not is_last(g):
                        queries_keys(g + 1, 1 - u)
                    context(TPS - 1)
                    pe.wait_ge(s["ct_hi"], g * TPS + TPS)
                    pe.wait_ge(s["ct_lo"], g * TPS + TPS)
                    for half in range(2):
                        for t in range(2 * half, 2 * half + 2):
                            sl = slice(t * P, (t + 1) * P)
                            for f in range(KT):
                                ins = mm3(ps[:, 6 + half, (t % 2) * D:(t % 2 + 1) * D], (m.c_hi[:, f, sl], m.c_lo[:, f, sl]),
                                          both(ao, slice(f * D, (f + 1) * D)), f == 0, f == KT - 1)
                        ins.then_inc(s["y_ready"], 1)

                queries_keys(0, 0)
                each_sequence(pe, body, True)

            pe.wait_ge(small_loaded, 48)
            pe.wait_ge(ready0, 4)
            transposes(0)
            pe.wait_ge(tern, 2)
            nc.tensor.matmul(ps[:, 7, 0:2], const("ones"), tsum[:], start=True, stop=True).then_inc(tern_sum, 1)
            pe.wait_ge(w_lo_done, FIRST)
            for n, kind in enumerate(SUBLAYERS):
                if n:
                    pe.wait_ge(x_updated, N0(n))
                {"ffn0": ffn0, "l1ffn": l1ffn, "gla": gla, "win": win}[kind](n)


def constants(np):
    p = np.arange(P)[:, None]
    f = np.arange(P)[None, :]
    q, kk = p % QB, np.arange(KB)[None, :]
    e, j = np.arange(NE)[:, None], np.arange(NE)[None, :]
    c = {
        "ident": p == f,
        "ones": np.ones((P, P)),
        "causal": f >= p,
        "cumref": ((p <= f) * 1.0 - (p < P // 2)) / GATE_NORM,
        "after": (p > f) / GATE_NORM,
        "ends": np.concatenate([(p < P // 2) * 1.0, np.ones((P, 1))], 1) / GATE_NORM,
        "tri": np.broadcast_to((j < e).reshape(1, NE * NE), (P, NE * NE)),
        "window": np.where((kk >= q) & (kk <= q + 2 * PAD), 0.0, MASKED),
        "heads": p // AD == np.arange(8)[None, :],
        "iota": np.broadcast_to(np.arange(TILES)[None], (P, TILES)),
        "regions": np.broadcast_to(np.arange(NE)[None] * REGION, (P, NE)),
        "edge": np.concatenate([p % KB >= PAD, p % KB < KB - PAD], 1),
    }
    return np.concatenate([np.asarray(c[n], np.float32) for n in CONST_COLS], 1)


def laid_out(np, a):
    def tiles(w):
        k, n = w.shape
        return np.ascontiguousarray(w.reshape(k // P, P, n).transpose(1, 0, 2).reshape(P, -1))

    def down(v):
        return v.reshape(-1, P).T

    qkv = a["L1_attn_w_qkv"].reshape(AH, 3, AD, D).transpose(1, 0, 2, 3).reshape(3 * D, D)
    bqkv = a["L1_attn_b_qkv"].reshape(AH, 3, AD).transpose(1, 0, 2).reshape(3, D)
    rows = np.concatenate([a["L0_attn_bgk2"], a["L1_ffn_b2"], a["L1_attn_b_out"], bqkv[2], bqkv[2],
                           a["L0_ffn_expert_bias"]])
    later = {
        "w_up": tiles(a["L0_ffn_w12"].reshape(-1, D).T),
        "w_dn": tiles(a["L0_ffn_w3"].transpose(0, 2, 1).reshape(-1, D)),
        "g_qk": tiles(np.concatenate([a["L0_attn_Wq"], a["L0_attn_Wk"]]).T),
        "g_v": tiles(a["L0_attn_Wv"].T), "g_g": tiles(a["L0_attn_Wg"].T), "g_k1": tiles(a["L0_attn_Wgk1"].T),
        "g_k2": np.concatenate([a["L0_attn_Wgk2"].T, np.zeros((P - LOW, H * DK), np.float32)]),
        "a_o": tiles(a["L1_attn_w_out"].T),
    }
    return {
        "x": a["L0_attn_x"].reshape(-1, D),
        "consts": constants(np),
        "rows": np.ascontiguousarray(np.broadcast_to(rows[None], (P, rows.size))),
        "cols": np.ascontiguousarray(np.concatenate([down(a["L1_ffn_b1"]), down(bqkv[0]), down(bqkv[1]),
                                                     down(a["L0_attn_rms_w"])], 1)),
        "w_sh1": tiles(a["L0_ffn_shared_w1"].T), "w_sh2": tiles(a["L0_ffn_shared_w2"].T),
        "w_sh3": tiles(a["L0_ffn_shared_w3"].T), "w_r": tiles(a["L0_ffn_router_w"].T),
        "w_later": np.ascontiguousarray(np.concatenate([later[n] for n in LATER], 1)),
        "g_o": tiles(a["L0_attn_Wout"].T),
        "a_qkv": tiles(qkv.T),
        "w_1": tiles(a["L1_ffn_W1"].T), "w_2": tiles(a["L1_ffn_W2"].T),
    }


def kernel(**inputs):
    import numpy as np
    import concourse.bacc as bacc
    from concourse.bass_utils import run_bass_kernel_spmd

    nc = bacc.Bacc("TRN2", target_bir_lowering=False, num_devices=1)
    arrays = laid_out(np, {k: np.asarray(v) for k, v in inputs.items()})
    T = {n: nc.dram_tensor(f"in_{n}", v.shape, mybir.dt.from_np(v.dtype), kind="ExternalInput").ap()
         for n, v in arrays.items()}
    out = nc.dram_tensor("out_x", (NSEQ * SEQ, D), F32, kind="ExternalOutput").ap()
    build(nc, T, out)
    r = run_bass_kernel_spmd(nc, [{f"in_{n}": v for n, v in arrays.items()}], core_ids=[0])
    return r.results[0]["out_x"].reshape(NSEQ, SEQ, D)
```
